# Optimizing a Trainium2 kernel written in Bass

```python
import numpy as np
import jax
import jax.numpy as jnp

def _softmax(x, axis=-1):
    return jax.nn.softmax(x, axis=axis)

def _gelu(x):
    return jax.nn.gelu(x, approximate=True)

def _silu(x):
    return jax.nn.silu(x)

def _sigmoid(x):
    return jax.nn.sigmoid(x)

def _layernorm(x, axis=-1, eps=1e-05):
    m = jnp.mean(x, axis=axis, keepdims=True)
    v = jnp.var(x, axis=axis, keepdims=True)
    return (x - m) / jnp.sqrt(v + eps)

def _scatter_add(tgt, idx, src, axis=0):
    return tgt.at[idx].add(src)

def _segment_sum(src, seg, n):
    return jax.ops.segment_sum(src, seg, n)
kernel_name = 'mk_xattn_ffn_d1_seqx_r4_84ec20'

def setup_inputs(seed: int=0):
    np.random.seed(seed)
    _w = jnp.asarray

    def _rec_inputs():
        import jax
        import jax.numpy as jnp
        _rk = jax.random.key(seed)
        x = -0.0003929 + 0.9999 * jax.random.normal(jax.random.fold_in(_rk, 1), (32, 112, 512), jnp.float32)
        _lenS = 112 - jax.random.randint(jax.random.fold_in(_rk, 7), (32,), 0, max(1, 112 // 4) + 1, jnp.int32)
        _lenS2 = 375 - jax.random.randint(jax.random.fold_in(_rk, 8), (32,), 0, max(1, 375 // 4) + 1, jnp.int32)
        _ctx_2048P = jax.random.normal(jax.random.fold_in(_rk, 11), (32, 16, 512), jnp.float32)
        _ctx_2048c = jax.random.dirichlet(jax.random.fold_in(_rk, 511), 0.3 * jnp.ones((16,), jnp.float32), (32, 375))
        _ctx_2048t = jnp.einsum('bsk,bkd->bsd', _ctx_2048c, _ctx_2048P)
        _ctx_2048t = _ctx_2048t * jax.lax.rsqrt(jnp.mean(jnp.square(_ctx_2048t)) + 1e-12) * 0.953939
        ctx_2048 = -0.000514642 + 1.00011 * (_ctx_2048t + 0.3 * jax.random.normal(jax.random.fold_in(_rk, 611), (32, 375, 512), jnp.float32))
        _validS = jnp.arange(112)[None, :] < _lenS[:, None]
        _validS2 = jnp.arange(375)[None, :] < _lenS2[:, None]
        _causal = jnp.tril(jnp.ones((112, 112), dtype=bool))
        mask_BxSxS2_ff0 = jnp.where(jnp.ones((32, 112, 375), dtype=bool), 0.0, -1000000000.0).astype(jnp.float32)
        return (x, ctx_2048, mask_BxSxS2_ff0)
    x, ctx_2048, mask_BxSxS2_ff0 = _rec_inputs()

    def _L0_xattn_setup():
        import jax, jax.numpy as jnp
        import numpy as np
        NUM_HEADS = 16
        EPS = 1e-08

        def _dyn_quant(x):
            s = jnp.maximum(jnp.max(jnp.abs(x), axis=-1, keepdims=True) / 127.0, EPS)
            q = jnp.clip(jnp.round(x / s), -127.0, 127.0)
            return (q, s)

        def _quant_weight(w):
            s = jnp.maximum(jnp.max(jnp.abs(w), axis=1, keepdims=True) / 127.0, EPS)
            q = jnp.clip(jnp.round(w / s), -127.0, 127.0)
            return (q, s)

        def _w8a8_linear(x, w, b):
            qx, sx = _dyn_quant(x)
            qw, sw = _quant_weight(w)
            y = jnp.einsum('bnc,oc->bno', qx, qw) * (sx * sw[:, 0])
            return y + b
        key = jax.random.key(seed)
        ks = jax.random.split(key, 9)
        B, N, L, C = (2, 1024, 128, 512)
        sc = 0.02
        return {'x': jax.random.normal(ks[0], (B, N, C), jnp.float32), 'cond': jax.random.normal(ks[1], (B, L, C), jnp.float32), 'mask': jnp.zeros((B, N, L), jnp.float32), 'wq': jax.random.normal(ks[2], (C, C), jnp.float32) * sc, 'bq': jnp.zeros((C,), jnp.float32), 'wk': jax.random.normal(ks[3], (C, C), jnp.float32) * sc, 'bk': jnp.zeros((C,), jnp.float32), 'wv': jax.random.normal(ks[4], (C, C), jnp.float32) * sc, 'bv': jnp.zeros((C,), jnp.float32), 'wo': jax.random.normal(ks[5], (C, C), jnp.float32) * sc, 'bo': jnp.zeros((C,), jnp.float32)}
    _L0_xattn_all = _L0_xattn_setup()
    _L0_xattn_in = {k: v for k, v in _L0_xattn_all.items() if k in ('wq', 'bq', 'wk', 'bk', 'wv', 'bv', 'wo', 'bo')}
    del _L0_xattn_all

    def _L0_ffn_setup():
        import jax, jax.numpy as jnp
        import numpy as np
        from jax import lax
        TOP_K = 2
        NORM_TOPK = True
        W_SCALE = 0.02
        key = jax.random.key(seed)
        k1, k2, k3, k4 = jax.random.split(key, 4)
        B, S, D = (4, 512, 512)
        E, H = (8, 352)
        x = jax.random.normal(k1, (B, S, D), dtype=jnp.float32)
        gate_up_proj = jax.random.normal(k2, (E, 2 * H, D), dtype=jnp.float32) * W_SCALE
        down_proj = jax.random.normal(k3, (E, D, H), dtype=jnp.float32) * W_SCALE
        router_w = jax.random.normal(k4, (E, D), dtype=jnp.float32) * W_SCALE
        return {'x': x, 'gate_up_proj': gate_up_proj, 'down_proj': down_proj, 'router_w': router_w}
    _L0_ffn_all = _L0_ffn_setup()
    _L0_ffn_in = {k: v for k, v in _L0_ffn_all.items() if k in ('gate_up_proj', 'down_proj', 'router_w')}
    del _L0_ffn_all
    return {'x': x, 'ctx_2048': ctx_2048, 'mask_BxSxS2_ff0': mask_BxSxS2_ff0, 'L0_xattn_wq': _L0_xattn_in['wq'], 'L0_xattn_bq': _L0_xattn_in['bq'], 'L0_xattn_wk': _L0_xattn_in['wk'], 'L0_xattn_bk': _L0_xattn_in['bk'], 'L0_xattn_wv': _L0_xattn_in['wv'], 'L0_xattn_bv': _L0_xattn_in['bv'], 'L0_xattn_wo': _L0_xattn_in['wo'], 'L0_xattn_bo': _L0_xattn_in['bo'], 'L0_ffn_gate_up_proj': _L0_ffn_in['gate_up_proj'], 'L0_ffn_down_proj': _L0_ffn_in['down_proj'], 'L0_ffn_router_w': _L0_ffn_in['router_w']}

def reference(x, ctx_2048, mask_BxSxS2_ff0, L0_xattn_wq, L0_xattn_bq, L0_xattn_wk, L0_xattn_bk, L0_xattn_wv, L0_xattn_bv, L0_xattn_wo, L0_xattn_bo, L0_ffn_gate_up_proj, L0_ffn_down_proj, L0_ffn_router_w):
    import jax
    import jax.numpy as jnp

    def _L0_xattn_ref(x, cond, mask, wq, bq, wk, bk, wv, bv, wo, bo):
        import jax, jax.numpy as jnp
        import numpy as np
        NUM_HEADS = 16
        EPS = 1e-08

        def _dyn_quant(x):
            s = jnp.maximum(jnp.max(jnp.abs(x), axis=-1, keepdims=True) / 127.0, EPS)
            q = jnp.clip(jnp.round(x / s), -127.0, 127.0)
            return (q, s)

        def _quant_weight(w):
            s = jnp.maximum(jnp.max(jnp.abs(w), axis=1, keepdims=True) / 127.0, EPS)
            q = jnp.clip(jnp.round(w / s), -127.0, 127.0)
            return (q, s)

        def _w8a8_linear(x, w, b):
            qx, sx = _dyn_quant(x)
            qw, sw = _quant_weight(w)
            y = jnp.einsum('bnc,oc->bno', qx, qw) * (sx * sw[:, 0])
            return y + b
        B, N, C = x.shape
        L = cond.shape[1]
        H = NUM_HEADS
        D = C // H
        inv_sqrt_d = np.float32(1.0 / np.sqrt(D))
        q = _w8a8_linear(x, wq, bq).reshape(B, N, H, D).transpose(0, 2, 1, 3)
        k = (cond @ wk.T + bk).reshape(B, L, H, D).transpose(0, 2, 1, 3)
        v = (cond @ wv.T + bv).reshape(B, L, H, D).transpose(0, 2, 1, 3)
        scores = jnp.einsum('bhnd,bhld->bhnl', q, k) * inv_sqrt_d + mask[:, None]
        attn = jax.nn.softmax(scores, axis=-1)
        o = jnp.einsum('bhnl,bhld->bhnd', attn, v)
        o = o.transpose(0, 2, 1, 3).reshape(B, N, C)
        return _w8a8_linear(o, wo, bo)

    def _L0_ffn_ref(x, gate_up_proj, down_proj, router_w):
        import jax, jax.numpy as jnp
        import numpy as np
        from jax import lax
        TOP_K = 2
        NORM_TOPK = True
        W_SCALE = 0.02
        B, S, D = x.shape
        E = gate_up_proj.shape[0]
        h = x.reshape(-1, D)
        T = h.shape[0]
        logits = h @ router_w.T
        probs = jax.nn.softmax(logits.astype(jnp.float32), axis=-1)
        vals, idx = lax.top_k(probs, TOP_K)
        if NORM_TOPK:
            vals = vals / vals.sum(axis=-1, keepdims=True)
        combine = jnp.zeros((T, E), dtype=probs.dtype)
        combine = combine.at[jnp.arange(T)[:, None], idx].add(vals)

        def step(acc, per_expert):
            gup, dp, cw = per_expert
            gate, up = jnp.split(h @ gup.T, 2, axis=-1)
            y = jax.nn.silu(gate) * up @ dp.T
            return (acc + cw[:, None].astype(acc.dtype) * y, None)
        out, _ = lax.scan(step, jnp.zeros_like(h), (gate_up_proj, down_proj, combine.T))
        return out.reshape(B, S, D)
    x = x + _L0_xattn_ref(_layernorm(x, axis=-1), ctx_2048, mask_BxSxS2_ff0, L0_xattn_wq, L0_xattn_bq, L0_xattn_wk, L0_xattn_bk, L0_xattn_wv, L0_xattn_bv, L0_xattn_wo, L0_xattn_bo)
    x = x + _L0_ffn_ref(_layernorm(x, axis=-1), L0_ffn_gate_up_proj, L0_ffn_down_proj, L0_ffn_router_w)
    return x

_drawn_inputs = setup_inputs


def setup_inputs(seed=0):
    import zlib

    import numpy as np

    out = dict(_drawn_inputs(seed))
    spreads = {'L0_xattn_bq': (0.0, 0.8),
     'L0_xattn_bk': (0.0, 0.8),
     'L0_xattn_bv': (0.0, 0.1),
     'L0_xattn_bo': (0.0, 0.1)}
    factors = {'L0_xattn_wq': 7.261, 'L0_xattn_wk': 7.168}
    for name, (base, spread) in spreads.items():
        noise = np.random.default_rng([zlib.crc32(name.encode()), seed]).standard_normal(out[name].shape)
        drawn = base * np.exp(spread * noise) if base else spread * noise
        out[name] = jnp.asarray(drawn.astype(out[name].dtype))
    for name, factor in factors.items():
        out[name] = (out[name] * factor).astype(out[name].dtype)
    return out
```

```python
import concourse.bass as bass
from concourse import mybir
from contextlib import ExitStack

F32 = mybir.dt.float32
F32R = mybir.dt.float32r
BF16 = mybir.dt.bfloat16
I32 = mybir.dt.int32
ALU = mybir.AluOpType
ACT = mybir.ActivationFunctionType
AX = mybir.AxisListType

H = 16
QMAX = 127.0
QEPS = 1e-8
LN_EPS = 1e-5
ROUND = 12582912.0
BIG = 3.0e38
QUARTER = 32


def prepare_weights(nc, W, wq, wk_t, wv_t, wo, bq, bk, bv, bo, router_t):
    C = 512
    KT = C // 128
    D = C // H
    N = W["tokens"]
    with ExitStack() as ctx:
        sb = lambda name, shape, dt=F32: ctx.enter_context(nc.sbuf_tensor(name, shape, dt))
        sem = lambda name: ctx.enter_context(nc.semaphore(name))
        pt = [ctx.enter_context(nc.psum_tensor(f"w_pt{i}", [128, 512], F32)) for i in range(2)]
        ps = ctx.enter_context(nc.psum_tensor("w_ps", [128, 512], F32))
        raw = {n: sb(f"raw_{n}", [128, KT, C]) for n in ("q", "o", "k", "v")}
        low = {n: sb(f"raw_low_{n}", [128, KT, C]) for n in ("k", "v")}
        amax = sb("w_amax", [128, 2, KT])
        scale = sb("w_scale", [128, 2, KT])
        inv = sb("w_inv", [128, 2, KT])
        shifted = sb("w_shifted", [128, 2, KT, C])
        ints = sb("w_ints", [128, 2, KT, C], BF16)
        spread = sb("w_spread", [128, 2, KT, N])
        ones = sb("w_ones", [128, N])
        loaded = {n: sem(f"w_loaded_{n}") for n in ("q", "o", "k", "v")}
        rows_loaded = sem("rows_loaded")
        ident_made, ident_cast = sem("ident_made"), sem("ident_cast")
        amax_done, scale_done, inv_done = sem("w_amax_done"), sem("w_scale_done"), sem("w_inv_done")
        shift_done, ints_done, spread_done = sem("w_shift_done"), sem("w_ints_done"), sem("w_spread_done")
        turned, turned_out = sem("w_turned"), sem("w_turned_out")
        row_made, row_out = sem("w_row_made"), sem("w_row_out")
        high_done, low_done, bias_done = sem("w_high_done"), sem("w_low_done"), sem("w_bias_done")
        pairs = (("q", W["wq_int"], W["wq_row"]), ("o", W["wo_int"], W["wo_row"]))
        inv_sqrt_d = float(1.0 / (float(D) ** 0.5))

        block = ctx.enter_context(nc.Block())

        @block.sync
        def _(sp):
            for n, src in (("q", wq), ("k", wk_t), ("v", wv_t), ("o", wo)):
                sp.dma_start(raw[n][:, :, :], src.rearrange("(t p) c -> p t c", p=128)).then_inc(loaded[n], 16)
            for dst, src in ((W["bq_row"], bq), (W["bv_row"], bv), (W["bo_row"], bo)):
                sp.dma_start(dst[:, :], src.rearrange("(a n) -> a n", a=1).to_broadcast([128, C])).then_inc(rows_loaded, 16)
            with nc.allow_non_contiguous_dma(reason="512 biases, once"):
                sp.dma_start(W["bk_col"][:, :], bk.rearrange("(g p) -> p g", p=128)).then_inc(rows_loaded, 16)
            sp.dma_start(W["router"][:, :, :], router_t.rearrange("(t p) e -> p t e", p=128)).then_inc(rows_loaded, 16)

        @block.gpsimd
        def _(pool):
            pool.memset(W["ident"][:, :], 0.0).then_inc(ident_made, 1)
            pool.memset(W["minus_half"][:, :], -0.5).then_inc(ident_made, 1)
            pool.memset(ones[:, :], 1.0).then_inc(ident_made, 1)
            pool.wait_ge(ident_made, 3)
            pool.affine_select(out=W["ident"][:, :], in_=W["ident"][:, :], compare_op=ALU.not_equal, fill=1.0,
                               base=0, pattern=[[-1, 128]], channel_multiplier=1).then_inc(ident_made, 1)
            pool.wait_ge(ident_made, 4)
            pool.tensor_copy(W["ident16"][:, :], W["ident"][:, :]).then_inc(ident_cast, 1)

        @block.scalar
        def _(act):
            for i, n in enumerate(("k", "v")):
                act.wait_ge(loaded[n], 16)
                for t in range(KT):
                    act.activation(W[f"w{n}_hi"][:, t, :], raw[n][:, t, :], ACT.Identity).then_inc(high_done, 1)

        @block.vector
        def _(dve):
            for i, (n, _, _) in enumerate(pairs):
                dve.wait_ge(loaded[n], 16)
                for t in range(KT):
                    dve.tensor_reduce(amax[:, i, t:t + 1], raw[n][:, t, :], AX.X, ALU.max,
                                      apply_absolute_value=True).then_inc(amax_done, 1)
                dve.wait_ge(amax_done, KT * (i + 1))
                dve.tensor_scalar(scale[:, i, :], amax[:, i, :], 1.0 / QMAX, QEPS, ALU.mult, ALU.max).then_inc(scale_done, 1)
                dve.wait_ge(scale_done, i + 1)
                dve.reciprocal(inv[:, i, :], scale[:, i, :]).then_inc(inv_done, 1)
                dve.wait_ge(inv_done, i + 1)
                for t in range(KT):
                    dve.tensor_scalar(shifted[:, i, t, :], raw[n][:, t, :], inv[:, i, t:t + 1], ROUND,
                                      ALU.mult, ALU.add).then_inc(shift_done, 1)
                dve.wait_ge(shift_done, KT * (i + 1))
                for t in range(KT):
                    dve.tensor_scalar(ints[:, i, t, :], shifted[:, i, t, :], ROUND, None,
                                      ALU.subtract).then_inc(ints_done, 1)
                dve.wait_ge(ident_made, 3)
                for t in range(KT):
                    dve.tensor_scalar(spread[:, i, t, :], ones[:, :], scale[:, i, t:t + 1], None,
                                      ALU.mult).then_inc(spread_done, 1)
            for i, n in enumerate(("k", "v")):
                dve.wait_ge(high_done, KT * (i + 1))
                for t in range(KT):
                    dve.tensor_tensor(W[f"w{n}_lo"][:, t, :], raw[n][:, t, :], W[f"w{n}_hi"][:, t, :].bitcast(F32),
                                      ALU.subtract).then_inc(low_done, 1)
            for i, (_, dst, _) in enumerate(pairs):
                for t in range(KT):
                    k = KT * i + t
                    dve.wait_ge(turned, k + 1)
                    dve.tensor_scalar(dst[:, t, :], pt[k % 2][:, :].bitcast(BF16)[:, 0:C], QMAX, -QMAX,
                                      ALU.min, ALU.max).then_inc(turned_out, 1)
            dve.wait_ge(rows_loaded, 16 * 5)
            for i, (_, _, row) in enumerate(pairs):
                dve.wait_ge(row_made, i + 1)
                dve.tensor_scalar(row[0:N, :], ps[0:N, :], -inv_sqrt_d if i == 0 else 1.0, None,
                                  ALU.mult).then_inc(row_out, 1)
            dve.tensor_scalar(W["bq_row"][:, :], W["bq_row"][:, :], -inv_sqrt_d, None, ALU.mult).then_inc(bias_done, 1)

        @block.tensor
        def _(pe):
            pe.wait_ge(ident_cast, 1)
            for i in range(2):
                pe.wait_ge(ints_done, KT * (i + 1))
                for t in range(KT):
                    k = KT * i + t
                    if k >= 2:
                        pe.wait_ge(turned_out, k - 1)
                    for o in range(KT):
                        mm = pe.transpose(pt[k % 2][:, :].bitcast(BF16)[:, 128 * o:128 * o + 128],
                                          ints[:, i, o, 128 * t:128 * t + 128], W["ident16"][:, :])
                    mm.then_inc(turned, 1)
            for i in range(2):
                pe.wait_ge(spread_done, KT * (i + 1))
                if i:
                    pe.wait_ge(row_out, i)
                for t in range(KT):
                    mm = pe.matmul(ps[0:N, 128 * t:128 * t + 128], spread[:, i, t, :], W["ident"][:, :],
                                   start=True, stop=True)
                mm.then_inc(row_made, 1)


def attention(nc, W, x, ctx_t, mask, x1, h2):
    B, N, C = x.shape
    L = ctx_t.shape[2]
    LP = L + L % 2
    KT = C // 128
    G4 = H // 4
    LT = 3
    LC = L // LT
    assert L == LT * LC and LC <= 128 and N <= 112 and C == 512
    UNITS = KT + LT
    DS, RING_T = 4, 2
    KDMAS, QDMAS = 12, 12

    with ExitStack() as ctx:
        sb = lambda name, shape, dt=F32: ctx.enter_context(nc.sbuf_tensor(name, shape, dt))
        sem = lambda name: ctx.enter_context(nc.semaphore(name))
        bank = lambda name: ctx.enter_context(nc.psum_tensor(name, [128, 512], F32))
        proj, score, turn = [bank("proj0"), bank("proj1")], [bank("score0"), bank("score1")], [bank("turn0"), bank("turn1")]
        out_t, misc = bank("out_t"), bank("misc")
        misc16 = misc[:, :].bitcast(BF16)

        stage = sb("ctx_stage", [128, KT, LP])
        c_hi, c_lo = sb("ctx_hi", [128, 2, KT, LP], F32R), sb("ctx_lo", [128, 2, KT, LP], F32R)
        k_hi, k_lo = sb("k_hi", [128, G4, LP], F32R), sb("k_lo", [128, G4, LP], F32R)
        k_st = sb("k_stack", [96, 2, H, LP], F32R)
        q_hi, q_lo = sb("q_hi", [128, G4, N], F32R), sb("q_lo", [128, G4, N], F32R)
        q_st = sb("q_stack", [96, 2, H, N], F32R)
        v = sb("v", [LC, 2, LT, C])
        neg_mask = sb("neg_mask", [N, 2, L])
        probs = sb("probs", [N, DS, L])
        probs_t = sb("probs_t", [LC, RING_T, LT, N])
        neg_max, total = sb("neg_max", [N, 2, H]), sb("total", [N, 2, H])
        x_in, x_res = sb("x_in", [N, 2, C]), sb("x_res", [N, C])
        stats, mv, rstd = sb("stats", [N, 6]), sb("mv", [N, 2]), sb("rstd", [N, 1])
        var_eps = sb("var_eps", [N, 1])
        shifted = sb("shifted", [N, C])
        x_amax, x_scale, x_inv = sb("x_amax", [N, 1]), sb("x_scale", [N, 2]), sb("x_inv", [N, 1])
        x_int, x_int_t = sb("x_int", [N, C], BF16), sb("x_int_t", [128, KT, N], BF16)
        q_tok = sb("q_tok", [N, C])
        out_ts = sb("out_ts", [128, G4, N])
        inv_total = sb("inv_total", [N, H])
        o_tok = sb("o_tok", [N, C])
        o_amax, o_scale, o_inv = sb("o_amax", [N, 1]), sb("o_scale", [N, 1]), sb("o_inv", [N, 1])
        o_int, o_int_t = sb("o_int", [N, C], BF16), sb("o_int_t", [128, KT, N], BF16)
        y = sb("y", [N, C])
        x1_s = sb("x1_s", [N, C])
        stats2, mv2, rstd2, var_eps2 = sb("stats2", [N, 6]), sb("mv2", [N, 2]), sb("rstd2", [N, 1]), sb("var_eps2", [N, 1])
        h2_s = sb("h2_s", [N, C])
        h2_t = sb("h2_t", [128, KT, N])

        ctx_in, x_in_ld, x_res_ld, mask_in = sem("ctx_in"), sem("x_in_ld"), sem("x_res_ld"), sem("mask_in")
        stage_pad = sem("stage_pad")
        c_hi_made, c_lo_made = sem("c_hi_made"), sem("c_lo_made")
        unit_made, unit_out = sem("unit_made"), sem("unit_out")
        k_hi_made, k_stacked = sem("k_hi_made"), sem("k_stacked")
        ln1, rstd_made = sem("ln1"), sem("rstd_made")
        q_made, q_out = sem("q_made"), sem("q_out")
        q_biased, q_hi_made, q_stacked = sem("q_biased"), sem("q_hi_made"), sem("q_stacked")
        mask_negated = sem("mask_negated")
        scored, masked, softmaxed = sem("scored"), sem("masked"), sem("softmaxed")
        turned, turned_out, valued = sem("turned"), sem("turned_out"), sem("valued")
        out_t_out = sem("out_t_out")
        o_made, o_out, o_steps = sem("o_made"), sem("o_out"), sem("o_steps")
        x1_steps, ln2, rstd2_made = sem("x1_steps"), sem("ln2"), sem("rstd2_made")
        r_made, r_out = sem("r_made"), sem("r_out")
        x1_stored, h2_stored = sem("x1_stored"), sem("h2_stored")
        waits_taken = sem("waits_taken")

        def need(eng, s, count):
            if not isinstance(count, int) or count > 0:
                eng.wait_ge(s, count)

        def waited(eng):
            eng.sem_inc(waits_taken, 1)

        def iterations(eng, body):
            lo, hi = 3, B - 3 - (B - 6) % 2
            for it in range(-3, min(lo, B + 2)):
                body(it, it)
            with eng.Fori(0, (hi - lo) // 2) as j:
                for k in range(2):
                    body(j * 2 + (lo + k), lo + k, True)
            for it in range(hi, B + 2):
                body(it, it)

        def stages(it, inside):
            if inside:
                return [True] * 6
            return [0 <= it + d < B for d in range(-2, 4)]

        block = ctx.enter_context(nc.Block())

        @block.sync
        def _(sp):
            def body(it, par, inside=False):
                has_m2, has_m, _, has_n, has_nn, has_n3 = stages(it, inside)
                n, m, m2, n3 = it + 1, it - 1, it - 2, it + 3
                if has_n:
                    need(sp, masked, H * (n - 1))
                    sp.dma_start(neg_mask[:, (par + 1) % 2, :], mask[n, :, :]).then_inc(mask_in, 16)
                if has_m2:
                    need(sp, x1_steps, 2 * m2 + 2)
                    sp.dma_start(x1[m2, :, :], x1_s[:, :]).then_inc(x1_stored, 16)
                    need(sp, ln2, 3 * m2 + 3)
                    sp.dma_start(h2[m2, :, :], h2_s[:, :]).then_inc(h2_stored, 16)
                if has_m:
                    need(sp, x1_steps, 2 * m - 1)
                    sp.dma_start(x_res[:, :], x[m, :, :]).then_inc(x_res_ld, 16)
                if has_n:
                    q = (par + 1) % 2
                    need(sp, unit_out, UNITS * n + KT)
                    need(sp, scored, H * (n - 1))
                    for i in range(4):
                        rows = slice(QUARTER * i, QUARTER * i + QUARTER)
                        for r, src in ((0, k_hi), (1, k_lo), (2, k_hi)):
                            sp.dma_start(k_st[QUARTER * r:QUARTER * r + QUARTER, q, i:H:4, :].bitcast(F32),
                                         src[rows, :, :].bitcast(F32)).then_inc(k_stacked, 16)
                    need(sp, q_out, 3 * n + 3)
                    for i in range(4):
                        rows = slice(QUARTER * i, QUARTER * i + QUARTER)
                        for r, src in ((0, q_hi), (1, q_hi), (2, q_lo)):
                            sp.dma_start(q_st[QUARTER * r:QUARTER * r + QUARTER, q, i:H:4, :].bitcast(F32),
                                         src[rows, :, :].bitcast(F32)).then_inc(q_stacked, 16)
                if has_n3:
                    need(sp, c_lo_made, n3)
                    need(sp, c_hi_made, n3)
                    sp.dma_start(stage[:, :, 0:L], ctx_t[n3, :, :].rearrange("(t p) l -> p t l", p=128)).then_inc(ctx_in, 16)
                    need(sp, ln1, 8 * (n3 - 2) + 7)
                    sp.dma_start(x_in[:, (par + 3) % 2, :], x[n3, :, :]).then_inc(x_in_ld, 16)

            iterations(sp, body)
            sp.wait_ge(x1_stored, 16 * B)
            sp.wait_ge(h2_stored, 16 * B)

        @block.gpsimd
        def _(pool):
            pool.memset(stage[:, :, L:LP], 0.0).then_inc(stage_pad, 1)
            pool.wait_ge(stage_pad, 1)

            def body(it, par, inside=False):
                has_m2, has_m, _, has_n, has_nn, _ = stages(it, inside)
                n, m2, nn = it + 1, it - 2, it + 2
                if has_m2:
                    p = par % 2
                    need(pool, x_res_ld, 16 * (m2 + 1))
                    need(pool, o_out, 3 * m2 + 3)
                    pool.tensor_tensor(y[:, :], y[:, :], x_res[:, :], ALU.add).then_inc(x1_steps, 1)
                    need(pool, x1_steps, 2 * m2 + 1)
                    need(pool, x1_stored, 16 * m2)
                    need(pool, ln2, 3 * m2)
                    pool.tensor_tensor(x1_s[:, :], y[:, :], W["bo_row"][0:N, :], ALU.add).then_inc(x1_steps, 1)
                    need(pool, ln2, 3 * m2 + 2)
                    waited(pool)
                    pool.tensor_scalar(var_eps2[:, :], mv2[:, 1:2], 1.0, LN_EPS, ALU.mult, ALU.add).then_inc(rstd2_made, 1)
                    need(pool, rstd2_made, 2 * m2 + 1)
                    pool.tensor_tensor(rstd2[:, :], var_eps2[:, :], W["minus_half"][0:N, :], ALU.pow).then_inc(rstd2_made, 1)
                if has_n:
                    q = (par + 1) % 2
                    need(pool, mask_in, 16 * (n + 1))
                    waited(pool)
                    pool.tensor_scalar(neg_mask[:, q, :], neg_mask[:, q, :], -1.0, 0.0, ALU.mult, ALU.add).then_inc(mask_negated, 1)
                    need(pool, q_out, 3 * n + 2)
                    need(pool, q_made, 3 * n)
                    pool.tensor_tensor(q_tok[:, :], q_tok[:, :], W["bq_row"][0:N, :], ALU.add).then_inc(q_biased, 1)
                if has_nn:
                    need(pool, ln1, 8 * nn + 2)
                    waited(pool)
                    pool.tensor_scalar(var_eps[:, :], mv[:, 1:2], 1.0, LN_EPS, ALU.mult, ALU.add).then_inc(rstd_made, 1)
                    need(pool, rstd_made, 2 * nn + 1)
                    pool.tensor_tensor(rstd[:, :], var_eps[:, :], W["minus_half"][0:N, :], ALU.pow).then_inc(rstd_made, 1)
                    need(pool, c_hi_made, nn + 1)
                    pool.tensor_tensor(c_lo[:, par % 2, :, :], stage[:, :, :], c_hi[:, par % 2, :, :].bitcast(F32),
                                       ALU.subtract).then_inc(c_lo_made, 1)

            iterations(pool, body)

        @block.scalar
        def _(act):
            def turn_out(b, h):
                k = b * H + h
                need(act, turned, k + 1)
                need(act, valued, k - RING_T + 1)
                act.activation(probs_t[:, h % RING_T, :, :], turn[h % 2][0:LC, 0:LT * N].rearrange("p (l n) -> p l n", l=LT),
                               ACT.Copy).then_inc(turned_out, 1)

            def softmax(b, par, h):
                need(act, masked, b * H + h + 1)
                if h == 0:
                    need(act, o_steps, 6 * (b - 2) + 1)
                act.activation(probs[:, h % DS, :], probs[:, h % DS, :], ACT.Exp, bias=neg_max[:, par % 2, h:h + 1],
                               scale=-1.0, accum_out=total[:, par % 2, h:h + 1]).then_inc(softmaxed, 1)

            def body(it, par, inside=False):
                has_m2, has_m, has_a, has_n, has_nn, _ = stages(it, inside)
                n, m, m2, nn = it + 1, it - 1, it - 2, it + 2
                for h in range(H):
                    if h < 2 and has_m:
                        turn_out(m, H - 2 + h)
                    if h >= 2 and has_a:
                        turn_out(it, h - 2)
                    if has_a:
                        softmax(it, par, h)
                    if h == 2 and has_m:
                        need(act, valued, H * (m + 1))
                        need(act, o_made, 3 * (m - 1) + 1)
                        act.activation(out_ts[:, :, :], out_t[:, 0:G4 * N].rearrange("p (g n) -> p g n", g=G4),
                                       ACT.Copy).then_inc(out_t_out, 1)
                    if h in (1, 3, 5, 7) and has_n:
                        g = h // 2
                        need(act, unit_made, UNITS * n + g + 1)
                        if g == 0:
                            need(act, k_stacked, 16 * KDMAS * n)
                        act.activation(k_hi[:, g, :], proj[(par + 1 + g) % 2][:, 0:LP], ACT.Identity,
                                       bias=W["bk_col"][:, g:g + 1]).then_inc(k_hi_made, 1)
                    if h == 3 and has_m2:
                        need(act, r_made, 2 * m2 + 1)
                        act.activation(h2_t[:, :, :], misc[:, 0:KT * N].rearrange("p (t n) -> p t n", t=KT),
                                       ACT.Copy).then_inc(r_out, 1)
                    if h == 9 and has_n:
                        need(act, q_made, 3 * n + 3)
                        need(act, q_stacked, 16 * QDMAS * n)
                        act.activation(q_hi[:, :, :], misc[:, 0:G4 * N].rearrange("p (g n) -> p g n", g=G4),
                                       ACT.Identity).then_inc(q_hi_made, 1)
                    if h == 10 and has_nn:
                        need(act, ctx_in, 16 * (nn + 1))
                        if not isinstance(nn, int) or nn < 2:
                            act.wait_ge(stage_pad, 1)
                        need(act, unit_made, UNITS * (nn - 1))
                        act.activation(c_hi[:, par % 2, :, :], stage[:, :, :], ACT.Identity).then_inc(c_hi_made, 1)

            iterations(act, body)

        @block.vector
        def _(dve):
            def quantize(src, amax, scale, inv, shift, ints, chain, base):
                need(dve, chain, base)
                dve.tensor_scalar(scale, amax, 1.0 / QMAX, QEPS, ALU.mult, ALU.max).then_inc(chain, 1)
                need(dve, chain, base + 1)
                dve.reciprocal(inv, scale).then_inc(chain, 1)
                need(dve, chain, base + 2)
                dve.tensor_scalar(shift, src, inv, ROUND, ALU.mult, ALU.add).then_inc(chain, 1)
                need(dve, chain, base + 3)
                dve.tensor_scalar(ints, shift, ROUND, None, ALU.subtract).then_inc(chain, 1)

            def body(it, par, inside=False):
                has_m2, has_m, has_a, has_n, has_nn, _ = stages(it, inside)
                n, m, m2, nn = it + 1, it - 1, it - 2, it + 2
                p, q = par % 2, (par + 1) % 2
                for h in range(H):
                    if has_a:
                        k = it * H + h
                        if h == 0:
                            need(dve, mask_negated, it + 1)
                        need(dve, scored, k + 1)
                        need(dve, turned, k - DS + 1)
                        waited(dve)
                        dve.tensor_tensor_reduce(probs[:, h % DS, :], score[h % 2][0:N, 0:L], neg_mask[:, p, :], 1.0, BIG,
                                                 ALU.add, ALU.min, neg_max[:, p, h:h + 1]).then_inc(masked, 1)
                    if h == 0 and has_m2:
                        need(dve, o_made, 3 * m2 + 3)
                        need(dve, x1_steps, 2 * m2)
                        dve.scalar_tensor_tensor(y[:, :], misc[0:N, :], o_scale[:, 0:1], W["wo_row"][0:N, :],
                                                 ALU.mult, ALU.mult).then_inc(o_out, 1)
                    if h == 1 and has_m2:
                        need(dve, x1_steps, 2 * m2 + 2)
                        dve.bn_stats(stats2[:, :], x1_s[:, :]).then_inc(ln2, 1)
                        need(dve, ln2, 3 * m2 + 1)
                        waited(dve)
                        dve.bn_aggr(mv2[:, :], stats2[:, :]).then_inc(ln2, 1)
                    if h == 2 and has_m2:
                        need(dve, rstd2_made, 2 * m2 + 2)
                        need(dve, h2_stored, 16 * m2)
                        dve.tensor_scalar(h2_s[:, :], x1_s[:, :], mv2[:, 0:1], rstd2[:, 0:1],
                                          ALU.subtract, ALU.mult).then_inc(ln2, 1)
                    if h == 4 and has_m2:
                        need(dve, r_made, 2 * m2 + 2)
                        dve.tensor_copy(W["logits"][0:N, bass.ds(m2, 1), :] if inside else W["logits"][0:N, m2:m2 + 1, :],
                                        misc[0:N, 0:8].rearrange("p (a e) -> p a e", a=1)).then_inc(r_out, 1)
                    if h in (2, 4, 6, 8) and has_n:
                        g = h // 2 - 1
                        need(dve, k_hi_made, G4 * n + g + 1)
                        dve.scalar_tensor_tensor(k_lo[:, g, :], proj[(q + g) % 2][:, 0:LP], W["bk_col"][:, g:g + 1],
                                                 k_hi[:, g, :].bitcast(F32), ALU.add, ALU.subtract).then_inc(unit_out, 1)
                    if h == 5 and has_n:
                        need(dve, q_made, 3 * n + 1)
                        dve.tensor_scalar(x_int_t[:, :, :], misc16[:, 0:KT * N].rearrange("p (t n) -> p t n", t=KT),
                                          QMAX, -QMAX, ALU.min, ALU.max).then_inc(q_out, 1)
                    if h == 7 and has_n:
                        need(dve, q_made, 3 * n + 2)
                        dve.scalar_tensor_tensor(q_tok[:, :], misc[0:N, :], x_scale[:, q:q + 1], W["wq_row"][0:N, :],
                                                 ALU.mult, ALU.mult).then_inc(q_out, 1)
                    if h == 10 and has_n:
                        need(dve, q_hi_made, n + 1)
                        dve.tensor_tensor(q_lo[:, :, :], misc[:, 0:G4 * N].rearrange("p (g n) -> p g n", g=G4),
                                          q_hi[:, :, :].bitcast(F32), ALU.subtract).then_inc(q_out, 1)
                    if h in (9, 11, 13) and has_n:
                        l = (h - 9) // 2
                        need(dve, unit_made, UNITS * n + KT + 1 + l)
                        if l == 0:
                            need(dve, valued, H * (n - 1))
                        dve.tensor_tensor(v[:, q, l, :], proj[(q + KT + l) % 2][0:LC, :], W["bv_row"][0:LC, :],
                                          ALU.add).then_inc(unit_out, 1)
                    if h == 9 and has_nn:
                        need(dve, x_in_ld, 16 * (nn + 1))
                        dve.bn_stats(stats[:, :], x_in[:, p, :]).then_inc(ln1, 1)
                        need(dve, ln1, 8 * nn + 1)
                        waited(dve)
                        dve.bn_aggr(mv[:, :], stats[:, :]).then_inc(ln1, 1)
                    if h == 10 and has_nn:
                        need(dve, rstd_made, 2 * nn + 2)
                        dve.tensor_scalar(x_in[:, p, :], x_in[:, p, :], mv[:, 0:1], rstd[:, 0:1],
                                          ALU.subtract, ALU.mult).then_inc(ln1, 1)
                    if h == 11 and has_m:
                        need(dve, softmaxed, H * (m + 1))
                        dve.reciprocal(inv_total[:, :], total[:, q, :]).then_inc(o_steps, 1)
                        need(dve, o_steps, 6 * m + 1)
                        need(dve, o_made, 3 * m + 1)
                        dve.tensor_tensor(o_tok[:, :].rearrange("p (h d) -> p h d", h=H),
                                          misc[0:N, :].rearrange("p (h d) -> p h d", h=H),
                                          inv_total[:, :].unsqueeze(2).to_broadcast([N, H, C // H]), ALU.mult).then_inc(o_out, 1)
                        need(dve, o_out, 3 * m + 1)
                        dve.tensor_reduce(o_amax[:, :], o_tok[:, :], AX.X, ALU.max, apply_absolute_value=True).then_inc(o_steps, 1)
                    if h == 12 and has_m:
                        quantize(o_tok[:, :], o_amax[:, :], o_scale[:, :], o_inv[:, :], shifted[:, :], o_int[:, :], o_steps, 6 * m + 2)
                    if h == 12 and has_nn:
                        need(dve, ln1, 8 * nn + 3)
                        dve.tensor_reduce(x_amax[:, :], x_in[:, p, :], AX.X, ALU.max, apply_absolute_value=True).then_inc(ln1, 1)
                    if h == 13 and has_m:
                        need(dve, o_made, 3 * m + 2)
                        dve.tensor_scalar(o_int_t[:, :, :], misc16[:, 0:KT * N].rearrange("p (t n) -> p t n", t=KT),
                                          QMAX, -QMAX, ALU.min, ALU.max).then_inc(o_out, 1)
                    if h == 14 and has_nn:
                        need(dve, q_made, 3 * (nn - 1) + 1)
                        quantize(x_in[:, p, :], x_amax[:, :], x_scale[:, p:p + 1], x_inv[:, :], shifted[:, :], x_int[:, :], ln1, 8 * nn + 4)

            iterations(dve, body)

        @block.tensor
        def _(pe):
            def scores(b, par, h):
                k = b * H + h
                if h == 0:
                    need(pe, k_stacked, 16 * KDMAS * (b + 1))
                    need(pe, q_stacked, 16 * QDMAS * (b + 1))
                need(pe, masked, k - 1)
                pe.matmul(score[h % 2][0:N, 0:LP], q_st[:, par % 2, h, :], k_st[:, par % 2, h, :],
                          start=True, stop=True).then_inc(scored, 1)

            def turn_probs(b, h):
                k = b * H + h
                need(pe, softmaxed, k + 1)
                need(pe, turned_out, k - 1)
                for l in range(LT):
                    mm = pe.transpose(turn[h % 2][0:LC, l * N:(l + 1) * N], probs[:, h % DS, l * LC:(l + 1) * LC],
                                      W["ident"][0:N, 0:N])
                mm.then_inc(turned, 1)

            def values(b, par, h):
                k = b * H + h
                if h == 0:
                    need(pe, unit_out, UNITS * (b + 1))
                    need(pe, out_t_out, b)
                need(pe, turned_out, k + 1)
                i, g = h % 4, h // 4
                for l in range(LT):
                    mm = pe.matmul(out_t[QUARTER * i:QUARTER * i + QUARTER, g * N:(g + 1) * N],
                                   v[:, par % 2, l, QUARTER * h:QUARTER * h + QUARTER], probs_t[:, h % RING_T, l, :],
                                   start=(l == 0), stop=(l == LT - 1), skip_group_check=True)
                mm.then_inc(valued, 1)

            def turn_to_misc(src, ident, dst, rows, cols):
                for t in range(KT):
                    mm = pe.transpose(dst[0:cols, t * rows:(t + 1) * rows], src(t), ident)
                return mm

            def body(it, par, inside=False):
                has_m2, has_m, has_a, has_n, has_nn, _ = stages(it, inside)
                n, m, m2, nn = it + 1, it - 1, it - 2, it + 2
                p, q = par % 2, (par + 1) % 2
                for h in range(H):
                    if has_a:
                        scores(it, par, h)
                    if h < 2 and has_m:
                        turn_probs(m, H - 2 + h)
                    if h >= 2 and has_a:
                        turn_probs(it, h - 2)
                    if h < 3 and has_m:
                        values(m, par + 1, H - 3 + h)
                    if h >= 3 and has_a:
                        values(it, par, h - 3)
                    if h in (0, 2, 4, 6) and has_n:
                        g = h // 2
                        if g == 0:
                            need(pe, c_lo_made, n + 1)
                            need(pe, c_hi_made, n + 1)
                        need(pe, unit_out, UNITS * n + g - 1)
                        for t in range(KT):
                            for j, (w, c) in enumerate((("wk_hi", c_hi), ("wk_hi", c_lo), ("wk_lo", c_hi))):
                                mm = pe.matmul(proj[(q + g) % 2][:, 0:LP], W[w][:, t, 128 * g:128 * g + 128], c[:, q, t, :],
                                               start=(t == 0 and j == 0), stop=(t == KT - 1 and j == 2))
                        mm.then_inc(unit_made, 1)
                    if h in (8, 10, 12) and has_n:
                        l = (h - 8) // 2
                        need(pe, unit_out, UNITS * n + KT + l - 1)
                        for t in range(KT):
                            for j, (w, c) in enumerate((("wv_hi", c_hi), ("wv_lo", c_hi), ("wv_hi", c_lo))):
                                mm = pe.matmul(proj[(q + KT + l) % 2][0:LC, :], c[:, q, t, l * LC:(l + 1) * LC], W[w][:, t, :],
                                               start=(t == 0 and j == 0), stop=(t == KT - 1 and j == 2))
                        mm.then_inc(unit_made, 1)
                    if h == 3 and has_m2:
                        need(pe, ln2, 3 * m2 + 3)
                        need(pe, o_out, 3 * m2 + 3)
                        turn_to_misc(lambda t: h2_s[:, 128 * t:128 * t + 128], W["ident"][0:N, 0:N], misc, N, 128).then_inc(r_made, 1)
                    if h == 4 and has_m2:
                        need(pe, r_out, 2 * m2 + 1)
                        for t in range(KT):
                            mm = pe.matmul(misc[0:N, 0:8], h2_t[:, t, :], W["router"][:, t, :], start=(t == 0), stop=(t == KT - 1))
                        mm.then_inc(r_made, 1)
                    if h == 5 and has_n:
                        need(pe, ln1, 8 * n + 8)
                        need(pe, q_out, 3 * n)
                        if has_m2:
                            need(pe, r_out, 2 * m2 + 2)
                        turn_to_misc(lambda t: x_int[:, 128 * t:128 * t + 128], W["ident16"][0:N, 0:N], misc16, N, 128).then_inc(q_made, 1)
                    if h == 7 and has_n:
                        need(pe, q_out, 3 * n + 1)
                        for t in range(KT):
                            mm = pe.matmul(misc[0:N, :], x_int_t[:, t, :], W["wq_int"][:, t, :], start=(t == 0), stop=(t == KT - 1))
                        mm.then_inc(q_made, 1)
                    if h == 9 and has_n:
                        need(pe, q_biased, n + 1)
                        turn_to_misc(lambda t: q_tok[:, 128 * t:128 * t + 128], W["ident"][0:N, 0:N], misc, N, 128).then_inc(q_made, 1)
                    if h == 11 and has_m:
                        need(pe, out_t_out, m + 1)
                        if has_n:
                            need(pe, q_out, 3 * n + 3)
                        if has_m2:
                            need(pe, r_out, 2 * m2 + 2)
                        turn_to_misc(lambda t: out_ts[:, t, :], W["ident"][:, :], misc, 128, N).then_inc(o_made, 1)
                    if h == 13 and has_m:
                        need(pe, o_steps, 6 * m + 6)
                        turn_to_misc(lambda t: o_int[:, 128 * t:128 * t + 128], W["ident16"][0:N, 0:N], misc16, N, 128).then_inc(o_made, 1)
                    if h == 15 and has_m:
                        need(pe, o_out, 3 * m + 2)
                        for t in range(KT):
                            mm = pe.matmul(misc[0:N, :], o_int_t[:, t, :], W["wo_int"][:, t, :], start=(t == 0), stop=(t == KT - 1))
                        mm.then_inc(o_made, 1)

            iterations(pe, body)



E = 8
SLOTS = 128
PAD_ROWS = SLOTS


def most_tiles(tokens):
    return (2 * tokens + E * (SLOTS - 1)) // SLOTS


def route(nc, W, R, weights_by_token):
    N, B = W["tokens"], W["batches"]
    T, NT = N * B, R["tiles"]
    NTP = NT + NT % 2
    lg = W["logits"]
    with ExitStack() as ctx:
        sb = lambda name, shape, dt=F32: ctx.enter_context(nc.sbuf_tensor(name, shape, dt))
        sem = lambda name: ctx.enter_context(nc.semaphore(name))
        rank_ps = ctx.enter_context(nc.psum_tensor("rank_ps", [128, 512], F32))
        cols_ps = ctx.enter_context(nc.psum_tensor("cols_ps", [128, 512], F32))
        slot_ps = ctx.enter_context(nc.psum_tensor("slot_ps", [128, 512], F32))
        F16 = mybir.dt.float16
        prio = sb("prio", [128, E])
        iota = sb("iota", [128, 128])
        token = sb("token", [128, B])
        pad_row = sb("pad_row", [128, 1])
        below, ones16 = sb("below", [128, 128], BF16), sb("ones16", [128, 128], BF16)
        ones = sb("ones", [128, B])
        top = [sb(f"top{i}", [N, B]) for i in range(2)]
        one = [sb(f"one{i}", [N, B, E]) for i in range(2)]
        rest, work = sb("rest", [N, B, E]), sb("work", [N, B, E])
        best = sb("best", [N, B])
        gap, grown, sum2 = sb("gap", [N, B]), sb("grown", [N, B]), sb("sum2", [N, B])
        share = [sb(f"share{i}", [N, B]) for i in range(2)]
        cw = sb("cw", [N, B, E])
        taken = sb("taken", [N, B, E], BF16)
        until = sb("until", [128, B, E])
        cnt_i, tiles, last, first = sb("cnt_i", [128, E], I32), sb("tiles", [128, E]), sb("last", [128, E]), sb("first", [128, E])
        slot = sb("slot", [N, B, E])
        at = [sb(f"at{i}", [N, B]) for i in range(2)]
        at_i, hi_i, lo_i = sb("at_i", [N, B], I32), sb("hi_i", [N, B], I32), sb("lo_i", [N, B], I32)
        hi_f, lo_f = sb("hi_f", [N, B]), sb("lo_f", [N, B])
        at_row = sb("at_row", [N, 2, B, SLOTS], F16)
        at_tile = sb("at_tile", [N, 2, B, 2, NTP], F16)
        past = sb("past", [128, NTP, E])
        expert = sb("expert", [128, NTP])
        found, number = sb("found", [128, 2, NTP]), sb("number", [128, NTP])
        consts, steps = sem("route_consts"), sem("route_steps")
        grown_done, ranked, placed, stored = sem("grown_done"), sem("ranked"), sem("placed"), sem("weights_stored")
        taken_done, spread_done = sem("taken_done"), sem("at_done")
        block = ctx.enter_context(nc.Block())

        @block.gpsimd
        def _(pool):
            pool.iota(prio[:, :], [[-1, E]], base=E, channel_multiplier=0, allow_small_or_imprecise_dtypes=True).then_inc(consts, 1)
            pool.iota(iota[:, :], [[1, 128]], base=0, channel_multiplier=0, allow_small_or_imprecise_dtypes=True).then_inc(consts, 1)
            pool.iota(token[:, :], [[N, B]], base=-(T // 2), channel_multiplier=1, allow_small_or_imprecise_dtypes=True).then_inc(consts, 1)
            pool.iota(pad_row[:, :], [[1, 1]], base=T, channel_multiplier=1, allow_small_or_imprecise_dtypes=True).then_inc(consts, 1)
            pool.memset(ones16[:, :], 1.0).then_inc(consts, 1)
            pool.memset(below[:, :], 1.0).then_inc(consts, 1)
            pool.memset(ones[:, :], 1.0).then_inc(consts, 1)
            pool.wait_ge(consts, 7)
            pool.affine_select(out=below[:, :], in_=below[:, :], compare_op=ALU.is_gt, fill=0.0, base=0,
                               pattern=[[1, 128]], channel_multiplier=-1).then_inc(consts, 1)

        @block.scalar
        def _(act):
            act.wait_ge(steps, R["gap_step"])
            act.activation(grown[:, :], gap[:, :], ACT.Exp).then_inc(grown_done, 1)

        @block.sync
        def _(sp):
            sp.wait_ge(steps, R["cw_step"])
            sp.dma_start(weights_by_token.rearrange("(b n) e -> n b e", n=N), cw[:, :, :]).then_inc(stored, 16)
            sp.wait_ge(stored, 16)

        @block.tensor
        def _(pe):
            pe.wait_ge(taken_done, 1)
            pe.wait_ge(consts, 8)
            flat = taken[:, :, :].rearrange("p b e -> p (b e)")
            pe.matmul(rank_ps[0:N, 0:B * E], below[0:N, 0:N], flat, start=True, stop=True).then_inc(ranked, 1)
            pe.matmul(cols_ps[:, 0:B * E], ones16[0:N, :], flat, start=True, stop=True).then_inc(ranked, 1)
            for i in range(2):
                pe.wait_ge(spread_done, i + 1)
                for b in range(B):
                    mm = pe.matmul(slot_ps[:, 0:2 * NTP], at_row[:, i, b, :], at_tile[:, i, b, :, :].rearrange("p v t -> p (v t)"),
                                   start=(i == 0 and b == 0), stop=(i == 1 and b == B - 1))
            mm.then_inc(placed, 1)

        @block.vector
        def _(dve):
            count = [0]

            def link(ins):
                count[0] += 1
                ins.then_inc(steps, 1)
                dve.wait_ge(steps, count[0])

            over_b = lambda a: a.unsqueeze(1).to_broadcast([N, B, E])
            over_e = lambda a: a.unsqueeze(2).to_broadcast([N, B, E])
            dve.wait_ge(consts, 8)
            left = lg[0:N, :, :]
            for i in range(2):
                link(dve.tensor_reduce(top[i][:, :], left, AX.X, ALU.max))
                link(dve.tensor_tensor(work[:, :, :], left, over_e(top[i][:, :]), ALU.is_equal))
                link(dve.tensor_tensor(work[:, :, :], work[:, :, :], over_b(prio[0:N, :]), ALU.mult))
                link(dve.tensor_reduce(best[:, :], work[:, :, :], AX.X, ALU.max))
                link(dve.tensor_tensor(one[i][:, :, :], over_b(prio[0:N, :]), over_e(best[:, :]), ALU.is_equal))
                if i == 0:
                    link(dve.scalar_tensor_tensor(rest[:, :, :], one[0][:, :, :], -BIG, left, ALU.mult, ALU.add))
                    left = rest[:, :, :]
            dve.tensor_tensor(taken[:, :, :], one[0][:, :, :], one[1][:, :, :], ALU.add).then_inc(taken_done, 1)
            link(dve.tensor_tensor(gap[:, :], top[1][:, :], top[0][:, :], ALU.subtract))
            assert count[0] == R["gap_step"]
            dve.wait_ge(grown_done, 1)
            link(dve.tensor_scalar(sum2[:, :], grown[:, :], 1.0, None, ALU.add))
            link(dve.reciprocal(share[0][:, :], sum2[:, :]))
            link(dve.tensor_tensor(share[1][:, :], grown[:, :], share[0][:, :], ALU.mult))
            link(dve.tensor_tensor(work[:, :, :], one[1][:, :, :], over_e(share[1][:, :]), ALU.mult))
            link(dve.tensor_tensor(cw[:, :, :], one[0][:, :, :], over_e(share[0][:, :]), ALU.mult))
            link(dve.tensor_tensor(cw[:, :, :], cw[:, :, :], work[:, :, :], ALU.add))
            assert count[0] == R["cw_step"]
            dve.wait_ge(ranked, 2)
            cols = cols_ps[:, 0:B * E].rearrange("p (b e) -> p b e", e=E)
            for e in range(E):
                link(dve.tensor_tensor_scan(until[:, :, e], ones[:, :], cols[:, :, e], 0.0, ALU.mult, ALU.add))
            link(dve.tensor_scalar(cnt_i[:, :], until[:, B - 1, :], float(SLOTS - 1), None, ALU.add))
            link(dve.tensor_scalar(cnt_i[:, :], cnt_i[:, :], 7, None, ALU.arith_shift_right))
            link(dve.tensor_copy(tiles[:, :], cnt_i[:, :]))
            link(dve.tensor_tensor_scan(last[:, :], ones[:, 0:E] if B >= E else prio[:, :], tiles[:, :], 0.0, ALU.mult, ALU.add))
            link(dve.tensor_tensor(first[:, :], last[:, :], tiles[:, :], ALU.subtract))
            link(dve.tensor_scalar(first[:, :], first[:, :], float(SLOTS), None, ALU.mult))
            link(dve.tensor_tensor(slot[:, :, :], until[0:N, :, :], cols[0:N, :, :], ALU.subtract))
            link(dve.tensor_tensor(slot[:, :, :], slot[:, :, :], over_b(first[0:N, :]), ALU.add))
            link(dve.tensor_tensor(slot[:, :, :], slot[:, :, :],
                                   rank_ps[0:N, 0:B * E].rearrange("p (b e) -> p b e", e=E), ALU.add))
            for i in range(2):
                link(dve.tensor_tensor(work[:, :, :], one[i][:, :, :], slot[:, :, :], ALU.mult))
                link(dve.tensor_reduce(at[i][:, :], work[:, :, :], AX.X, ALU.add))
                link(dve.tensor_copy(at_i[:, :], at[i][:, :]))
                link(dve.tensor_scalar(hi_i[:, :], at_i[:, :], 7, None, ALU.arith_shift_right))
                link(dve.tensor_copy(hi_f[:, :], hi_i[:, :]))
                link(dve.scalar_tensor_tensor(lo_f[:, :], hi_f[:, :], -float(SLOTS), at[i][:, :], ALU.mult, ALU.add))
                link(dve.tensor_tensor(at_row[:, i, :, :], iota[0:N, :].unsqueeze(1).to_broadcast([N, B, SLOTS]),
                                       lo_f[:, :].unsqueeze(2).to_broadcast([N, B, SLOTS]), ALU.is_equal))
                link(dve.tensor_tensor(at_tile[:, i, :, 1, :], iota[0:N, 0:NTP].unsqueeze(1).to_broadcast([N, B, NTP]),
                                       hi_f[:, :].unsqueeze(2).to_broadcast([N, B, NTP]), ALU.is_equal))
                dve.tensor_tensor(at_tile[:, i, :, 0, :], at_tile[:, i, :, 1, :],
                                  token[0:N, :].unsqueeze(2).to_broadcast([N, B, NTP]), ALU.mult).then_inc(spread_done, 1)
            link(dve.tensor_tensor(past[:, :, :], iota[:, 0:NTP].unsqueeze(2).to_broadcast([128, NTP, E]),
                                   last[:, :].unsqueeze(1).to_broadcast([128, NTP, E]), ALU.is_ge))
            link(dve.tensor_reduce(expert[:, :], past[:, :, :], AX.X, ALU.add))
            link(dve.tensor_scalar(R["expert"][:, :], expert[:, :], float(E - 1), None, ALU.min))
            dve.wait_ge(placed, 1)
            link(dve.tensor_copy(found[:, :, :], slot_ps[:, 0:2 * NTP].rearrange("p (v t) -> p v t", v=2)))
            link(dve.scalar_tensor_tensor(number[:, :], found[:, 1, :], float(T // 2), found[:, 0, :], ALU.mult, ALU.add))
            link(dve.tensor_copy(R["gather"][:, :], number[:, :]))
            link(dve.tensor_scalar(found[:, 0, :], found[:, 1, :], -1.0, 1.0, ALU.mult, ALU.add))
            link(dve.scalar_tensor_tensor(number[:, :], found[:, 0, :], pad_row[:, 0:1], number[:, :], ALU.mult, ALU.add))
            link(dve.tensor_copy(R["scatter"][:, :], number[:, :]))


def experts(nc, W, R, h2, weights_by_token, gate_up_t, down_t, out):
    NT = R["tiles"]
    C, F2 = gate_up_t.shape[1:]
    F = F2 // 2
    KT, FT = C // 128, -(-F // 128)
    FP = FT * 128
    FK = [min(128, F - 128 * k) for k in range(FT)]
    with ExitStack() as ctx:
        sb = lambda name, shape, dt=F32: ctx.enter_context(nc.sbuf_tensor(name, shape, dt))
        sem = lambda name: ctx.enter_context(nc.semaphore(name))
        bank = lambda name: ctx.enter_context(nc.psum_tensor(name, [128, 512], F32))
        h_ps, a_ps = bank("h_ps"), bank("a_ps")
        gate_ps, up_ps, y_ps = [[bank(f"{n}_ps{i}") for i in range(2)] for n in ("gate", "up", "y")]
        gu = sb("gate_up", [128, E * KT * F2])
        dn = sb("down", [128, E * FT * C])
        rows, cw = sb("rows", [128, 2, C]), sb("cw_rows", [128, 2, E])
        gi, si = [sb(f"gather_idx{i}", [128, 1], I32) for i in range(2)], [sb(f"scatter_idx{i}", [128, 1], I32) for i in range(2)]
        share = sb("row_share", [128, 2])
        h_t = sb("h_t", [128, 2, C])
        silu, a = sb("silu", [128, 2, F]), sb("a", [128, 2, FP])
        a_t = sb("a_t", [128, FP])
        y = sb("y_rows", [128, 2, C])
        zero = sb("zero", [128, C])
        loaded = [sem(f"expert_loaded{e}") for e in range(E)]
        weights_ready, padded, zeroed = sem("weights_ready"), sem("padded"), sem("pad_rows_zeroed")
        pad_written = sem("pad_rows_written")
        gi_set, si_set, go = sem("gi_set"), sem("si_set"), sem("go")
        rows_in, cw_in, scattered = [sem("rows_in0"), sem("rows_in1")], [sem("cw_in0"), sem("cw_in1")], sem("scattered")
        h_turned, h_ready, gated, silu_made, act_made = sem("h_turned"), sem("h_ready"), sem("gated"), sem("silu_made"), sem("act_made")
        a_turned, a_ready, down_made, share_made, y_made = sem("a_turned"), sem("a_ready"), sem("down_made"), sem("share_made"), sem("y_made")

        def need(eng, s, count):
            if not isinstance(count, int) or count > 0:
                eng.wait_ge(s, count)

        def iterations(eng, body):
            lo, hi = 4, NT - 2 - NT % 2
            for t in range(-2, min(lo, NT + 2)):
                body(t, t // 2, t % 2)
            with eng.Fori(lo // 2, hi // 2) as j:
                for k in range(2):
                    body(j * 2 + k, j, k, True)
            for t in range(hi, NT + 2):
                body(t, t // 2, t % 2)

        def exists(t, inside):
            return inside or 0 <= t < NT

        def column(table, t, inside):
            return table[:, bass.ds(t, 1)] if inside else table[:, t:t + 1]

        def expert_of(eng, t, inside):
            return eng.value_load(R["expert"][0:1, bass.ds(t, 1)] if inside else R["expert"][0:1, t:t + 1], min_val=0, max_val=E - 1)

        block = ctx.enter_context(nc.Block())

        @block.sync
        def _(sp):
            sp.wait_ge(zeroed, 1)
            sp.dma_start(out[W["rows"]:W["rows"] + PAD_ROWS, :], zero[:, :]).then_inc(pad_written, 16)
            for e in range(E):
                sp.dma_start(gu[:, e * KT * F2:(e + 1) * KT * F2].rearrange("p (t f) -> p t f", t=KT),
                             gate_up_t[e, :, :].rearrange("(t p) f -> p t f", p=128)).then_inc(loaded[e], 16)
                d = dn[:, e * FT * C:(e + 1) * FT * C].rearrange("p (t c) -> p t c", t=FT)
                full = F // 128
                sp.dma_start(d[:, 0:full, :], down_t[e, 0:128 * full, :].rearrange("(t p) c -> p t c", p=128)).then_inc(loaded[e], 16)
                sp.dma_start(d[0:FK[-1], full, :], down_t[e, 128 * full:F, :]).then_inc(loaded[e], 16)
            for e in range(E):
                sp.wait_ge(loaded[e], 48)
                sp.sem_inc(weights_ready, 1)

        @block.gpsimd
        def _(pool):
            pool.memset(zero[:, :], 0.0).then_inc(zeroed, 1)

            def body(t, half, par, inside=False):
                if exists(t + 2, inside):
                    need(pool, rows_in[par], 16 * (half + 1))
                    need(pool, cw_in[par], 16 * (half + 1))
                    pool.tensor_copy(gi[par][:, :], column(R["gather"], t + 2, inside)).then_inc(gi_set, 1)
                    need(pool, gi_set, t + 3)
                    need(pool, h_turned, t + 1)
                    need(pool, share_made, t + 1)
                    pool.sem_inc(go, 1)
                    pool.indirect_dma_start(rows[:, par, :], None, h2, bass.IndirectOffsetOnAxis(ap=gi[par][:, 0:1], axis=0)).then_inc(rows_in[par], 16)
                    pool.indirect_dma_start(cw[:, par, :], None, weights_by_token, bass.IndirectOffsetOnAxis(ap=gi[par][:, 0:1], axis=0)).then_inc(cw_in[par], 16)
                if exists(t - 2, inside):
                    need(pool, scattered, 16 * (t - 2))
                    pool.tensor_copy(si[par][:, :], column(R["scatter"], t - 2, inside)).then_inc(si_set, 1)
                    need(pool, si_set, t - 1)
                    need(pool, y_made, t - 1)
                    pool.sem_inc(go, 1)
                    pool.indirect_dma_start(out, bass.IndirectOffsetOnAxis(ap=si[par][:, 0:1], axis=0), y[:, par, :], None,
                                            compute_op=ALU.add).then_inc(scattered, 16)

            pool.wait_ge(pad_written, 16)
            iterations(pool, body)
            pool.wait_ge(scattered, 16 * NT)

        @block.scalar
        def _(act):
            def body(t, half, par, inside=False):
                other = 1 - par
                if exists(t - 1, inside):
                    need(act, a_turned, t)
                    need(act, down_made, t - 1)
                    act.activation(a_t[:, :], a_ps[:, 0:FP], ACT.Copy).then_inc(a_ready, 1)
                if exists(t, inside):
                    need(act, gated, t + 1)
                    need(act, act_made, t - 1)
                    act.activation(silu[:, par, :], gate_ps[par][:, 0:F], ACT.Silu).then_inc(silu_made, 1)
                if exists(t - 1, inside):
                    need(act, down_made, t)
                    need(act, share_made, t)
                    need(act, scattered, 16 * (t - 2))
                    act.activation(y[:, other, :], y_ps[other][:, 0:C], ACT.Copy, scale=share[:, other:other + 1]).then_inc(y_made, 1)
                if exists(t + 1, inside):
                    need(act, h_turned, t + 2)
                    need(act, gated, t)
                    act.activation(h_t[:, other, :], h_ps[:, 0:C], ACT.Copy).then_inc(h_ready, 1)

            iterations(act, body)

        @block.vector
        def _(dve):
            dve.memset(a[:, :, F:FP], 0.0).then_inc(padded, 1)

            def body(t, half, par, inside=False):
                if exists(t, inside):
                    e = expert_of(dve, t, inside)
                    need(dve, cw_in[par], 16 * (half + 1))
                    need(dve, y_made, t - 1)
                    dve.tensor_copy(share[:, par:par + 1], cw[:, par, bass.ds(e, 1)]).then_inc(share_made, 1)
                    need(dve, silu_made, t + 1)
                    need(dve, a_turned, t - 1)
                    dve.tensor_tensor(a[:, par, 0:F], silu[:, par, :], up_ps[par][:, 0:F], ALU.mult).then_inc(act_made, 1)

            iterations(dve, body)

        @block.tensor
        def _(pe):
            pe.wait_ge(padded, 1)

            def body(t, half, par, inside=False):
                other = 1 - par
                if exists(t - 1, inside):
                    e1 = expert_of(pe, t - 1, inside)
                    need(pe, act_made, t)
                    need(pe, a_ready, t - 1)
                    for k in range(FT):
                        mm = pe.transpose(a_ps[:, 128 * k:128 * k + 128], a[:, other, 128 * k:128 * k + 128], W["ident"][:, :])
                    mm.then_inc(a_turned, 1)
                if exists(t, inside):
                    e = expert_of(pe, t, inside)
                    pe.wait_ge(weights_ready, e + 1)
                    need(pe, h_ready, t + 1)
                    need(pe, act_made, t - 1)
                    for k in range(KT):
                        for i, ps in enumerate((gate_ps[par], up_ps[par])):
                            mm = pe.matmul(ps[:, 0:F], h_t[:, par, 128 * k:128 * k + 128], gu[:, bass.ds(e * (KT * F2) + (k * F2 + i * F), F)],
                                           start=(k == 0), stop=(k == KT - 1))
                    mm.then_inc(gated, 1)
                if exists(t - 1, inside):
                    need(pe, a_ready, t)
                    need(pe, y_made, t - 2)
                    for k in range(FT):
                        mm = pe.matmul(y_ps[other][:, 0:C], a_t[0:FK[k], 128 * k:128 * k + 128], dn[0:FK[k], bass.ds(e1 * (FT * C) + k * C, C)],
                                       start=(k == 0), stop=(k == FT - 1))
                    mm.then_inc(down_made, 1)
                if exists(t + 1, inside):
                    need(pe, rows_in[other], 16 * ((par + 1) // 2 + half + 1))
                    need(pe, h_ready, t + 1)
                    for k in range(KT):
                        mm = pe.transpose(h_ps[:, 128 * k:128 * k + 128], rows[:, other, 128 * k:128 * k + 128], W["ident"][:, :])
                    mm.then_inc(h_turned, 1)

            iterations(pe, body)


def program(nc, x, ctx_t, mask, wq, bq, wk_t, bk, wv_t, bv, wo, bo, gate_up_t, down_t, router_t, out):
    B, N, C = x.shape
    T = B * N
    h2 = nc.dram_tensor("h2_rows", (T, C), F32, kind="Internal").ap()
    weights_by_token = nc.dram_tensor("weights_by_token", (T, E), F32, kind="Internal").ap()
    with ExitStack() as ctx:
        sb = lambda name, shape, dt=F32: ctx.enter_context(nc.sbuf_tensor(name, shape, dt))
        W = {"tokens": N, "batches": B, "rows": T, "ident": sb("ident", [128, 128]), "ident16": sb("ident16", [128, 128], BF16),
             "logits": sb("logits", [128, B, E])}
        with ExitStack() as first:
            sb = lambda name, shape, dt=F32: first.enter_context(nc.sbuf_tensor(name, shape, dt))
            W.update({n: sb(n, [128, 4, C], F32R) for n in ("wk_hi", "wk_lo", "wv_hi", "wv_lo")})
            W.update({n: sb(n, [128, 4, C], BF16) for n in ("wq_int", "wo_int")})
            W.update({n: sb(n, [128, C]) for n in ("wq_row", "wo_row", "bq_row", "bv_row", "bo_row")})
            W.update(bk_col=sb("bk_col", [128, 4]), router=sb("router", [128, 4, E]), minus_half=sb("minus_half", [128, 1]))
            prepare_weights(nc, W, wq, wk_t, wv_t, wo, bq, bk, bv, bo, router_t)
            attention(nc, W, x, ctx_t, mask, out[0:T, :].rearrange("(b n) c -> b n c", n=N),
                      h2.rearrange("(b n) c -> b n c", n=N))
        sb = lambda name, shape, dt=F32: ctx.enter_context(nc.sbuf_tensor(name, shape, dt))
        NT = most_tiles(T)
        width = NT + NT % 2
        R = {"tiles": NT, "gap_step": 12, "cw_step": 18, "gather": sb("gather", [128, width], I32),
             "scatter": sb("scatter", [128, width], I32), "expert": sb("expert_of_tile", [128, width], I32)}
        route(nc, W, R, weights_by_token)
        experts(nc, W, R, h2, weights_by_token, gate_up_t, down_t, out)


_OUT = "out"


def kernel(x, ctx_2048, mask_BxSxS2_ff0, L0_xattn_wq, L0_xattn_bq, L0_xattn_wk, L0_xattn_bk, L0_xattn_wv, L0_xattn_bv,
           L0_xattn_wo, L0_xattn_bo, L0_ffn_gate_up_proj, L0_ffn_down_proj, L0_ffn_router_w):
    import numpy as np
    import concourse.bacc as bacc
    from concourse import mybir as _mybir
    from concourse.bass_utils import run_bass_kernel_spmd as run

    turn = lambda a, *axes: np.ascontiguousarray(np.transpose(np.asarray(a), axes))
    whole = lambda a: np.ascontiguousarray(np.asarray(a))
    arrays = {
        "x": whole(x), "ctx_t": turn(ctx_2048, 0, 2, 1), "mask": whole(mask_BxSxS2_ff0),
        "wq": whole(L0_xattn_wq), "bq": whole(L0_xattn_bq), "wk_t": turn(L0_xattn_wk, 1, 0), "bk": whole(L0_xattn_bk),
        "wv_t": turn(L0_xattn_wv, 1, 0), "bv": whole(L0_xattn_bv), "wo": whole(L0_xattn_wo), "bo": whole(L0_xattn_bo),
        "gate_up_t": turn(L0_ffn_gate_up_proj, 0, 2, 1), "down_t": turn(L0_ffn_down_proj, 0, 2, 1),
        "router_t": turn(L0_ffn_router_w, 1, 0),
    }
    nc = bacc.Bacc("TRN2", target_bir_lowering=False, num_devices=1)
    aps = {n: nc.dram_tensor(n, a.shape, _mybir.dt.from_np(a.dtype), kind="ExternalInput").ap() for n, a in arrays.items()}
    B, N, C = arrays["x"].shape
    aps[_OUT] = nc.dram_tensor(_OUT, (B * N + PAD_ROWS, C), _mybir.dt.float32, kind="ExternalOutput").ap()
    program(nc, **aps)
    r = run(nc, [arrays], core_ids=[0])
    return r.results[0][_OUT][:B * N].reshape(B, N, C)
```

```python
import concourse.bass as bass
from concourse import mybir
from contextlib import ExitStack

F32 = mybir.dt.float32
F32R = mybir.dt.float32r
BF16 = mybir.dt.bfloat16
I32 = mybir.dt.int32
ALU = mybir.AluOpType
ACT = mybir.ActivationFunctionType
AX = mybir.AxisListType

H = 16
QMAX = 127.0
QEPS = 1e-8
LN_EPS = 1e-5
ROUND = 12582912.0
BIG = 3.0e38
QUARTER = 32


def prepare_weights(nc, W, wq, wk_t, wv_t, wo, bq, bk, bv, bo, router_t):
    C = 512
    KT = C // 128
    D = C // H
    N = W["tokens"]
    with ExitStack() as ctx:
        sb = lambda name, shape, dt=F32: ctx.enter_context(nc.sbuf_tensor(name, shape, dt))
        sem = lambda name: ctx.enter_context(nc.semaphore(name))
        pt = [ctx.enter_context(nc.psum_tensor(f"w_pt{i}", [128, 512], F32)) for i in range(2)]
        ps = ctx.enter_context(nc.psum_tensor("w_ps", [128, 512], F32))
        raw = {n: sb(f"raw_{n}", [128, KT, C]) for n in ("q", "o", "k", "v")}
        low = {n: sb(f"raw_low_{n}", [128, KT, C]) for n in ("k", "v")}
        amax = sb("w_amax", [128, 2, KT])
        scale = sb("w_scale", [128, 2, KT])
        inv = sb("w_inv", [128, 2, KT])
        shifted = sb("w_shifted", [128, 2, KT, C])
        ints = sb("w_ints", [128, 2, KT, C], BF16)
        spread = sb("w_spread", [128, 2, KT, N])
        ones = sb("w_ones", [128, N])
        loaded = {n: sem(f"w_loaded_{n}") for n in ("q", "o", "k", "v")}
        rows_loaded = sem("rows_loaded")
        ident_made, ident_cast = sem("ident_made"), sem("ident_cast")
        amax_done, scale_done, inv_done = sem("w_amax_done"), sem("w_scale_done"), sem("w_inv_done")
        shift_done, ints_done, spread_done = sem("w_shift_done"), sem("w_ints_done"), sem("w_spread_done")
        turned, turned_out = sem("w_turned"), sem("w_turned_out")
        row_made, row_out = sem("w_row_made"), sem("w_row_out")
        high_done, low_done, bias_done = sem("w_high_done"), sem("w_low_done"), sem("w_bias_done")
        pairs = (("q", W["wq_int"], W["wq_row"]), ("o", W["wo_int"], W["wo_row"]))
        inv_sqrt_d = float(1.0 / (float(D) ** 0.5))

        block = ctx.enter_context(nc.Block())

        @block.sync
        def _(sp):
            for n, src in (("q", wq), ("k", wk_t), ("v", wv_t), ("o", wo)):
                sp.dma_start(raw[n][:, :, :], src.rearrange("(t p) c -> p t c", p=128)).then_inc(loaded[n], 16)
            for dst, src in ((W["bq_row"], bq), (W["bv_row"], bv), (W["bo_row"], bo)):
                sp.dma_start(dst[:, :], src.rearrange("(a n) -> a n", a=1).to_broadcast([128, C])).then_inc(rows_loaded, 16)
            with nc.allow_non_contiguous_dma(reason="512 biases, once"):
                sp.dma_start(W["bk_col"][:, :], bk.rearrange("(g p) -> p g", p=128)).then_inc(rows_loaded, 16)
            sp.dma_start(W["router"][:, :, :], router_t.rearrange("(t p) e -> p t e", p=128)).then_inc(rows_loaded, 16)

        @block.gpsimd
        def _(pool):
            pool.memset(W["ident"][:, :], 0.0).then_inc(ident_made, 1)
            pool.memset(W["minus_half"][:, :], -0.5).then_inc(ident_made, 1)
            pool.memset(ones[:, :], 1.0).then_inc(ident_made, 1)
            pool.wait_ge(ident_made, 3)
            pool.affine_select(out=W["ident"][:, :], in_=W["ident"][:, :], compare_op=ALU.not_equal, fill=1.0,
                               base=0, pattern=[[-1, 128]], channel_multiplier=1).then_inc(ident_made, 1)
            pool.wait_ge(ident_made, 4)
            pool.tensor_copy(W["ident16"][:, :], W["ident"][:, :]).then_inc(ident_cast, 1)

        @block.scalar
        def _(act):
            for i, n in enumerate(("k", "v")):
                act.wait_ge(loaded[n], 16)
                for t in range(KT):
                    act.activation(W[f"w{n}_hi"][:, t, :], raw[n][:, t, :], ACT.Identity).then_inc(high_done, 1)

        @block.vector
        def _(dve):
            for i, (n, _, _) in enumerate(pairs):
                dve.wait_ge(loaded[n], 16)
                for t in range(KT):
                    dve.tensor_reduce(amax[:, i, t:t + 1], raw[n][:, t, :], AX.X, ALU.max,
                                      apply_absolute_value=True).then_inc(amax_done, 1)
                dve.wait_ge(amax_done, KT * (i + 1))
                dve.tensor_scalar(scale[:, i, :], amax[:, i, :], 1.0 / QMAX, QEPS, ALU.mult, ALU.max).then_inc(scale_done, 1)
                dve.wait_ge(scale_done, i + 1)
                dve.reciprocal(inv[:, i, :], scale[:, i, :]).then_inc(inv_done, 1)
                dve.wait_ge(inv_done, i + 1)
                for t in range(KT):
                    dve.tensor_scalar(shifted[:, i, t, :], raw[n][:, t, :], inv[:, i, t:t + 1], ROUND,
                                      ALU.mult, ALU.add).then_inc(shift_done, 1)
                dve.wait_ge(shift_done, KT * (i + 1))
                for t in range(KT):
                    dve.tensor_scalar(ints[:, i, t, :], shifted[:, i, t, :], ROUND, None,
                                      ALU.subtract).then_inc(ints_done, 1)
                dve.wait_ge(ident_made, 3)
                for t in range(KT):
                    dve.tensor_scalar(spread[:, i, t, :], ones[:, :], scale[:, i, t:t + 1], None,
                                      ALU.mult).then_inc(spread_done, 1)
            for i, n in enumerate(("k", "v")):
                dve.wait_ge(high_done, KT * (i + 1))
                for t in range(KT):
                    dve.tensor_tensor(W[f"w{n}_lo"][:, t, :], raw[n][:, t, :], W[f"w{n}_hi"][:, t, :].bitcast(F32),
                                      ALU.subtract).then_inc(low_done, 1)
            for i, (_, dst, _) in enumerate(pairs):
                for t in range(KT):
                    k = KT * i + t
                    dve.wait_ge(turned, k + 1)
                    dve.tensor_scalar(dst[:, t, :], pt[k % 2][:, :].bitcast(BF16)[:, 0:C], QMAX, -QMAX,
                                      ALU.min, ALU.max).then_inc(turned_out, 1)
            dve.wait_ge(rows_loaded, 16 * 5)
            for i, (_, _, row) in enumerate(pairs):
                dve.wait_ge(row_made, i + 1)
                dve.tensor_scalar(row[0:N, :], ps[0:N, :], -inv_sqrt_d if i == 0 else 1.0, None,
                                  ALU.mult).then_inc(row_out, 1)
            dve.tensor_scalar(W["bq_row"][:, :], W["bq_row"][:, :], -inv_sqrt_d, None, ALU.mult).then_inc(bias_done, 1)

        @block.tensor
        def _(pe):
            pe.wait_ge(ident_cast, 1)
            for i in range(2):
                pe.wait_ge(ints_done, KT * (i + 1))
                for t in range(KT):
                    k = KT * i + t
                    if k >= 2:
                        pe.wait_ge(turned_out, k - 1)
                    for o in range(KT):
                        mm = pe.transpose(pt[k % 2][:, :].bitcast(BF16)[:, 128 * o:128 * o + 128],
                                          ints[:, i, o, 128 * t:128 * t + 128], W["ident16"][:, :])
                    mm.then_inc(turned, 1)
            for i in range(2):
                pe.wait_ge(spread_done, KT * (i + 1))
                if i:
                    pe.wait_ge(row_out, i)
                for t in range(KT):
                    mm = pe.matmul(ps[0:N, 128 * t:128 * t + 128], spread[:, i, t, :], W["ident"][:, :],
                                   start=True, stop=True)
                mm.then_inc(row_made, 1)


def attention(nc, W, x, ctx_t, mask, x1, h2):
    B, N, C = x.shape
    L = ctx_t.shape[2]
    LP = L + L % 2
    KT = C // 128
    G4 = H // 4
    LT = 3
    LC = L // LT
    assert L == LT * LC and LC <= 128 and N <= 112 and C == 512
    UNITS = KT + LT
    DS, RING_T = 4, 2
    KDMAS, QDMAS = 12, 12

    with ExitStack() as ctx:
        sb = lambda name, shape, dt=F32: ctx.enter_context(nc.sbuf_tensor(name, shape, dt))
        sem = lambda name: ctx.enter_context(nc.semaphore(name))
        bank = lambda name: ctx.enter_context(nc.psum_tensor(name, [128, 512], F32))
        proj, score, turn = [bank("proj0"), bank("proj1")], [bank("score0"), bank("score1")], [bank("turn0"), bank("turn1")]
        out_t, misc = bank("out_t"), bank("misc")
        misc16 = misc[:, :].bitcast(BF16)

        stage = sb("ctx_stage", [128, KT, LP])
        c_hi, c_lo = sb("ctx_hi", [128, 2, KT, LP], F32R), sb("ctx_lo", [128, 2, KT, LP], F32R)
        k_hi, k_lo = sb("k_hi", [128, G4, LP], F32R), sb("k_lo", [128, G4, LP], F32R)
        k_st = sb("k_stack", [96, H, LP], F32R)
        q_hi, q_lo = sb("q_hi", [128, G4, N], F32R), sb("q_lo", [128, G4, N], F32R)
        q_st = sb("q_stack", [96, 2, H, N], F32R)
        v = sb("v", [LC, 2, LT, C])
        neg_mask = sb("neg_mask", [N, 2, L])
        probs = sb("probs", [N, DS, L])
        probs_t = sb("probs_t", [LC, RING_T, LT, N])
        neg_max, total = sb("neg_max", [N, 2, H]), sb("total", [N, 2, H])
        x_in, x_res = sb("x_in", [N, 2, C]), sb("x_res", [N, C])
        stats, mv, rstd = sb("stats", [N, 6]), sb("mv", [N, 2]), sb("rstd", [N, 1])
        var_eps = sb("var_eps", [N, 1])
        shifted = sb("shifted", [N, C])
        x_amax, x_scale, x_inv = sb("x_amax", [N, 1]), sb("x_scale", [N, 2]), sb("x_inv", [N, 1])
        x_int, x_int_t = sb("x_int", [N, C], BF16), sb("x_int_t", [128, KT, N], BF16)
        q_tok = sb("q_tok", [N, C])
        out_ts = sb("out_ts", [128, G4, N])
        inv_total = sb("inv_total", [N, H])
        o_tok = sb("o_tok", [N, C])
        o_amax, o_scale, o_inv = sb("o_amax", [N, 1]), sb("o_scale", [N, 1]), sb("o_inv", [N, 1])
        o_int, o_int_t = sb("o_int", [N, C], BF16), sb("o_int_t", [128, KT, N], BF16)
        y = sb("y", [N, C])
        x1_s = sb("x1_s", [N, C])
        stats2, mv2, rstd2, var_eps2 = sb("stats2", [N, 6]), sb("mv2", [N, 2]), sb("rstd2", [N, 1]), sb("var_eps2", [N, 1])
        h2_s = sb("h2_s", [N, C])
        h2_t = sb("h2_t", [128, KT, N])
        WG, WD = W["gate_up_flat"].shape[1] // B, W["down_flat"].shape[1] // B
        w_raw, w_hi, w_lo = sb("w_raw", [128, WG + WD]), sb("w_hi", [128, WG + WD], F32R), sb("w_lo", [128, WG + WD], F32R)

        ctx_in, x_in_ld, x_res_ld, mask_in = sem("ctx_in"), sem("x_in_ld"), sem("x_res_ld"), sem("mask_in")
        stage_pad = sem("stage_pad")
        c_hi_made, c_lo_made = sem("c_hi_made"), sem("c_lo_made")
        unit_made, unit_out = sem("unit_made"), sem("unit_out")
        k_hi_made, k_stacked = sem("k_hi_made"), [sem("k_stacked0"), sem("k_stacked1")]
        ln1, rstd_made = sem("ln1"), sem("rstd_made")
        q_made, q_out = sem("q_made"), sem("q_out")
        q_biased, q_hi_made, q_stacked = sem("q_biased"), sem("q_hi_made"), sem("q_stacked")
        mask_negated = sem("mask_negated")
        scored, masked, softmaxed = sem("scored"), sem("masked"), sem("softmaxed")
        turned, turned_out, valued = sem("turned"), sem("turned_out"), sem("valued")
        out_t_out = sem("out_t_out")
        o_made, o_out, o_steps = sem("o_made"), sem("o_out"), sem("o_steps")
        x1_steps, ln2, rstd2_made = sem("x1_steps"), sem("ln2"), sem("rstd2_made")
        r_made, r_out = sem("r_made"), sem("r_out")
        x1_stored, h2_stored = sem("x1_stored"), sem("h2_stored")
        w_in, w_hi_made, w_lo_made, w_stored = sem("w_in"), sem("w_hi_made"), sem("w_lo_made"), sem("w_stored")
        waits_taken = sem("waits_taken")

        def need(eng, s, count):
            if not isinstance(count, int) or count > 0:
                eng.wait_ge(s, count)

        def waited(eng):
            eng.sem_inc(waits_taken, 1)

        def iterations(eng, body):
            lo, hi = 3, B - 3 - (B - 6) % 2
            for it in range(-3, min(lo, B + 2)):
                body(it, it)
            with eng.Fori(0, (hi - lo) // 2) as j:
                for k in range(2):
                    body(j * 2 + (lo + k), lo + k, True)
            for it in range(hi, B + 2):
                body(it, it)

        def stages(it, inside):
            if inside:
                return [True] * 6
            return [0 <= it + d < B for d in range(-2, 4)]

        block = ctx.enter_context(nc.Block())

        @block.sync
        def _(sp):
            def stack_keys(half):
                for i in range(4):
                    rows = slice(QUARTER * i, QUARTER * i + QUARTER)
                    for r, src in ((0, k_hi), (1, k_lo), (2, k_hi)):
                        sp.dma_start(k_st[QUARTER * r:QUARTER * r + QUARTER, 8 * half + i:8 * half + 8:4, :].bitcast(F32),
                                     src[rows, 2 * half:2 * half + 2, :].bitcast(F32)).then_inc(k_stacked[half], 16)

            def body(it, par, inside=False):
                has_m2, has_m, has_a, has_n, has_nn, has_n3 = stages(it, inside)
                n, m, m2, n3 = it + 1, it - 1, it - 2, it + 3
                if has_a:
                    need(sp, unit_out, UNITS * it + KT)
                    if inside or it > 0:
                        waited(sp)
                        need(sp, scored, H * it)
                    stack_keys(1)
                    need(sp, w_lo_made, it)
                    sp.dma_start(w_raw[:, 0:WG], W["gate_up_flat"][:, bass.ds(it * WG, WG)]).then_inc(w_in, 16)
                    sp.dma_start(w_raw[:, WG:WG + WD], W["down_flat"][:, bass.ds(it * WD, WD)]).then_inc(w_in, 16)
                if has_n:
                    need(sp, masked, H * (n - 1))
                    sp.dma_start(neg_mask[:, (par + 1) % 2, :], mask[n, :, :]).then_inc(mask_in, 16)
                if has_m2:
                    need(sp, x1_steps, 2 * m2 + 2)
                    sp.dma_start(x1[m2, :, :], x1_s[:, :]).then_inc(x1_stored, 16)
                    need(sp, ln2, 3 * m2 + 3)
                    sp.dma_start(h2[m2, :, :], h2_s[:, :]).then_inc(h2_stored, 16)
                if has_m:
                    need(sp, x1_steps, 2 * m)
                    sp.dma_start(x_res[:, :], x[m, :, :]).then_inc(x_res_ld, 16)
                if has_n:
                    q = (par + 1) % 2
                    need(sp, unit_out, UNITS * n + KT // 2)
                    if has_a:
                        waited(sp)
                        need(sp, scored, H * it + H // 2)
                    stack_keys(0)
                    need(sp, q_out, 3 * n + 3)
                    for i in range(4):
                        rows = slice(QUARTER * i, QUARTER * i + QUARTER)
                        for r, src in ((0, q_hi), (1, q_hi), (2, q_lo)):
                            sp.dma_start(q_st[QUARTER * r:QUARTER * r + QUARTER, q, i:H:4, :].bitcast(F32),
                                         src[rows, :, :].bitcast(F32)).then_inc(q_stacked, 16)
                if has_n3:
                    need(sp, c_lo_made, n3)
                    need(sp, c_hi_made, n3)
                    sp.dma_start(stage[:, :, 0:L], ctx_t[n3, :, :].rearrange("(t p) l -> p t l", p=128)).then_inc(ctx_in, 16)
                    need(sp, ln1, 8 * (n3 - 2) + 7)
                    sp.dma_start(x_in[:, (par + 3) % 2, :], x[n3, :, :]).then_inc(x_in_ld, 16)
                if has_a:
                    need(sp, w_lo_made, it + 1)
                    for src, gate_up_part, down_part in ((w_hi, "gate_up_hi", "down_hi"), (w_lo, "gate_up_lo", "down_lo")):
                        sp.dma_start(W[gate_up_part][:, bass.ds(it * WG, WG)], src[:, 0:WG].bitcast(F32)).then_inc(w_stored, 16)
                        sp.dma_start(W[down_part][:, bass.ds(it * WD, WD)], src[:, WG:WG + WD].bitcast(F32)).then_inc(w_stored, 16)

            iterations(sp, body)
            sp.wait_ge(x1_stored, 16 * B)
            sp.wait_ge(h2_stored, 16 * B)
            sp.wait_ge(w_stored, 64 * B)

        @block.gpsimd
        def _(pool):
            pool.memset(stage[:, :, L:LP], 0.0).then_inc(stage_pad, 1)
            pool.wait_ge(stage_pad, 1)

            def body(it, par, inside=False):
                has_m2, has_m, has_a, has_n, has_nn, _ = stages(it, inside)
                n, m, m2, nn = it + 1, it - 1, it - 2, it + 2
                if has_m2:
                    need(pool, o_out, 3 * m2 + 3)
                    need(pool, x1_steps, 2 * m2 + 1)
                    need(pool, x1_stored, 16 * m2)
                    need(pool, ln2, 3 * m2)
                    pool.tensor_tensor(x1_s[:, :], y[:, :], x_res[:, :], ALU.add).then_inc(x1_steps, 1)
                    need(pool, ln2, 3 * m2 + 2)
                    waited(pool)
                    pool.tensor_scalar(var_eps2[:, :], mv2[:, 1:2], 1.0, LN_EPS, ALU.mult, ALU.add).then_inc(rstd2_made, 1)
                    need(pool, rstd2_made, 2 * m2 + 1)
                    pool.tensor_tensor(rstd2[:, :], var_eps2[:, :], W["minus_half"][0:N, :], ALU.pow).then_inc(rstd2_made, 1)
                if has_n:
                    q = (par + 1) % 2
                    need(pool, mask_in, 16 * (n + 1))
                    waited(pool)
                    pool.tensor_scalar(neg_mask[:, q, :], neg_mask[:, q, :], -1.0, 0.0, ALU.mult, ALU.add).then_inc(mask_negated, 1)
                    need(pool, q_out, 3 * n + 2)
                    need(pool, q_made, 3 * n)
                    pool.tensor_tensor(q_tok[:, :], q_tok[:, :], W["bq_row"][0:N, :], ALU.add).then_inc(q_biased, 1)
                if has_m:
                    need(pool, x_res_ld, 16 * (m + 1))
                    need(pool, x1_steps, 2 * m)
                    pool.tensor_tensor(x_res[:, :], x_res[:, :], W["bo_row"][0:N, :], ALU.add).then_inc(x1_steps, 1)
                if has_nn:
                    need(pool, ln1, 8 * nn + 2)
                    waited(pool)
                    pool.tensor_scalar(var_eps[:, :], mv[:, 1:2], 1.0, LN_EPS, ALU.mult, ALU.add).then_inc(rstd_made, 1)
                    need(pool, rstd_made, 2 * nn + 1)
                    pool.tensor_tensor(rstd[:, :], var_eps[:, :], W["minus_half"][0:N, :], ALU.pow).then_inc(rstd_made, 1)
                    need(pool, c_hi_made, nn + 1)
                    pool.tensor_tensor(c_lo[:, par % 2, :, :], stage[:, :, :], c_hi[:, par % 2, :, :].bitcast(F32),
                                       ALU.subtract).then_inc(c_lo_made, 1)
                if has_a:
                    need(pool, w_hi_made, it + 1)
                    need(pool, w_stored, 64 * it)
                    pool.tensor_tensor(w_lo[:, :], w_raw[:, :], w_hi[:, :].bitcast(F32), ALU.subtract).then_inc(w_lo_made, 1)

            iterations(pool, body)

        @block.scalar
        def _(act):
            def turn_out(b, h):
                k = b * H + h
                need(act, turned, k + 1)
                need(act, valued, k - RING_T + 1)
                act.activation(probs_t[:, h % RING_T, :, :], turn[h % 2][0:LC, 0:LT * N].rearrange("p (l n) -> p l n", l=LT),
                               ACT.Copy).then_inc(turned_out, 1)

            def softmax(b, par, h):
                need(act, masked, b * H + h + 1)
                if h == 0:
                    need(act, o_steps, 6 * (b - 2) + 1)
                act.activation(probs[:, h % DS, :], probs[:, h % DS, :], ACT.Exp, bias=neg_max[:, par % 2, h:h + 1],
                               scale=-1.0, accum_out=total[:, par % 2, h:h + 1]).then_inc(softmaxed, 1)

            def body(it, par, inside=False):
                has_m2, has_m, has_a, has_n, has_nn, _ = stages(it, inside)
                n, m, m2, nn = it + 1, it - 1, it - 2, it + 2
                for h in range(H):
                    if h < 2 and has_m:
                        turn_out(m, H - 2 + h)
                    if h >= 2 and has_a:
                        turn_out(it, h - 2)
                    if h in (3, 5, 7, 9) and has_n:
                        g = h // 2 - 1
                        need(act, unit_made, UNITS * n + g + 1)
                        if g % 2 == 0:
                            need(act, k_stacked[g // 2], 16 * KDMAS * n)
                        act.activation(k_hi[:, g, :], proj[(par + 1 + g) % 2][:, 0:LP], ACT.Identity,
                                       bias=W["bk_col"][:, g:g + 1]).then_inc(k_hi_made, 1)
                    if has_a:
                        softmax(it, par, h)
                    if h == 2 and has_m:
                        need(act, valued, H * (m + 1))
                        need(act, o_made, 3 * (m - 1) + 1)
                        act.activation(out_ts[:, :, :], out_t[:, 0:G4 * N].rearrange("p (g n) -> p g n", g=G4),
                                       ACT.Copy).then_inc(out_t_out, 1)
                    if h == 4 and has_m2:
                        need(act, r_made, 2 * m2 + 1)
                        act.activation(h2_t[:, :, :], misc[:, 0:KT * N].rearrange("p (t n) -> p t n", t=KT),
                                       ACT.Copy).then_inc(r_out, 1)
                    if h == 9 and has_n:
                        need(act, q_made, 3 * n + 3)
                        need(act, q_stacked, 16 * QDMAS * n)
                        act.activation(q_hi[:, :, :], misc[:, 0:G4 * N].rearrange("p (g n) -> p g n", g=G4),
                                       ACT.Identity).then_inc(q_hi_made, 1)
                    if h == 10 and has_nn:
                        need(act, ctx_in, 16 * (nn + 1))
                        if not isinstance(nn, int) or nn < 2:
                            act.wait_ge(stage_pad, 1)
                        need(act, unit_made, UNITS * (nn - 1))
                        act.activation(c_hi[:, par % 2, :, :], stage[:, :, :], ACT.Identity).then_inc(c_hi_made, 1)

                    if h == 12 and has_a:
                        need(act, w_in, 32 * (it + 1))
                        need(act, w_stored, 64 * it)
                        act.activation(w_hi[:, :], w_raw[:, :], ACT.Identity).then_inc(w_hi_made, 1)

            iterations(act, body)

        @block.vector
        def _(dve):
            def quantize(src, amax, scale, inv, shift, ints, chain, base):
                need(dve, chain, base)
                dve.tensor_scalar(scale, amax, 1.0 / QMAX, QEPS, ALU.mult, ALU.max).then_inc(chain, 1)
                need(dve, chain, base + 1)
                dve.reciprocal(inv, scale).then_inc(chain, 1)
                need(dve, chain, base + 2)
                dve.tensor_scalar(shift, src, inv, ROUND, ALU.mult, ALU.add).then_inc(chain, 1)
                need(dve, chain, base + 3)
                dve.tensor_scalar(ints, shift, ROUND, None, ALU.subtract).then_inc(chain, 1)

            def body(it, par, inside=False):
                has_m2, has_m, has_a, has_n, has_nn, _ = stages(it, inside)
                n, m, m2, nn = it + 1, it - 1, it - 2, it + 2
                p, q = par % 2, (par + 1) % 2
                for h in range(H):
                    if has_a:
                        k = it * H + h
                        if h == 0:
                            need(dve, mask_negated, it + 1)
                        need(dve, scored, k + 1)
                        need(dve, turned, k - DS + 1)
                        waited(dve)
                        dve.tensor_tensor_reduce(probs[:, h % DS, :], score[h % 2][0:N, 0:L], neg_mask[:, p, :], 1.0, BIG,
                                                 ALU.add, ALU.min, neg_max[:, p, h:h + 1]).then_inc(masked, 1)
                    if h == 0 and has_m2:
                        need(dve, o_made, 3 * m2 + 3)
                        need(dve, x1_steps, 2 * m2)
                        dve.scalar_tensor_tensor(y[:, :], misc[0:N, :], o_scale[:, 0:1], W["wo_row"][0:N, :],
                                                 ALU.mult, ALU.mult).then_inc(o_out, 1)
                    if h == 2 and has_m2:
                        need(dve, x1_steps, 2 * m2 + 2)
                        dve.bn_stats(stats2[:, :], x1_s[:, :]).then_inc(ln2, 1)
                        need(dve, ln2, 3 * m2 + 1)
                        waited(dve)
                        dve.bn_aggr(mv2[:, :], stats2[:, :]).then_inc(ln2, 1)
                    if h == 3 and has_m2:
                        need(dve, rstd2_made, 2 * m2 + 2)
                        need(dve, h2_stored, 16 * m2)
                        dve.tensor_scalar(h2_s[:, :], x1_s[:, :], mv2[:, 0:1], rstd2[:, 0:1],
                                          ALU.subtract, ALU.mult).then_inc(ln2, 1)
                    if h == 5 and has_m2:
                        need(dve, r_made, 2 * m2 + 2)
                        dve.tensor_copy(W["logits"][0:N, bass.ds(m2, 1), :] if inside else W["logits"][0:N, m2:m2 + 1, :],
                                        misc[0:N, 0:8].rearrange("p (a e) -> p a e", a=1)).then_inc(r_out, 1)
                    if h in (3, 5, 7, 9) and has_n:
                        g = h // 2 - 1
                        need(dve, k_hi_made, G4 * n + g + 1)
                        dve.scalar_tensor_tensor(k_lo[:, g, :], proj[(q + g) % 2][:, 0:LP], W["bk_col"][:, g:g + 1],
                                                 k_hi[:, g, :].bitcast(F32), ALU.add, ALU.subtract).then_inc(unit_out, 1)
                    if h == 6 and has_n:
                        need(dve, q_made, 3 * n + 1)
                        dve.tensor_scalar(x_int_t[:, :, :], misc16[:, 0:KT * N].rearrange("p (t n) -> p t n", t=KT),
                                          QMAX, -QMAX, ALU.min, ALU.max).then_inc(q_out, 1)
                    if h == 8 and has_n:
                        need(dve, q_made, 3 * n + 2)
                        dve.scalar_tensor_tensor(q_tok[:, :], misc[0:N, :], x_scale[:, q:q + 1], W["wq_row"][0:N, :],
                                                 ALU.mult, ALU.mult).then_inc(q_out, 1)
                    if h == 10 and has_n:
                        need(dve, q_hi_made, n + 1)
                        dve.tensor_tensor(q_lo[:, :, :], misc[:, 0:G4 * N].rearrange("p (g n) -> p g n", g=G4),
                                          q_hi[:, :, :].bitcast(F32), ALU.subtract).then_inc(q_out, 1)
                    if h in (11, 13, 15) and has_n:
                        l = (h - 11) // 2
                        need(dve, unit_made, UNITS * n + KT + 1 + l)
                        if l == 0:
                            need(dve, valued, H * (n - 1))
                        dve.tensor_tensor(v[:, q, l, :], proj[(q + KT + l) % 2][0:LC, :], W["bv_row"][0:LC, :],
                                          ALU.add).then_inc(unit_out, 1)
                    if h == 9 and has_nn:
                        need(dve, x_in_ld, 16 * (nn + 1))
                        dve.bn_stats(stats[:, :], x_in[:, p, :]).then_inc(ln1, 1)
                        need(dve, ln1, 8 * nn + 1)
                        waited(dve)
                        dve.bn_aggr(mv[:, :], stats[:, :]).then_inc(ln1, 1)
                    if h == 10 and has_nn:
                        need(dve, rstd_made, 2 * nn + 2)
                        dve.tensor_scalar(x_in[:, p, :], x_in[:, p, :], mv[:, 0:1], rstd[:, 0:1],
                                          ALU.subtract, ALU.mult).then_inc(ln1, 1)
                    if h == 11 and has_m:
                        need(dve, softmaxed, H * (m + 1))
                        dve.reciprocal(inv_total[:, :], total[:, q, :]).then_inc(o_steps, 1)
                        need(dve, o_steps, 6 * m + 1)
                        need(dve, o_made, 3 * m + 1)
                        dve.tensor_tensor(o_tok[:, :].rearrange("p (h d) -> p h d", h=H),
                                          misc[0:N, :].rearrange("p (h d) -> p h d", h=H),
                                          inv_total[:, :].unsqueeze(2).to_broadcast([N, H, C // H]), ALU.mult).then_inc(o_out, 1)
                        need(dve, o_out, 3 * m + 1)
                        dve.tensor_reduce(o_amax[:, :], o_tok[:, :], AX.X, ALU.max, apply_absolute_value=True).then_inc(o_steps, 1)
                    if h == 12 and has_m:
                        quantize(o_tok[:, :], o_amax[:, :], o_scale[:, :], o_inv[:, :], shifted[:, :], o_int[:, :], o_steps, 6 * m + 2)
                    if h == 12 and has_nn:
                        need(dve, ln1, 8 * nn + 3)
                        dve.tensor_reduce(x_amax[:, :], x_in[:, p, :], AX.X, ALU.max, apply_absolute_value=True).then_inc(ln1, 1)
                    if h == 13 and has_m:
                        need(dve, o_made, 3 * m + 2)
                        dve.tensor_scalar(o_int_t[:, :, :], misc16[:, 0:KT * N].rearrange("p (t n) -> p t n", t=KT),
                                          QMAX, -QMAX, ALU.min, ALU.max).then_inc(o_out, 1)
                    if h == 14 and has_nn:
                        need(dve, q_made, 3 * (nn - 1) + 1)
                        quantize(x_in[:, p, :], x_amax[:, :], x_scale[:, p:p + 1], x_inv[:, :], shifted[:, :], x_int[:, :], ln1, 8 * nn + 4)

            iterations(dve, body)

        @block.tensor
        def _(pe):
            def scores(b, par, h):
                k = b * H + h
                if h % 8 == 0:
                    need(pe, k_stacked[h // 8], 16 * KDMAS * (b + 1))
                if h == 0:
                    need(pe, q_stacked, 16 * QDMAS * (b + 1))
                need(pe, masked, k - 1)
                pe.matmul(score[h % 2][0:N, 0:LP], q_st[:, par % 2, h, :], k_st[:, h, :],
                          start=True, stop=True).then_inc(scored, 1)

            def turn_probs(b, h):
                k = b * H + h
                need(pe, softmaxed, k + 1)
                need(pe, turned_out, k - 1)
                for l in range(LT):
                    mm = pe.transpose(turn[h % 2][0:LC, l * N:(l + 1) * N], probs[:, h % DS, l * LC:(l + 1) * LC],
                                      W["ident"][0:N, 0:N])
                mm.then_inc(turned, 1)

            def values(b, par, h):
                k = b * H + h
                if h == 0:
                    need(pe, unit_out, UNITS * (b + 1))
                    need(pe, out_t_out, b)
                need(pe, turned_out, k + 1)
                i, g = h % 4, h // 4
                for l in range(LT):
                    mm = pe.matmul(out_t[QUARTER * i:QUARTER * i + QUARTER, g * N:(g + 1) * N],
                                   v[:, par % 2, l, QUARTER * h:QUARTER * h + QUARTER], probs_t[:, h % RING_T, l, :],
                                   start=(l == 0), stop=(l == LT - 1), skip_group_check=True)
                mm.then_inc(valued, 1)

            def project(n, q, u, t):
                if u == 0 and t == 0:
                    need(pe, c_lo_made, n + 1)
                    need(pe, c_hi_made, n + 1)
                if t == 0:
                    need(pe, unit_out, UNITS * n + u - 1)
                bank = proj[(q + u) % 2]
                if u < KT:
                    for w, c in (("wk_hi", c_hi), ("wk_hi", c_lo), ("wk_lo", c_hi)):
                        mm = pe.matmul(bank[:, 0:LP], W[w][:, t, 128 * u:128 * u + 128], c[:, q, t, :],
                                       start=(t == 0 and w == "wk_hi" and c is c_hi), stop=(t == KT - 1 and w == "wk_lo"))
                else:
                    l = u - KT
                    for w, c in (("wv_hi", c_hi), ("wv_lo", c_hi), ("wv_hi", c_lo)):
                        mm = pe.matmul(bank[0:LC, :], c[:, q, t, l * LC:(l + 1) * LC], W[w][:, t, :],
                                       start=(t == 0 and w == "wv_hi" and c is c_hi), stop=(t == KT - 1 and c is c_lo))
                if t == KT - 1:
                    mm.then_inc(unit_made, 1)

            def turn_to_misc(src, ident, dst, rows, cols):
                for t in range(KT):
                    mm = pe.transpose(dst[0:cols, t * rows:(t + 1) * rows], src(t), ident)
                return mm

            def body(it, par, inside=False):
                has_m2, has_m, has_a, has_n, has_nn, _ = stages(it, inside)
                n, m, m2, nn = it + 1, it - 1, it - 2, it + 2
                p, q = par % 2, (par + 1) % 2
                for h in range(H):
                    if has_a:
                        scores(it, par, h)
                    if h < 2 and has_m:
                        turn_probs(m, H - 2 + h)
                    if h >= 2 and has_a:
                        turn_probs(it, h - 2)
                    if h < 3 and has_m:
                        values(m, par + 1, H - 3 + h)
                    if h >= 3 and has_a:
                        values(it, par, h - 3)
                    if h < H - 1 and has_n:
                        for step in range(KT * UNITS * h // (H - 1), KT * UNITS * (h + 1) // (H - 1)):
                            project(n, q, step // KT, step % KT)
                    if h == 4 and has_m2:
                        need(pe, ln2, 3 * m2 + 3)
                        need(pe, o_out, 3 * m2 + 3)
                        turn_to_misc(lambda t: h2_s[:, 128 * t:128 * t + 128], W["ident"][0:N, 0:N], misc, N, 128).then_inc(r_made, 1)
                    if h == 5 and has_m2:
                        need(pe, r_out, 2 * m2 + 1)
                        for t in range(KT):
                            mm = pe.matmul(misc[0:N, 0:8], h2_t[:, t, :], W["router"][:, t, :], start=(t == 0), stop=(t == KT - 1))
                        mm.then_inc(r_made, 1)
                    if h == 6 and has_n:
                        need(pe, ln1, 8 * n + 8)
                        need(pe, q_out, 3 * n)
                        if has_m2:
                            need(pe, r_out, 2 * m2 + 2)
                        turn_to_misc(lambda t: x_int[:, 128 * t:128 * t + 128], W["ident16"][0:N, 0:N], misc16, N, 128).then_inc(q_made, 1)
                    if h == 7 and has_n:
                        need(pe, q_out, 3 * n + 1)
                        for t in range(KT):
                            mm = pe.matmul(misc[0:N, :], x_int_t[:, t, :], W["wq_int"][:, t, :], start=(t == 0), stop=(t == KT - 1))
                        mm.then_inc(q_made, 1)
                    if h == 9 and has_n:
                        need(pe, q_biased, n + 1)
                        turn_to_misc(lambda t: q_tok[:, 128 * t:128 * t + 128], W["ident"][0:N, 0:N], misc, N, 128).then_inc(q_made, 1)
                    if h == 11 and has_m:
                        need(pe, out_t_out, m + 1)
                        if has_n:
                            need(pe, q_out, 3 * n + 3)
                        if has_m2:
                            need(pe, r_out, 2 * m2 + 2)
                        turn_to_misc(lambda t: out_ts[:, t, :], W["ident"][:, :], misc, 128, N).then_inc(o_made, 1)
                    if h == 13 and has_m:
                        need(pe, o_steps, 6 * m + 6)
                        turn_to_misc(lambda t: o_int[:, 128 * t:128 * t + 128], W["ident16"][0:N, 0:N], misc16, N, 128).then_inc(o_made, 1)
                    if h == 15 and has_m:
                        need(pe, o_out, 3 * m + 2)
                        for t in range(KT):
                            mm = pe.matmul(misc[0:N, :], o_int_t[:, t, :], W["wo_int"][:, t, :], start=(t == 0), stop=(t == KT - 1))
                        mm.then_inc(o_made, 1)

            iterations(pe, body)



E = 8
SLOTS = 128
PAD_ROWS = SLOTS


def most_tiles(tokens):
    return (2 * tokens + E * (SLOTS - 1)) // SLOTS


def route(nc, W, R, weights_by_token):
    N, B = W["tokens"], W["batches"]
    T, NT = N * B, R["tiles"]
    NTP = NT + NT % 2
    lg = W["logits"]
    with ExitStack() as ctx:
        sb = lambda name, shape, dt=F32: ctx.enter_context(nc.sbuf_tensor(name, shape, dt))
        sem = lambda name: ctx.enter_context(nc.semaphore(name))
        rank_ps = ctx.enter_context(nc.psum_tensor("rank_ps", [128, 512], F32))
        cols_ps = ctx.enter_context(nc.psum_tensor("cols_ps", [128, 512], F32))
        slot_ps = ctx.enter_context(nc.psum_tensor("slot_ps", [128, 512], F32))
        F16 = mybir.dt.float16
        prio = sb("prio", [128, E])
        iota = sb("iota", [128, 128])
        token = sb("token", [128, B])
        pad_row = sb("pad_row", [128, 1])
        below, ones16 = sb("below", [128, 128], BF16), sb("ones16", [128, 128], BF16)
        ones = sb("ones", [128, B])
        top = [sb(f"top{i}", [N, B]) for i in range(2)]
        one = [sb(f"one{i}", [N, B, E]) for i in range(2)]
        rest, work = sb("rest", [N, B, E]), sb("work", [N, B, E])
        best = sb("best", [N, B])
        gap, grown, sum2 = sb("gap", [N, B]), sb("grown", [N, B]), sb("sum2", [N, B])
        share = [sb(f"share{i}", [N, B]) for i in range(2)]
        cw = sb("cw", [N, B, E])
        taken = sb("taken", [N, B, E], BF16)
        until = sb("until", [128, B, E])
        cnt_i, tiles, last, first = sb("cnt_i", [128, E], I32), sb("tiles", [128, E]), sb("last", [128, E]), sb("first", [128, E])
        slot = sb("slot", [N, B, E])
        at = [sb(f"at{i}", [N, B]) for i in range(2)]
        at_i, hi_i, lo_i = sb("at_i", [N, B], I32), sb("hi_i", [N, B], I32), sb("lo_i", [N, B], I32)
        hi_f, lo_f = sb("hi_f", [N, B]), sb("lo_f", [N, B])
        at_row = sb("at_row", [N, 2, B, SLOTS], F16)
        at_tile = sb("at_tile", [N, 2, B, 2, NTP], F16)
        past = sb("past", [128, NTP, E])
        expert = sb("expert", [128, NTP])
        found, number = sb("found", [128, 2, NTP]), sb("number", [128, NTP])
        consts, steps = sem("route_consts"), sem("route_steps")
        grown_done, ranked, placed, stored = sem("grown_done"), sem("ranked"), sem("placed"), sem("weights_stored")
        taken_done, spread_done = sem("taken_done"), sem("at_done")
        block = ctx.enter_context(nc.Block())

        @block.gpsimd
        def _(pool):
            pool.iota(prio[:, :], [[-1, E]], base=E, channel_multiplier=0, allow_small_or_imprecise_dtypes=True).then_inc(consts, 1)
            pool.iota(iota[:, :], [[1, 128]], base=0, channel_multiplier=0, allow_small_or_imprecise_dtypes=True).then_inc(consts, 1)
            pool.iota(token[:, :], [[N, B]], base=-(T // 2), channel_multiplier=1, allow_small_or_imprecise_dtypes=True).then_inc(consts, 1)
            pool.iota(pad_row[:, :], [[1, 1]], base=T, channel_multiplier=1, allow_small_or_imprecise_dtypes=True).then_inc(consts, 1)
            pool.memset(ones16[:, :], 1.0).then_inc(consts, 1)
            pool.memset(below[:, :], 1.0).then_inc(consts, 1)
            pool.memset(ones[:, :], 1.0).then_inc(consts, 1)
            pool.wait_ge(consts, 7)
            pool.affine_select(out=below[:, :], in_=below[:, :], compare_op=ALU.is_gt, fill=0.0, base=0,
                               pattern=[[1, 128]], channel_multiplier=-1).then_inc(consts, 1)

        @block.scalar
        def _(act):
            act.wait_ge(steps, R["gap_step"])
            act.activation(grown[:, :], gap[:, :], ACT.Exp).then_inc(grown_done, 1)

        @block.sync
        def _(sp):
            load_expert(sp, R, 0)
            load_expert(sp, R, 1)
            sp.wait_ge(steps, R["cw_step"])
            sp.dma_start(weights_by_token.rearrange("(b n) e -> n b e", n=N), cw[:, :, :]).then_inc(stored, 16)
            sp.wait_ge(stored, 16)

        @block.tensor
        def _(pe):
            pe.wait_ge(taken_done, 1)
            pe.wait_ge(consts, 8)
            flat = taken[:, :, :].rearrange("p b e -> p (b e)")
            pe.matmul(rank_ps[0:N, 0:B * E], below[0:N, 0:N], flat, start=True, stop=True).then_inc(ranked, 1)
            pe.matmul(cols_ps[:, 0:B * E], ones16[0:N, :], flat, start=True, stop=True).then_inc(ranked, 1)
            for i in range(2):
                pe.wait_ge(spread_done, i + 1)
                for b in range(B):
                    mm = pe.matmul(slot_ps[:, 0:2 * NTP], at_row[:, i, b, :], at_tile[:, i, b, :, :].rearrange("p v t -> p (v t)"),
                                   start=(i == 0 and b == 0), stop=(i == 1 and b == B - 1))
            mm.then_inc(placed, 1)

        @block.vector
        def _(dve):
            count = [0]

            def link(ins):
                count[0] += 1
                ins.then_inc(steps, 1)
                dve.wait_ge(steps, count[0])

            over_b = lambda a: a.unsqueeze(1).to_broadcast([N, B, E])
            over_e = lambda a: a.unsqueeze(2).to_broadcast([N, B, E])
            dve.wait_ge(consts, 8)
            left = lg[0:N, :, :]
            for i in range(2):
                link(dve.tensor_reduce(top[i][:, :], left, AX.X, ALU.max))
                link(dve.tensor_tensor(work[:, :, :], left, over_e(top[i][:, :]), ALU.is_equal))
                link(dve.tensor_tensor(work[:, :, :], work[:, :, :], over_b(prio[0:N, :]), ALU.mult))
                link(dve.tensor_reduce(best[:, :], work[:, :, :], AX.X, ALU.max))
                link(dve.tensor_tensor(one[i][:, :, :], over_b(prio[0:N, :]), over_e(best[:, :]), ALU.is_equal))
                if i == 0:
                    link(dve.scalar_tensor_tensor(rest[:, :, :], one[0][:, :, :], -BIG, left, ALU.mult, ALU.add))
                    left = rest[:, :, :]
            dve.tensor_tensor(taken[:, :, :], one[0][:, :, :], one[1][:, :, :], ALU.add).then_inc(taken_done, 1)
            link(dve.tensor_tensor(gap[:, :], top[1][:, :], top[0][:, :], ALU.subtract))
            assert count[0] == R["gap_step"]
            dve.wait_ge(grown_done, 1)
            link(dve.tensor_scalar(sum2[:, :], grown[:, :], 1.0, None, ALU.add))
            link(dve.reciprocal(share[0][:, :], sum2[:, :]))
            link(dve.tensor_tensor(share[1][:, :], grown[:, :], share[0][:, :], ALU.mult))
            link(dve.tensor_tensor(work[:, :, :], one[1][:, :, :], over_e(share[1][:, :]), ALU.mult))
            link(dve.tensor_tensor(cw[:, :, :], one[0][:, :, :], over_e(share[0][:, :]), ALU.mult))
            link(dve.tensor_tensor(cw[:, :, :], cw[:, :, :], work[:, :, :], ALU.add))
            assert count[0] == R["cw_step"]
            dve.wait_ge(ranked, 2)
            cols = cols_ps[:, 0:B * E].rearrange("p (b e) -> p b e", e=E)
            for e in range(E):
                link(dve.tensor_tensor_scan(until[:, :, e], ones[:, :], cols[:, :, e], 0.0, ALU.mult, ALU.add))
            link(dve.tensor_scalar(cnt_i[:, :], until[:, B - 1, :], float(SLOTS - 1), None, ALU.add))
            link(dve.tensor_scalar(cnt_i[:, :], cnt_i[:, :], 7, None, ALU.arith_shift_right))
            link(dve.tensor_copy(tiles[:, :], cnt_i[:, :]))
            link(dve.tensor_tensor_scan(last[:, :], ones[:, 0:E] if B >= E else prio[:, :], tiles[:, :], 0.0, ALU.mult, ALU.add))
            link(dve.tensor_tensor(first[:, :], last[:, :], tiles[:, :], ALU.subtract))
            link(dve.tensor_scalar(first[:, :], first[:, :], float(SLOTS), None, ALU.mult))
            link(dve.tensor_tensor(slot[:, :, :], until[0:N, :, :], cols[0:N, :, :], ALU.subtract))
            link(dve.tensor_tensor(slot[:, :, :], slot[:, :, :], over_b(first[0:N, :]), ALU.add))
            link(dve.tensor_tensor(slot[:, :, :], slot[:, :, :],
                                   rank_ps[0:N, 0:B * E].rearrange("p (b e) -> p b e", e=E), ALU.add))
            for i in range(2):
                link(dve.tensor_tensor(work[:, :, :], one[i][:, :, :], slot[:, :, :], ALU.mult))
                link(dve.tensor_reduce(at[i][:, :], work[:, :, :], AX.X, ALU.add))
                link(dve.tensor_copy(at_i[:, :], at[i][:, :]))
                link(dve.tensor_scalar(hi_i[:, :], at_i[:, :], 7, None, ALU.arith_shift_right))
                link(dve.tensor_copy(hi_f[:, :], hi_i[:, :]))
                link(dve.scalar_tensor_tensor(lo_f[:, :], hi_f[:, :], -float(SLOTS), at[i][:, :], ALU.mult, ALU.add))
                link(dve.tensor_tensor(at_row[:, i, :, :], iota[0:N, :].unsqueeze(1).to_broadcast([N, B, SLOTS]),
                                       lo_f[:, :].unsqueeze(2).to_broadcast([N, B, SLOTS]), ALU.is_equal))
                link(dve.tensor_tensor(at_tile[:, i, :, 1, :], iota[0:N, 0:NTP].unsqueeze(1).to_broadcast([N, B, NTP]),
                                       hi_f[:, :].unsqueeze(2).to_broadcast([N, B, NTP]), ALU.is_equal))
                dve.tensor_tensor(at_tile[:, i, :, 0, :], at_tile[:, i, :, 1, :],
                                  token[0:N, :].unsqueeze(2).to_broadcast([N, B, NTP]), ALU.mult).then_inc(spread_done, 1)
            link(dve.tensor_tensor(past[:, :, :], iota[:, 0:NTP].unsqueeze(2).to_broadcast([128, NTP, E]),
                                   last[:, :].unsqueeze(1).to_broadcast([128, NTP, E]), ALU.is_ge))
            link(dve.tensor_reduce(expert[:, :], past[:, :, :], AX.X, ALU.add))
            link(dve.tensor_scalar(R["expert"][:, :], expert[:, :], float(E - 1), None, ALU.min))
            link(dve.tensor_copy(R["last"][:, :], last[:, :]))
            dve.wait_ge(placed, 1)
            link(dve.tensor_copy(found[:, :, :], slot_ps[:, 0:2 * NTP].rearrange("p (v t) -> p v t", v=2)))
            link(dve.scalar_tensor_tensor(number[:, :], found[:, 1, :], float(T // 2), found[:, 0, :], ALU.mult, ALU.add))
            link(dve.tensor_copy(R["gather"][:, :], number[:, :]))
            link(dve.tensor_scalar(found[:, 0, :], found[:, 1, :], -1.0, 1.0, ALU.mult, ALU.add))
            link(dve.scalar_tensor_tensor(number[:, :], found[:, 0, :], pad_row[:, 0:1], number[:, :], ALU.mult, ALU.add))
            link(dve.tensor_copy(R["scatter"][:, :], number[:, :]))


EXPERT_DMAS = 8


def load_expert(sp, R, e):
    C, F2 = R["gate_up_dram_hi"].shape[1:]
    F = F2 // 2
    full, KT = F // 128, C // 128
    FT = -(-F // 128)
    piece = 0
    for part in ("hi", "lo"):
        gate_up = R[f"gate_up_{part}"][:, e % 2 * KT * F2:(e % 2 + 1) * KT * F2].bitcast(F32).rearrange("p (t f) -> p t f", t=KT)
        down = R[f"down_{part}"][:, e % 2 * FT * C:(e % 2 + 1) * FT * C].bitcast(F32).rearrange("p (t c) -> p t c", t=FT)
        gate_up_src = R[f"gate_up_dram_{part}"][e, :, :].rearrange("(t p) f -> p t f", p=128)
        down_src = R[f"down_dram_{part}"][e, :, :]
        for dst, src in ((gate_up[:, 0:KT // 2, :], gate_up_src[:, 0:KT // 2, :]),
                         (gate_up[:, KT // 2:KT, :], gate_up_src[:, KT // 2:KT, :]),
                         (down[:, 0:full, :], down_src[0:128 * full, :].rearrange("(t p) c -> p t c", p=128)),
                         (down[0:F - 128 * full, full, :], down_src[128 * full:F, :])):
            if piece and e >= 2:
                sp.wait_ge(R["loaded"][e], 16 * piece)
            sp.dma_start(dst, src).then_inc(R["loaded"][e], 16)
            piece += 1


def experts(nc, W, R, h2, weights_by_token, out):
    NT = R["tiles"]
    C, F2 = R["gate_up_dram_hi"].shape[1:]
    F = F2 // 2
    KT, FT = C // 128, -(-F // 128)
    FP = FT * 128
    FK = [min(128, F - 128 * k) for k in range(FT)]
    with ExitStack() as ctx:
        sb = lambda name, shape, dt=F32: ctx.enter_context(nc.sbuf_tensor(name, shape, dt))
        sem = lambda name: ctx.enter_context(nc.semaphore(name))
        bank = lambda name: ctx.enter_context(nc.psum_tensor(name, [128, 512], F32))
        h_ps, a_ps = bank("h_ps"), bank("a_ps")
        gate_ps, up_ps, y_ps = [[bank(f"{n}_ps{i}") for i in range(2)] for n in ("gate", "up", "y")]
        rows, cw = sb("rows", [128, 2, C]), sb("cw_rows", [128, 2, E])
        gi, si = [sb(f"gather_idx{i}", [128, 1], I32) for i in range(2)], [sb(f"scatter_idx{i}", [128, 1], I32) for i in range(2)]
        share = sb("row_share", [128, 2])
        h_hi, h_lo = sb("h_hi", [128, 2, C], F32R), sb("h_lo", [128, 2, C], F32R)
        silu, a = sb("silu", [128, 2, F]), sb("a", [128, 2, FP])
        a_hi, a_lo = sb("a_hi", [128, FP], F32R), sb("a_lo", [128, FP], F32R)
        y = sb("y_rows", [128, 2, C])
        zero = sb("zero", [128, C])
        padded, zeroed = sem("padded"), sem("pad_rows_zeroed")
        pad_written, place_free = sem("pad_rows_written"), sem("place_free")
        gi_set, si_set, go = sem("gi_set"), sem("si_set"), sem("go")
        rows_in, cw_in, scattered = [sem("rows_in0"), sem("rows_in1")], [sem("cw_in0"), sem("cw_in1")], sem("scattered")
        h_turned, h_hi_made, h_lo_made, gated, silu_made, act_made = sem("h_turned"), sem("h_hi_made"), sem("h_lo_made"), sem("gated"), sem("silu_made"), sem("act_made")
        a_turned, a_hi_made, a_lo_made, down_made, share_made, y_made = sem("a_turned"), sem("a_hi_made"), sem("a_lo_made"), sem("down_made"), sem("share_made"), sem("y_made")

        def need(eng, s, count):
            if not isinstance(count, int) or count > 0:
                eng.wait_ge(s, count)

        def iterations(eng, body):
            lo, hi = 4, NT - 2 - NT % 2
            for t in range(-2, min(lo, NT + 2)):
                body(t, t // 2, t % 2)
            with eng.Fori(lo // 2, hi // 2) as j:
                for k in range(2):
                    body(j * 2 + k, j, k, True)
            for t in range(hi, NT + 2):
                body(t, t // 2, t % 2)

        def exists(t, inside):
            return inside or 0 <= t < NT

        def column(table, t, inside):
            return table[:, bass.ds(t, 1)] if inside else table[:, t:t + 1]

        def expert_of(eng, t, inside):
            return eng.value_load(R["expert"][0:1, bass.ds(t, 1)] if inside else R["expert"][0:1, t:t + 1], min_val=0, max_val=E - 1)

        block = ctx.enter_context(nc.Block())

        @block.sync
        def _(sp):
            sp.wait_ge(zeroed, 1)
            sp.dma_start(out[W["rows"]:W["rows"] + PAD_ROWS, :], zero[:, :]).then_inc(pad_written, 16)
            for e in range(E):
                if e >= 2:
                    sp.wait_ge(down_made, sp.value_load(R["last"][0:1, e - 2:e - 1], min_val=0, max_val=NT) + 1)
                    sp.sem_inc(place_free, 1)
                    load_expert(sp, R, e)
                sp.wait_ge(R["loaded"][e], 16 * EXPERT_DMAS)
                sp.sem_inc(R["weights_ready"], 1)

        @block.gpsimd
        def _(pool):
            pool.memset(zero[:, :], 0.0).then_inc(zeroed, 1)

            def body(t, half, par, inside=False):
                if exists(t + 2, inside):
                    need(pool, rows_in[par], 16 * (half + 1))
                    need(pool, cw_in[par], 16 * (half + 1))
                    pool.tensor_copy(gi[par][:, :], column(R["gather"], t + 2, inside)).then_inc(gi_set, 1)
                    need(pool, gi_set, t + 3)
                    need(pool, h_turned, t + 1)
                    need(pool, share_made, t + 1)
                    pool.sem_inc(go, 1)
                    pool.indirect_dma_start(rows[:, par, :], None, h2, bass.IndirectOffsetOnAxis(ap=gi[par][:, 0:1], axis=0)).then_inc(rows_in[par], 16)
                    pool.indirect_dma_start(cw[:, par, :], None, weights_by_token, bass.IndirectOffsetOnAxis(ap=gi[par][:, 0:1], axis=0)).then_inc(cw_in[par], 16)
                if exists(t - 2, inside):
                    need(pool, scattered, 16 * (t - 2))
                    pool.tensor_copy(si[par][:, :], column(R["scatter"], t - 2, inside)).then_inc(si_set, 1)
                    need(pool, si_set, t - 1)
                    need(pool, y_made, t - 1)
                    pool.sem_inc(go, 1)
                    pool.indirect_dma_start(out, bass.IndirectOffsetOnAxis(ap=si[par][:, 0:1], axis=0), y[:, par, :], None,
                                            compute_op=ALU.add).then_inc(scattered, 16)

            pool.wait_ge(pad_written, 16)
            iterations(pool, body)
            pool.wait_ge(scattered, 16 * NT)

        @block.scalar
        def _(act):
            def body(t, half, par, inside=False):
                other = 1 - par
                if exists(t - 1, inside):
                    need(act, a_turned, t)
                    need(act, down_made, t)
                    act.activation(a_hi[:, :], a_ps[:, 0:FP], ACT.Identity).then_inc(a_hi_made, 1)
                if exists(t + 1, inside):
                    need(act, h_turned, t + 2)
                    need(act, gated, t)
                    act.activation(h_hi[:, other, :], h_ps[:, 0:C], ACT.Identity).then_inc(h_hi_made, 1)
                if exists(t, inside):
                    need(act, gated, t + 1)
                    need(act, act_made, t - 1)
                    act.activation(silu[:, par, :], gate_ps[par][:, 0:F], ACT.Silu).then_inc(silu_made, 1)
                if exists(t - 1, inside):
                    need(act, down_made, t + 1)
                    need(act, share_made, t)
                    need(act, scattered, 16 * (t - 2))
                    act.activation(y[:, other, :], y_ps[other][:, 0:C], ACT.Copy, scale=share[:, other:other + 1]).then_inc(y_made, 1)

            iterations(act, body)

        @block.vector
        def _(dve):
            dve.memset(a[:, :, F:FP], 0.0).then_inc(padded, 1)

            def body(t, half, par, inside=False):
                other = 1 - par
                if exists(t - 1, inside):
                    need(dve, a_hi_made, t)
                    dve.tensor_tensor(a_lo[:, :], a_ps[:, 0:FP], a_hi[:, :].bitcast(F32), ALU.subtract).then_inc(a_lo_made, 1)
                if exists(t + 1, inside):
                    need(dve, h_hi_made, t + 2)
                    dve.tensor_tensor(h_lo[:, other, :], h_ps[:, 0:C], h_hi[:, other, :].bitcast(F32), ALU.subtract).then_inc(h_lo_made, 1)
                if exists(t, inside):
                    e = expert_of(dve, t, inside)
                    need(dve, cw_in[par], 16 * (half + 1))
                    need(dve, y_made, t - 1)
                    dve.tensor_copy(share[:, par:par + 1], cw[:, par, bass.ds(e, 1)]).then_inc(share_made, 1)
                    need(dve, silu_made, t + 1)
                    need(dve, a_turned, t - 1)
                    dve.tensor_tensor(a[:, par, 0:F], silu[:, par, :], up_ps[par][:, 0:F], ALU.mult).then_inc(act_made, 1)

            iterations(dve, body)

        @block.tensor
        def _(pe):
            pe.wait_ge(padded, 1)
            pe.sem_inc(down_made, 1)

            behind = {}

            def gate_and_up(t, par, place, steps):
                for k in steps:
                    for h, w in ((h_hi, "gate_up_hi"), (h_hi, "gate_up_lo"), (h_lo, "gate_up_hi")):
                        for i, ps in enumerate((gate_ps[par], up_ps[par])):
                            mm = pe.matmul(ps[:, 0:F], h[:, par, 128 * k:128 * k + 128],
                                           R[w][:, bass.ds(place * (KT * F2) + (k * F2 + i * F), F)],
                                           start=(k == 0 and h is h_hi and w == "gate_up_hi"), stop=(k == KT - 1 and h is h_lo))
                return mm

            def body(t, half, par, inside=False):
                other = 1 - par
                if exists(t - 1, inside):
                    place1 = (behind["expert"] if inside and par == 1 else expert_of(pe, t - 1, inside)) % 2
                if exists(t, inside):
                    expert = behind["expert"] = expert_of(pe, t, inside)
                    place = expert % 2
                    pe.wait_ge(R["weights_ready"], expert + 1)
                    need(pe, h_lo_made, t + 1)
                    need(pe, act_made, t - 1)
                    gate_and_up(t, par, place, range(KT // 2))
                if exists(t - 1, inside):
                    need(pe, act_made, t)
                    need(pe, a_lo_made, t - 1)
                    for k in range(FT):
                        mm = pe.transpose(a_ps[:, 128 * k:128 * k + 128], a[:, other, 128 * k:128 * k + 128], W["ident"][:, :])
                    mm.then_inc(a_turned, 1)
                if exists(t + 1, inside):
                    need(pe, rows_in[other], 16 * ((par + 1) // 2 + half + 1))
                    need(pe, h_lo_made, t + 1)
                    for k in range(KT):
                        mm = pe.transpose(h_ps[:, 128 * k:128 * k + 128], rows[:, other, 128 * k:128 * k + 128], W["ident"][:, :])
                    mm.then_inc(h_turned, 1)
                if exists(t, inside):
                    gate_and_up(t, par, place, range(KT // 2, KT)).then_inc(gated, 1)
                if exists(t - 1, inside):
                    need(pe, a_lo_made, t)
                    need(pe, y_made, t - 2)
                    for k in range(FT):
                        for h, w in ((a_hi, "down_hi"), (a_hi, "down_lo"), (a_lo, "down_hi")):
                            mm = pe.matmul(y_ps[other][:, 0:C], h[0:FK[k], 128 * k:128 * k + 128],
                                           R[w][0:FK[k], bass.ds(place1 * (FT * C) + k * C, C)],
                                           start=(k == 0 and h is a_hi and w == "down_hi"), stop=(k == FT - 1 and h is a_lo))
                    mm.then_inc(down_made, 1)

            iterations(pe, body)


def program(nc, x, ctx_t, mask, wq, bq, wk_t, bk, wv_t, bv, wo, bo, gate_up_t, down_t, router_t, out):
    B, N, C = x.shape
    T = B * N
    dram = lambda name, shape: nc.dram_tensor(name, shape, F32, kind="Internal").ap()
    h2, weights_by_token = dram("h2_rows", (T, C)), dram("weights_by_token", (T, E))
    gate_up_dram = {part: dram(f"gate_up_dram_{part}", gate_up_t.shape) for part in ("hi", "lo")}
    down_dram = {part: dram(f"down_dram_{part}", down_t.shape) for part in ("hi", "lo")}
    flat = lambda a: a.rearrange("e k n -> (e k n)").rearrange("(p f) -> p f", p=128)
    with ExitStack() as ctx:
        sb = lambda name, shape, dt=F32: ctx.enter_context(nc.sbuf_tensor(name, shape, dt))
        W = {"tokens": N, "batches": B, "rows": T, "ident": sb("ident", [128, 128]), "ident16": sb("ident16", [128, 128], BF16),
             "logits": sb("logits", [128, B, E]), "gate_up_flat": flat(gate_up_t), "down_flat": flat(down_t)}
        for part in ("hi", "lo"):
            W[f"gate_up_{part}"], W[f"down_{part}"] = flat(gate_up_dram[part]), flat(down_dram[part])
        with ExitStack() as first:
            sb = lambda name, shape, dt=F32: first.enter_context(nc.sbuf_tensor(name, shape, dt))
            W.update({n: sb(n, [128, 4, C], F32R) for n in ("wk_hi", "wk_lo", "wv_hi", "wv_lo")})
            W.update({n: sb(n, [128, 4, C], BF16) for n in ("wq_int", "wo_int")})
            W.update({n: sb(n, [128, C]) for n in ("wq_row", "wo_row", "bq_row", "bv_row", "bo_row")})
            W.update(bk_col=sb("bk_col", [128, 4]), router=sb("router", [128, 4, E]), minus_half=sb("minus_half", [128, 1]))
            prepare_weights(nc, W, wq, wk_t, wv_t, wo, bq, bk, bv, bo, router_t)
            attention(nc, W, x, ctx_t, mask, out[0:T, :].rearrange("(b n) c -> b n c", n=N),
                      h2.rearrange("(b n) c -> b n c", n=N))
        sb = lambda name, shape, dt=F32: ctx.enter_context(nc.sbuf_tensor(name, shape, dt))
        NT = most_tiles(T)
        width = NT + NT % 2
        F2, FT = gate_up_t.shape[2], -(-down_t.shape[1] // 128)
        R = {"tiles": NT, "gap_step": 12, "cw_step": 18, "gather": sb("gather", [128, width], I32),
             "scatter": sb("scatter", [128, width], I32), "expert": sb("expert_of_tile", [128, width], I32),
             "last": sb("last_tile", [128, E], I32),
             "loaded": [ctx.enter_context(nc.semaphore(f"expert_loaded{e}")) for e in range(E)],
             "weights_ready": ctx.enter_context(nc.semaphore("weights_ready"))}
        for part in ("hi", "lo"):
            R[f"gate_up_dram_{part}"], R[f"down_dram_{part}"] = gate_up_dram[part], down_dram[part]
            R[f"gate_up_{part}"] = sb(f"gate_up_{part}", [128, 2 * (C // 128) * F2], F32R)
            R[f"down_{part}"] = sb(f"down_{part}", [128, 2 * FT * C], F32R)
        route(nc, W, R, weights_by_token)
        experts(nc, W, R, h2, weights_by_token, out)


_OUT = "out"


def kernel(x, ctx_2048, mask_BxSxS2_ff0, L0_xattn_wq, L0_xattn_bq, L0_xattn_wk, L0_xattn_bk, L0_xattn_wv, L0_xattn_bv,
           L0_xattn_wo, L0_xattn_bo, L0_ffn_gate_up_proj, L0_ffn_down_proj, L0_ffn_router_w):
    import numpy as np
    import concourse.bacc as bacc
    from concourse import mybir as _mybir
    from concourse.bass_utils import run_bass_kernel_spmd as run

    turn = lambda a, *axes: np.ascontiguousarray(np.transpose(np.asarray(a), axes))
    whole = lambda a: np.ascontiguousarray(np.asarray(a))
    arrays = {
        "x": whole(x), "ctx_t": turn(ctx_2048, 0, 2, 1), "mask": whole(mask_BxSxS2_ff0),
        "wq": whole(L0_xattn_wq), "bq": whole(L0_xattn_bq), "wk_t": turn(L0_xattn_wk, 1, 0), "bk": whole(L0_xattn_bk),
        "wv_t": turn(L0_xattn_wv, 1, 0), "bv": whole(L0_xattn_bv), "wo": whole(L0_xattn_wo), "bo": whole(L0_xattn_bo),
        "gate_up_t": turn(L0_ffn_gate_up_proj, 0, 2, 1), "down_t": turn(L0_ffn_down_proj, 0, 2, 1),
        "router_t": turn(L0_ffn_router_w, 1, 0),
    }
    nc = bacc.Bacc("TRN2", target_bir_lowering=False, num_devices=1)
    aps = {n: nc.dram_tensor(n, a.shape, _mybir.dt.from_np(a.dtype), kind="ExternalInput").ap() for n, a in arrays.items()}
    B, N, C = arrays["x"].shape
    aps[_OUT] = nc.dram_tensor(_OUT, (B * N + PAD_ROWS, C), _mybir.dt.float32, kind="ExternalOutput").ap()
    program(nc, **aps)
    r = run(nc, [arrays], core_ids=[0])
    return r.results[0][_OUT][:B * N].reshape(B, N, C)
```

```python
import concourse.bass as bass
from concourse import mybir
from contextlib import ExitStack

F32 = mybir.dt.float32
F32R = mybir.dt.float32r
BF16 = mybir.dt.bfloat16
I32 = mybir.dt.int32
ALU = mybir.AluOpType
ACT = mybir.ActivationFunctionType
AX = mybir.AxisListType

H = 16
QMAX = 127.0
QEPS = 1e-8
LN_EPS = 1e-5
ROUND = 12582912.0
BIG = 3.0e38
QUARTER = 32


def prepare_weights(nc, W, x, ctx_t, wq, wk_t, wv_t, wo, bq, bk, bv, bo, router_t):
    C = 512
    KT = C // 128
    D = C // H
    N = W["tokens"]
    with ExitStack() as ctx:
        sb = lambda name, shape, dt=F32: ctx.enter_context(nc.sbuf_tensor(name, shape, dt))
        sem = lambda name: ctx.enter_context(nc.semaphore(name))
        pt = [ctx.enter_context(nc.psum_tensor(f"w_pt{i}", [128, 512], F32)) for i in range(2)]
        ps = ctx.enter_context(nc.psum_tensor("w_ps", [128, 512], F32))
        raw = {n: sb(f"raw_{n}", [128, KT, C]) for n in ("q", "o", "k", "v")}
        amax = sb("w_amax", [128, 2, KT])
        scale = sb("w_scale", [128, 2, KT])
        inv = sb("w_inv", [128, 2, KT])
        shifted = sb("w_shifted", [128, 2, KT, C])
        ints = sb("w_ints", [128, 2, KT, C], BF16)
        spread = sb("w_spread", [128, 2, KT, N])
        ones = sb("w_ones", [128, N])
        loaded = {n: sem(f"w_loaded_{n}") for n in ("q", "o", "k", "v")}
        rows_loaded = sem("rows_loaded")
        ident_made, ident_cast = sem("ident_made"), sem("ident_cast")
        amax_done, scale_done, inv_done = sem("w_amax_done"), sem("w_scale_done"), sem("w_inv_done")
        shift_done, ints_done, spread_done = sem("w_shift_done"), sem("w_ints_done"), sem("w_spread_done")
        turned, turned_out = sem("w_turned"), sem("w_turned_out")
        row_made, row_out = sem("w_row_made"), sem("w_row_out")
        high_done, low_done, bias_done = sem("w_high_done"), sem("w_low_done"), sem("w_bias_done")
        pairs = (("q", W["wq_int"], W["wq_row"]), ("o", W["wo_int"], W["wo_row"]))
        inv_sqrt_d = float(1.0 / (float(D) ** 0.5))

        block = ctx.enter_context(nc.Block())

        @block.sync
        def _(sp):
            for n, src in (("q", wq), ("k", wk_t), ("v", wv_t), ("o", wo)):
                sp.dma_start(raw[n][:, :, :], src.rearrange("(t p) c -> p t c", p=128)).then_inc(loaded[n], 16)
            sp.dma_start(W["stage"][:, :, 0:ctx_t.shape[2]], ctx_t[0, :, :].rearrange("(t p) l -> p t l", p=128)).then_inc(W["ctx_in"], 16)
            sp.dma_start(W["x_in"][:, 0, :], x[0, :, :]).then_inc(W["x_in_ld"], 16)
            for dst, src in ((W["bq_row"], bq), (W["bv_row"], bv), (W["bo_row"], bo)):
                sp.dma_start(dst[:, :], src.rearrange("(a n) -> a n", a=1).to_broadcast([128, C])).then_inc(rows_loaded, 16)
            with nc.allow_non_contiguous_dma(reason="512 biases, once"):
                sp.dma_start(W["bk_col"][:, :], bk.rearrange("(g p) -> p g", p=128)).then_inc(rows_loaded, 16)
            sp.dma_start(W["router"][:, :, :], router_t.rearrange("(t p) e -> p t e", p=128)).then_inc(rows_loaded, 16)

        @block.gpsimd
        def _(pool):
            pool.memset(W["ident"][:, :], 0.0).then_inc(ident_made, 1)
            pool.memset(W["minus_half"][:, :], -0.5).then_inc(ident_made, 1)
            pool.memset(ones[:, :], 1.0).then_inc(ident_made, 1)
            pool.wait_ge(ident_made, 3)
            pool.affine_select(out=W["ident"][:, :], in_=W["ident"][:, :], compare_op=ALU.not_equal, fill=1.0,
                               base=0, pattern=[[-1, 128]], channel_multiplier=1).then_inc(ident_made, 1)
            pool.wait_ge(ident_made, 4)
            pool.tensor_copy(W["ident16"][:, :], W["ident"][:, :]).then_inc(ident_cast, 1)
            pool.memset(W["stage"][:, :, ctx_t.shape[2]:], 0.0).then_inc(W["stage_pad"], 1)
            for i, n in enumerate(("k", "v")):
                for t in range(KT):
                    pool.wait_ge(high_done, KT * i + t + 1)
                    pool.tensor_tensor(W[f"w{n}_lo"][:, t, :], raw[n][:, t, :], W[f"w{n}_hi"][:, t, :].bitcast(F32),
                                       ALU.subtract).then_inc(low_done, 1)
            pool.wait_ge(W["c_hi_made"], 1)
            pool.tensor_tensor(W["c_lo"][:, 0, :, :], W["stage"][:, :, :], W["c_hi"][:, 0, :, :].bitcast(F32),
                               ALU.subtract).then_inc(W["c_lo_made"], 1)

        @block.scalar
        def _(act):
            for i, n in enumerate(("k", "v")):
                act.wait_ge(loaded[n], 16)
                for t in range(KT):
                    act.activation(W[f"w{n}_hi"][:, t, :], raw[n][:, t, :], ACT.Identity).then_inc(high_done, 1)
            act.wait_ge(ident_made, 3)
            for i in range(2):
                act.wait_ge(scale_done, i + 1)
                for t in range(KT):
                    act.activation(spread[:, i, t, :], ones[:, :], ACT.Copy, scale=scale[:, i, t:t + 1]).then_inc(spread_done, 1)
            act.wait_ge(W["ctx_in"], 16)
            act.wait_ge(W["stage_pad"], 1)
            act.activation(W["c_hi"][:, 0, :, :], W["stage"][:, :, :], ACT.Identity).then_inc(W["c_hi_made"], 1)
            for i, (_, _, row) in enumerate(pairs):
                act.wait_ge(row_made, i + 1)
                act.activation(row[0:N, :], ps[0:N, :], ACT.Copy, scale=-inv_sqrt_d if i == 0 else 1.0).then_inc(row_out, 1)

        @block.vector
        def _(dve):
            for i, (n, _, _) in enumerate(pairs):
                dve.wait_ge(loaded[n], 16)
                for t in range(KT):
                    dve.tensor_reduce(amax[:, i, t:t + 1], raw[n][:, t, :], AX.X, ALU.max,
                                      apply_absolute_value=True).then_inc(amax_done, 1)
                dve.wait_ge(amax_done, KT * (i + 1))
                dve.tensor_scalar(scale[:, i, :], amax[:, i, :], 1.0 / QMAX, QEPS, ALU.mult, ALU.max).then_inc(scale_done, 1)
                dve.wait_ge(scale_done, i + 1)
                dve.reciprocal(inv[:, i, :], scale[:, i, :]).then_inc(inv_done, 1)
                dve.wait_ge(inv_done, i + 1)
                for t in range(KT):
                    dve.tensor_scalar(shifted[:, i, t, :], raw[n][:, t, :], inv[:, i, t:t + 1], ROUND,
                                      ALU.mult, ALU.add).then_inc(shift_done, 1)
                dve.wait_ge(shift_done, KT * (i + 1))
                for t in range(KT):
                    dve.tensor_scalar(ints[:, i, t, :], shifted[:, i, t, :], ROUND, None,
                                      ALU.subtract).then_inc(ints_done, 1)
            for i, (_, dst, _) in enumerate(pairs):
                for t in range(KT):
                    k = KT * i + t
                    dve.wait_ge(turned, k + 1)
                    dve.tensor_scalar(dst[:, t, :], pt[k % 2][:, :].bitcast(BF16)[:, 0:C], QMAX, -QMAX,
                                      ALU.min, ALU.max).then_inc(turned_out, 1)
            dve.wait_ge(rows_loaded, 16 * 5)
            dve.tensor_scalar(W["bq_row"][:, :], W["bq_row"][:, :], -inv_sqrt_d, None, ALU.mult).then_inc(bias_done, 1)

        @block.tensor
        def _(pe):
            pe.wait_ge(ident_cast, 1)
            for i in range(2):
                pe.wait_ge(ints_done, KT * (i + 1))
                for t in range(KT):
                    k = KT * i + t
                    if k >= 2:
                        pe.wait_ge(turned_out, k - 1)
                    for o in range(KT):
                        mm = pe.transpose(pt[k % 2][:, :].bitcast(BF16)[:, 128 * o:128 * o + 128],
                                          ints[:, i, o, 128 * t:128 * t + 128], W["ident16"][:, :])
                    mm.then_inc(turned, 1)
                pe.wait_ge(spread_done, KT * (i + 1))
                if i:
                    pe.wait_ge(row_out, i)
                for t in range(KT):
                    mm = pe.matmul(ps[0:N, 128 * t:128 * t + 128], spread[:, i, t, :], W["ident"][:, :],
                                   start=True, stop=True)
                mm.then_inc(row_made, 1)


def attention(nc, W, x, ctx_t, mask, x1, h2):
    B, N, C = x.shape
    L = ctx_t.shape[2]
    LP = L + L % 2
    KT = C // 128
    G4 = H // 4
    LT = 3
    LC = L // LT
    assert L == LT * LC and LC <= 128 and N <= 112 and C == 512
    UNITS = KT + LT
    DS, RING_T = 4, 2
    KDMAS, QDMAS = 12, 12

    with ExitStack() as ctx:
        sb = lambda name, shape, dt=F32: ctx.enter_context(nc.sbuf_tensor(name, shape, dt))
        sem = lambda name: ctx.enter_context(nc.semaphore(name))
        bank = lambda name: ctx.enter_context(nc.psum_tensor(name, [128, 512], F32))
        proj, score, turn = [bank("proj0"), bank("proj1")], [bank("score0"), bank("score1")], [bank("turn0"), bank("turn1")]
        out_t, misc = bank("out_t"), bank("misc")
        misc16 = misc[:, :].bitcast(BF16)

        stage, c_hi, c_lo, x_in = W["stage"], W["c_hi"], W["c_lo"], W["x_in"]
        k_hi, k_lo = sb("k_hi", [128, G4, LP], F32R), sb("k_lo", [128, G4, LP], F32R)
        k_st = sb("k_stack", [96, H, LP], F32R)
        q_hi, q_lo = sb("q_hi", [128, G4, N], F32R), sb("q_lo", [128, G4, N], F32R)
        q_st = sb("q_stack", [96, 2, H, N], F32R)
        v = sb("v", [LC, 2, LT, C])
        neg_mask = sb("neg_mask", [N, 2, L])
        probs = sb("probs", [N, DS, L])
        probs_t = sb("probs_t", [LC, RING_T, LT, N])
        neg_max, total = sb("neg_max", [N, 2, H]), sb("total", [N, 2, H])
        x_res = sb("x_res", [N, C])
        stats, mv, rstd = sb("stats", [N, 6]), sb("mv", [N, 2]), sb("rstd", [N, 1])
        var_eps = sb("var_eps", [N, 1])
        shifted = sb("shifted", [N, C])
        x_amax, x_scale, x_inv = sb("x_amax", [N, 1]), sb("x_scale", [N, 2]), sb("x_inv", [N, 1])
        x_int, x_int_t = sb("x_int", [N, C], BF16), sb("x_int_t", [128, KT, N], BF16)
        q_tok = sb("q_tok", [N, C])
        out_ts = sb("out_ts", [128, G4, N])
        inv_total = sb("inv_total", [N, H])
        o_tok = sb("o_tok", [N, C])
        o_amax, o_scale, o_inv = sb("o_amax", [N, 1]), sb("o_scale", [N, 1]), sb("o_inv", [N, 1])
        o_int, o_int_t = sb("o_int", [N, C], BF16), sb("o_int_t", [128, KT, N], BF16)
        y = sb("y", [N, C])
        x1_s = sb("x1_s", [N, C])
        stats2, mv2, rstd2, var_eps2 = sb("stats2", [N, 6]), sb("mv2", [N, 2]), sb("rstd2", [N, 1]), sb("var_eps2", [N, 1])
        h2_s = sb("h2_s", [N, C])
        h2_t = sb("h2_t", [128, KT, N])
        WG, WD = W["gate_up_flat"].shape[1] // B, W["down_flat"].shape[1] // B
        w_raw, w_hi, w_lo = sb("w_raw", [128, WG + WD]), sb("w_hi", [128, WG + WD], F32R), sb("w_lo", [128, WG + WD], F32R)

        ctx_in, x_in_ld, x_res_ld, mask_in = W["ctx_in"], W["x_in_ld"], sem("x_res_ld"), sem("mask_in")
        c_hi_made, c_lo_made = W["c_hi_made"], W["c_lo_made"]
        unit_made, unit_out = sem("unit_made"), sem("unit_out")
        k_hi_made, k_stacked = sem("k_hi_made"), [sem("k_stacked0"), sem("k_stacked1")]
        ln1, rstd_made = sem("ln1"), sem("rstd_made")
        q_made, q_out = sem("q_made"), sem("q_out")
        q_biased, q_hi_made, q_stacked = sem("q_biased"), sem("q_hi_made"), sem("q_stacked")
        mask_negated = sem("mask_negated")
        scored, masked, softmaxed = sem("scored"), sem("masked"), sem("softmaxed")
        turned, turned_out, valued = sem("turned"), sem("turned_out"), sem("valued")
        out_t_out = sem("out_t_out")
        o_made, o_out, o_steps = sem("o_made"), sem("o_out"), sem("o_steps")
        x1_steps, ln2, rstd2_made = sem("x1_steps"), sem("ln2"), sem("rstd2_made")
        r_made, r_out = sem("r_made"), sem("r_out")
        x1_stored, h2_stored = sem("x1_stored"), sem("h2_stored")
        w_in, w_hi_made, w_lo_made, w_stored = sem("w_in"), sem("w_hi_made"), sem("w_lo_made"), sem("w_stored")
        waits_taken = sem("waits_taken")

        def need(eng, s, count):
            if not isinstance(count, int) or count > 0:
                eng.wait_ge(s, count)

        def waited(eng):
            eng.sem_inc(waits_taken, 1)

        def iterations(eng, body):
            lo, hi = 3, B - 3 - (B - 6) % 2
            for it in range(-3, min(lo, B + 2)):
                body(it, it)
            with eng.Fori(0, (hi - lo) // 2) as j:
                for k in range(2):
                    body(j * 2 + (lo + k), lo + k, True)
            for it in range(hi, B + 2):
                body(it, it)

        def stages(it, inside):
            if inside:
                return [True] * 6
            return [0 <= it + d < B for d in range(-2, 4)]

        block = ctx.enter_context(nc.Block())

        @block.sync
        def _(sp):
            def stack_keys(half):
                for i in range(4):
                    rows = slice(QUARTER * i, QUARTER * i + QUARTER)
                    for r, src in ((0, k_hi), (1, k_lo), (2, k_hi)):
                        sp.dma_start(k_st[QUARTER * r:QUARTER * r + QUARTER, 8 * half + i:8 * half + 8:4, :].bitcast(F32),
                                     src[rows, 2 * half:2 * half + 2, :].bitcast(F32)).then_inc(k_stacked[half], 16)

            def body(it, par, inside=False):
                has_m2, has_m, has_a, has_n, has_nn, has_n3 = stages(it, inside)
                n, m, m2, n3 = it + 1, it - 1, it - 2, it + 3
                if has_a:
                    need(sp, unit_out, UNITS * it + KT)
                    if inside or it > 0:
                        waited(sp)
                        need(sp, scored, H * it)
                    stack_keys(1)
                    need(sp, w_lo_made, it)
                    sp.dma_start(w_raw[:, 0:WG], W["gate_up_flat"][:, bass.ds(it * WG, WG)]).then_inc(w_in, 16)
                    sp.dma_start(w_raw[:, WG:WG + WD], W["down_flat"][:, bass.ds(it * WD, WD)]).then_inc(w_in, 16)
                if has_n:
                    need(sp, masked, H * (n - 1))
                    sp.dma_start(neg_mask[:, (par + 1) % 2, :], mask[n, :, :]).then_inc(mask_in, 16)
                if has_m2:
                    need(sp, x1_steps, 2 * m2 + 2)
                    sp.dma_start(x1[m2, :, :], x1_s[:, :]).then_inc(x1_stored, 16)
                    need(sp, ln2, 3 * m2 + 3)
                    sp.dma_start(h2[m2, :, :], h2_s[:, :]).then_inc(h2_stored, 16)
                if has_m:
                    need(sp, x1_steps, 2 * m)
                    sp.dma_start(x_res[:, :], x[m, :, :]).then_inc(x_res_ld, 16)
                if has_n:
                    q = (par + 1) % 2
                    need(sp, unit_out, UNITS * n + KT // 2)
                    if has_a:
                        waited(sp)
                        need(sp, scored, H * it + H // 2)
                    stack_keys(0)
                    need(sp, q_out, 3 * n + 3)
                    for i in range(4):
                        rows = slice(QUARTER * i, QUARTER * i + QUARTER)
                        for r, src in ((0, q_hi), (1, q_hi), (2, q_lo)):
                            sp.dma_start(q_st[QUARTER * r:QUARTER * r + QUARTER, q, i:H:4, :].bitcast(F32),
                                         src[rows, :, :].bitcast(F32)).then_inc(q_stacked, 16)
                if has_n3 and (inside or n3 > 0):
                    need(sp, c_lo_made, n3)
                    need(sp, c_hi_made, n3)
                    sp.dma_start(stage[:, :, 0:L], ctx_t[n3, :, :].rearrange("(t p) l -> p t l", p=128)).then_inc(ctx_in, 16)
                    need(sp, ln1, 8 * (n3 - 2) + 7)
                    sp.dma_start(x_in[:, (par + 3) % 2, :], x[n3, :, :]).then_inc(x_in_ld, 16)
                if has_a:
                    need(sp, w_lo_made, it + 1)
                    for src, gate_up_part, down_part in ((w_hi, "gate_up_hi", "down_hi"), (w_lo, "gate_up_lo", "down_lo")):
                        sp.dma_start(W[gate_up_part][:, bass.ds(it * WG, WG)], src[:, 0:WG].bitcast(F32)).then_inc(w_stored, 16)
                        sp.dma_start(W[down_part][:, bass.ds(it * WD, WD)], src[:, WG:WG + WD].bitcast(F32)).then_inc(w_stored, 16)

            iterations(sp, body)
            sp.wait_ge(x1_stored, 16 * B)
            sp.wait_ge(h2_stored, 16 * B)
            sp.wait_ge(w_stored, 64 * B)

        @block.gpsimd
        def _(pool):
            def body(it, par, inside=False):
                has_m2, has_m, has_a, has_n, has_nn, _ = stages(it, inside)
                n, m, m2, nn = it + 1, it - 1, it - 2, it + 2
                if has_m2:
                    need(pool, o_out, 3 * m2 + 3)
                    need(pool, x1_steps, 2 * m2 + 1)
                    need(pool, x1_stored, 16 * m2)
                    need(pool, ln2, 3 * m2)
                    pool.tensor_tensor(x1_s[:, :], y[:, :], x_res[:, :], ALU.add).then_inc(x1_steps, 1)
                    need(pool, ln2, 3 * m2 + 2)
                    waited(pool)
                    pool.tensor_scalar(var_eps2[:, :], mv2[:, 1:2], 1.0, LN_EPS, ALU.mult, ALU.add).then_inc(rstd2_made, 1)
                    need(pool, rstd2_made, 2 * m2 + 1)
                    pool.tensor_tensor(rstd2[:, :], var_eps2[:, :], W["minus_half"][0:N, :], ALU.pow).then_inc(rstd2_made, 1)
                if has_n:
                    q = (par + 1) % 2
                    need(pool, mask_in, 16 * (n + 1))
                    waited(pool)
                    pool.tensor_scalar(neg_mask[:, q, :], neg_mask[:, q, :], -1.0, 0.0, ALU.mult, ALU.add).then_inc(mask_negated, 1)
                    need(pool, q_out, 3 * n + 2)
                    need(pool, q_made, 3 * n)
                    pool.tensor_tensor(q_tok[:, :], q_tok[:, :], W["bq_row"][0:N, :], ALU.add).then_inc(q_biased, 1)
                if has_m:
                    need(pool, x_res_ld, 16 * (m + 1))
                    need(pool, x1_steps, 2 * m)
                    pool.tensor_tensor(x_res[:, :], x_res[:, :], W["bo_row"][0:N, :], ALU.add).then_inc(x1_steps, 1)
                if has_nn:
                    need(pool, ln1, 8 * nn + 2)
                    waited(pool)
                    pool.tensor_scalar(var_eps[:, :], mv[:, 1:2], 1.0, LN_EPS, ALU.mult, ALU.add).then_inc(rstd_made, 1)
                    need(pool, rstd_made, 2 * nn + 1)
                    pool.tensor_tensor(rstd[:, :], var_eps[:, :], W["minus_half"][0:N, :], ALU.pow).then_inc(rstd_made, 1)
                if has_nn and (inside or nn > 0):
                    need(pool, c_hi_made, nn + 1)
                    pool.tensor_tensor(c_lo[:, par % 2, :, :], stage[:, :, :], c_hi[:, par % 2, :, :].bitcast(F32),
                                       ALU.subtract).then_inc(c_lo_made, 1)
                if has_a:
                    need(pool, w_hi_made, it + 1)
                    need(pool, w_stored, 64 * it)
                    pool.tensor_tensor(w_lo[:, :], w_raw[:, :], w_hi[:, :].bitcast(F32), ALU.subtract).then_inc(w_lo_made, 1)

            iterations(pool, body)

        @block.scalar
        def _(act):
            def turn_out(b, h):
                k = b * H + h
                need(act, turned, k + 1)
                need(act, valued, k - RING_T + 1)
                act.activation(probs_t[:, h % RING_T, :, :], turn[h % 2][0:LC, 0:LT * N].rearrange("p (l n) -> p l n", l=LT),
                               ACT.Copy).then_inc(turned_out, 1)

            def softmax(b, par, h):
                need(act, masked, b * H + h + 1)
                if h == 0:
                    need(act, o_steps, 6 * (b - 2) + 1)
                act.activation(probs[:, h % DS, :], probs[:, h % DS, :], ACT.Exp, bias=neg_max[:, par % 2, h:h + 1],
                               scale=-1.0, accum_out=total[:, par % 2, h:h + 1]).then_inc(softmaxed, 1)

            def body(it, par, inside=False):
                has_m2, has_m, has_a, has_n, has_nn, _ = stages(it, inside)
                n, m, m2, nn = it + 1, it - 1, it - 2, it + 2
                for h in range(H):
                    if h < 2 and has_m:
                        turn_out(m, H - 2 + h)
                    if h >= 2 and has_a:
                        turn_out(it, h - 2)
                    if h in (3, 5, 7, 9) and has_n:
                        g = h // 2 - 1
                        need(act, unit_made, UNITS * n + g + 1)
                        if g % 2 == 0:
                            need(act, k_stacked[g // 2], 16 * KDMAS * n)
                        act.activation(k_hi[:, g, :], proj[(par + 1 + g) % 2][:, 0:LP], ACT.Identity,
                                       bias=W["bk_col"][:, g:g + 1]).then_inc(k_hi_made, 1)
                    if has_a:
                        softmax(it, par, h)
                    if h == 2 and has_m:
                        need(act, valued, H * (m + 1))
                        need(act, o_made, 3 * (m - 1) + 1)
                        act.activation(out_ts[:, :, :], out_t[:, 0:G4 * N].rearrange("p (g n) -> p g n", g=G4),
                                       ACT.Copy).then_inc(out_t_out, 1)
                    if h == 4 and has_m2:
                        need(act, r_made, 2 * m2 + 1)
                        act.activation(h2_t[:, :, :], misc[:, 0:KT * N].rearrange("p (t n) -> p t n", t=KT),
                                       ACT.Copy).then_inc(r_out, 1)
                    if h == 9 and has_n:
                        need(act, q_made, 3 * n + 3)
                        need(act, q_stacked, 16 * QDMAS * n)
                        act.activation(q_hi[:, :, :], misc[:, 0:G4 * N].rearrange("p (g n) -> p g n", g=G4),
                                       ACT.Identity).then_inc(q_hi_made, 1)
                    if h == 10 and has_nn and (inside or nn > 0):
                        need(act, ctx_in, 16 * (nn + 1))
                        need(act, unit_made, UNITS * (nn - 1))
                        act.activation(c_hi[:, par % 2, :, :], stage[:, :, :], ACT.Identity).then_inc(c_hi_made, 1)

                    if h == 12 and has_a:
                        need(act, w_in, 32 * (it + 1))
                        need(act, w_stored, 64 * it)
                        act.activation(w_hi[:, :], w_raw[:, :], ACT.Identity).then_inc(w_hi_made, 1)

            iterations(act, body)

        @block.vector
        def _(dve):
            def quantize(src, amax, scale, inv, shift, ints, chain, base):
                need(dve, chain, base)
                dve.tensor_scalar(scale, amax, 1.0 / QMAX, QEPS, ALU.mult, ALU.max).then_inc(chain, 1)
                need(dve, chain, base + 1)
                dve.reciprocal(inv, scale).then_inc(chain, 1)
                need(dve, chain, base + 2)
                dve.tensor_scalar(shift, src, inv, ROUND, ALU.mult, ALU.add).then_inc(chain, 1)
                need(dve, chain, base + 3)
                dve.tensor_scalar(ints, shift, ROUND, None, ALU.subtract).then_inc(chain, 1)

            def body(it, par, inside=False):
                has_m2, has_m, has_a, has_n, has_nn, _ = stages(it, inside)
                n, m, m2, nn = it + 1, it - 1, it - 2, it + 2
                p, q = par % 2, (par + 1) % 2
                for h in range(H):
                    if has_a:
                        k = it * H + h
                        if h == 0:
                            need(dve, mask_negated, it + 1)
                        need(dve, scored, k + 1)
                        need(dve, turned, k - DS + 1)
                        waited(dve)
                        dve.tensor_tensor_reduce(probs[:, h % DS, :], score[h % 2][0:N, 0:L], neg_mask[:, p, :], 1.0, BIG,
                                                 ALU.add, ALU.min, neg_max[:, p, h:h + 1]).then_inc(masked, 1)
                    if h == 0 and has_m2:
                        need(dve, o_made, 3 * m2 + 3)
                        need(dve, x1_steps, 2 * m2)
                        dve.scalar_tensor_tensor(y[:, :], misc[0:N, :], o_scale[:, 0:1], W["wo_row"][0:N, :],
                                                 ALU.mult, ALU.mult).then_inc(o_out, 1)
                    if h == 2 and has_m2:
                        need(dve, x1_steps, 2 * m2 + 2)
                        dve.bn_stats(stats2[:, :], x1_s[:, :]).then_inc(ln2, 1)
                        need(dve, ln2, 3 * m2 + 1)
                        waited(dve)
                        dve.bn_aggr(mv2[:, :], stats2[:, :]).then_inc(ln2, 1)
                    if h == 3 and has_m2:
                        need(dve, rstd2_made, 2 * m2 + 2)
                        need(dve, h2_stored, 16 * m2)
                        dve.tensor_scalar(h2_s[:, :], x1_s[:, :], mv2[:, 0:1], rstd2[:, 0:1],
                                          ALU.subtract, ALU.mult).then_inc(ln2, 1)
                    if h == 5 and has_m2:
                        need(dve, r_made, 2 * m2 + 2)
                        dve.tensor_copy(W["logits"][0:N, bass.ds(m2, 1), :] if inside else W["logits"][0:N, m2:m2 + 1, :],
                                        misc[0:N, 0:8].rearrange("p (a e) -> p a e", a=1)).then_inc(r_out, 1)
                    if h in (3, 5, 7, 9) and has_n:
                        g = h // 2 - 1
                        need(dve, k_hi_made, G4 * n + g + 1)
                        dve.scalar_tensor_tensor(k_lo[:, g, :], proj[(q + g) % 2][:, 0:LP], W["bk_col"][:, g:g + 1],
                                                 k_hi[:, g, :].bitcast(F32), ALU.add, ALU.subtract).then_inc(unit_out, 1)
                    if h == 6 and has_n:
                        need(dve, q_made, 3 * n + 1)
                        dve.tensor_scalar(x_int_t[:, :, :], misc16[:, 0:KT * N].rearrange("p (t n) -> p t n", t=KT),
                                          QMAX, -QMAX, ALU.min, ALU.max).then_inc(q_out, 1)
                    if h == 8 and has_n:
                        need(dve, q_made, 3 * n + 2)
                        dve.scalar_tensor_tensor(q_tok[:, :], misc[0:N, :], x_scale[:, q:q + 1], W["wq_row"][0:N, :],
                                                 ALU.mult, ALU.mult).then_inc(q_out, 1)
                    if h == 10 and has_n:
                        need(dve, q_hi_made, n + 1)
                        dve.tensor_tensor(q_lo[:, :, :], misc[:, 0:G4 * N].rearrange("p (g n) -> p g n", g=G4),
                                          q_hi[:, :, :].bitcast(F32), ALU.subtract).then_inc(q_out, 1)
                    if h in (11, 13, 15) and has_n:
                        l = (h - 11) // 2
                        need(dve, unit_made, UNITS * n + KT + 1 + l)
                        if l == 0:
                            need(dve, valued, H * (n - 1))
                        dve.tensor_tensor(v[:, q, l, :], proj[(q + KT + l) % 2][0:LC, :], W["bv_row"][0:LC, :],
                                          ALU.add).then_inc(unit_out, 1)
                    if h == 9 and has_nn:
                        need(dve, x_in_ld, 16 * (nn + 1))
                        dve.bn_stats(stats[:, :], x_in[:, p, :]).then_inc(ln1, 1)
                        need(dve, ln1, 8 * nn + 1)
                        waited(dve)
                        dve.bn_aggr(mv[:, :], stats[:, :]).then_inc(ln1, 1)
                    if h == 10 and has_nn:
                        need(dve, rstd_made, 2 * nn + 2)
                        dve.tensor_scalar(x_in[:, p, :], x_in[:, p, :], mv[:, 0:1], rstd[:, 0:1],
                                          ALU.subtract, ALU.mult).then_inc(ln1, 1)
                    if h == 11 and has_m:
                        need(dve, softmaxed, H * (m + 1))
                        dve.reciprocal(inv_total[:, :], total[:, q, :]).then_inc(o_steps, 1)
                        need(dve, o_steps, 6 * m + 1)
                        need(dve, o_made, 3 * m + 1)
                        dve.tensor_tensor(o_tok[:, :].rearrange("p (h d) -> p h d", h=H),
                                          misc[0:N, :].rearrange("p (h d) -> p h d", h=H),
                                          inv_total[:, :].unsqueeze(2).to_broadcast([N, H, C // H]), ALU.mult).then_inc(o_out, 1)
                        need(dve, o_out, 3 * m + 1)
                        dve.tensor_reduce(o_amax[:, :], o_tok[:, :], AX.X, ALU.max, apply_absolute_value=True).then_inc(o_steps, 1)
                    if h == 12 and has_m:
                        quantize(o_tok[:, :], o_amax[:, :], o_scale[:, :], o_inv[:, :], shifted[:, :], o_int[:, :], o_steps, 6 * m + 2)
                    if h == 12 and has_nn:
                        need(dve, ln1, 8 * nn + 3)
                        dve.tensor_reduce(x_amax[:, :], x_in[:, p, :], AX.X, ALU.max, apply_absolute_value=True).then_inc(ln1, 1)
                    if h == 13 and has_m:
                        need(dve, o_made, 3 * m + 2)
                        dve.tensor_scalar(o_int_t[:, :, :], misc16[:, 0:KT * N].rearrange("p (t n) -> p t n", t=KT),
                                          QMAX, -QMAX, ALU.min, ALU.max).then_inc(o_out, 1)
                    if h == 14 and has_nn:
                        need(dve, q_made, 3 * (nn - 1) + 1)
                        quantize(x_in[:, p, :], x_amax[:, :], x_scale[:, p:p + 1], x_inv[:, :], shifted[:, :], x_int[:, :], ln1, 8 * nn + 4)

            iterations(dve, body)

        @block.tensor
        def _(pe):
            def scores(b, par, h):
                k = b * H + h
                if h % 8 == 0:
                    need(pe, k_stacked[h // 8], 16 * KDMAS * (b + 1))
                if h == 0:
                    need(pe, q_stacked, 16 * QDMAS * (b + 1))
                need(pe, masked, k - 1)
                pe.matmul(score[h % 2][0:N, 0:LP], q_st[:, par % 2, h, :], k_st[:, h, :],
                          start=True, stop=True).then_inc(scored, 1)

            def turn_probs(b, h):
                k = b * H + h
                need(pe, softmaxed, k + 1)
                need(pe, turned_out, k - 1)
                for l in range(LT):
                    mm = pe.transpose(turn[h % 2][0:LC, l * N:(l + 1) * N], probs[:, h % DS, l * LC:(l + 1) * LC],
                                      W["ident"][0:N, 0:N])
                mm.then_inc(turned, 1)

            def values(b, par, h):
                k = b * H + h
                if h == 0:
                    need(pe, unit_out, UNITS * (b + 1))
                    need(pe, out_t_out, b)
                need(pe, turned_out, k + 1)
                i, g = h % 4, h // 4
                for l in range(LT):
                    mm = pe.matmul(out_t[QUARTER * i:QUARTER * i + QUARTER, g * N:(g + 1) * N],
                                   v[:, par % 2, l, QUARTER * h:QUARTER * h + QUARTER], probs_t[:, h % RING_T, l, :],
                                   start=(l == 0), stop=(l == LT - 1), skip_group_check=True)
                mm.then_inc(valued, 1)

            def project(n, q, u, t):
                if u == 0 and t == 0:
                    need(pe, c_lo_made, n + 1)
                    need(pe, c_hi_made, n + 1)
                if t == 0:
                    need(pe, unit_out, UNITS * n + u - 1)
                bank = proj[(q + u) % 2]
                if u < KT:
                    for w, c in (("wk_hi", c_hi), ("wk_hi", c_lo), ("wk_lo", c_hi)):
                        mm = pe.matmul(bank[:, 0:LP], W[w][:, t, 128 * u:128 * u + 128], c[:, q, t, :],
                                       start=(t == 0 and w == "wk_hi" and c is c_hi), stop=(t == KT - 1 and w == "wk_lo"))
                else:
                    l = u - KT
                    for w, c in (("wv_hi", c_hi), ("wv_lo", c_hi), ("wv_hi", c_lo)):
                        mm = pe.matmul(bank[0:LC, :], c[:, q, t, l * LC:(l + 1) * LC], W[w][:, t, :],
                                       start=(t == 0 and w == "wv_hi" and c is c_hi), stop=(t == KT - 1 and c is c_lo))
                if t == KT - 1:
                    mm.then_inc(unit_made, 1)

            def turn_to_misc(src, ident, dst, rows, cols):
                for t in range(KT):
                    mm = pe.transpose(dst[0:cols, t * rows:(t + 1) * rows], src(t), ident)
                return mm

            def body(it, par, inside=False):
                has_m2, has_m, has_a, has_n, has_nn, _ = stages(it, inside)
                n, m, m2, nn = it + 1, it - 1, it - 2, it + 2
                p, q = par % 2, (par + 1) % 2
                for h in range(H):
                    if h < 2 and has_m:
                        turn_probs(m, H - 2 + h)
                    if h >= 2 and has_a:
                        turn_probs(it, h - 2)
                    if has_a:
                        scores(it, par, h)
                    if h < H - 1 and has_n:
                        for step in range(KT * UNITS * h // (H - 1), KT * UNITS * (h + 1) // (H - 1)):
                            project(n, q, step // KT, step % KT)
                    if h == 4 and has_m2:
                        need(pe, ln2, 3 * m2 + 3)
                        need(pe, o_out, 3 * m2 + 3)
                        turn_to_misc(lambda t: h2_s[:, 128 * t:128 * t + 128], W["ident"][0:N, 0:N], misc, N, 128).then_inc(r_made, 1)
                    if h == 5 and has_m2:
                        need(pe, r_out, 2 * m2 + 1)
                        for t in range(KT):
                            mm = pe.matmul(misc[0:N, 0:8], h2_t[:, t, :], W["router"][:, t, :], start=(t == 0), stop=(t == KT - 1))
                        mm.then_inc(r_made, 1)
                    if h == 6 and has_n:
                        need(pe, ln1, 8 * n + 8)
                        need(pe, q_out, 3 * n)
                        if has_m2:
                            need(pe, r_out, 2 * m2 + 2)
                        turn_to_misc(lambda t: x_int[:, 128 * t:128 * t + 128], W["ident16"][0:N, 0:N], misc16, N, 128).then_inc(q_made, 1)
                    if h == 7 and has_n:
                        need(pe, q_out, 3 * n + 1)
                        for t in range(KT):
                            mm = pe.matmul(misc[0:N, :], x_int_t[:, t, :], W["wq_int"][:, t, :], start=(t == 0), stop=(t == KT - 1))
                        mm.then_inc(q_made, 1)
                    if h == 9 and has_n:
                        need(pe, q_biased, n + 1)
                        turn_to_misc(lambda t: q_tok[:, 128 * t:128 * t + 128], W["ident"][0:N, 0:N], misc, N, 128).then_inc(q_made, 1)
                    if h == 11 and has_m:
                        need(pe, out_t_out, m + 1)
                        if has_n:
                            need(pe, q_out, 3 * n + 3)
                        if has_m2:
                            need(pe, r_out, 2 * m2 + 2)
                        turn_to_misc(lambda t: out_ts[:, t, :], W["ident"][:, :], misc, 128, N).then_inc(o_made, 1)
                    if h == 13 and has_m:
                        need(pe, o_steps, 6 * m + 6)
                        turn_to_misc(lambda t: o_int[:, 128 * t:128 * t + 128], W["ident16"][0:N, 0:N], misc16, N, 128).then_inc(o_made, 1)
                    if h == 15 and has_m:
                        need(pe, o_out, 3 * m + 2)
                        for t in range(KT):
                            mm = pe.matmul(misc[0:N, :], o_int_t[:, t, :], W["wo_int"][:, t, :], start=(t == 0), stop=(t == KT - 1))
                        mm.then_inc(o_made, 1)
                    if h < 3 and has_m:
                        values(m, par + 1, H - 3 + h)
                    if h >= 3 and has_a:
                        values(it, par, h - 3)

            iterations(pe, body)



E = 8
SLOTS = 128
PAD_ROWS = SLOTS


def most_tiles(tokens):
    return (2 * tokens + E * (SLOTS - 1) + E - 2) // SLOTS


def route(nc, W, R, weights_by_token, pad_rows):
    N, B = W["tokens"], W["batches"]
    T, NT = N * B, R["tiles"]
    NTP = NT + NT % 2
    lg = W["logits"]
    with ExitStack() as ctx:
        sb = lambda name, shape, dt=F32: ctx.enter_context(nc.sbuf_tensor(name, shape, dt))
        sem = lambda name: ctx.enter_context(nc.semaphore(name))
        rank_ps = ctx.enter_context(nc.psum_tensor("rank_ps", [128, 512], F32))
        cols_ps = ctx.enter_context(nc.psum_tensor("cols_ps", [128, 512], F32))
        slot_ps = ctx.enter_context(nc.psum_tensor("slot_ps", [128, 512], F32))
        F16 = mybir.dt.float16
        prio = sb("prio", [128, E])
        iota = sb("iota", [128, 128])
        token = sb("token", [128, B])
        pad_row = sb("pad_row", [128, 1])
        at_or_after, ones16 = sb("from_here", [128, 128], BF16), sb("ones16", [128, 128], BF16)
        CONSTS = 9
        ones = sb("ones", [128, B])
        top = [sb(f"top{i}", [N, B]) for i in range(2)]
        one = [sb(f"one{i}", [N, B, E]) for i in range(2)]
        rest, work = sb("rest", [N, B, E]), sb("work", [N, B, E])
        best = sb("best", [N, B])
        gap, grown, sum2 = sb("gap", [N, B]), sb("grown", [N, B]), sb("sum2", [N, B])
        share = [sb(f"share{i}", [N, B]) for i in range(2)]
        cw, second, minus_one = sb("cw", [N, B, E]), sb("second_share", [N, B, E]), sb("minus_one", [N, B])
        cw_steps, scanned = sem("cw_steps"), sem("scanned")
        taken = sb("taken", [N, B, E], BF16)
        until = sb("until", [128, B, E])
        cnt_i, tiles, last, first = sb("cnt_i", [128, E], I32), sb("tiles", [128, E]), sb("last", [128, E]), sb("first", [128, E])
        slot = sb("slot", [N, B, E])
        at = sb("at", [N, 2, B])
        at_i, hi_i = sb("at_i", [N, 2, B], I32), sb("hi_i", [N, 2, B], I32)
        hi_f, lo_f = sb("hi_f", [N, 2, B]), sb("lo_f", [N, 2, B])
        HALVES = [(0, B // 2), (B // 2, B)]
        at_row = sb("at_row", [N, 2, B, SLOTS], F16)
        at_tile = sb("at_tile", [N, 2, B, 2, NTP], F16)
        past = sb("past", [128, NTP, E])
        expert, place, pair = sb("expert", [128, NTP]), sb("place", [128, NTP]), sb("pair", [128, NTP])
        place_i = sb("place_i", [128, NTP], I32)
        found, number = sb("found", [128, 2, NTP]), sb("number", [128, NTP])
        consts, steps = sem("route_consts"), sem("route_steps")
        grown_done, ranked, placed, stored = sem("grown_done"), sem("ranked"), sem("placed"), sem("weights_stored")
        taken_done, zeroed, pad_written = sem("taken_done"), sem("zeroed"), sem("pad_rows_written")
        tile_made, numbered, row_made = sem("at_tile_made"), sem("at_tile_numbered"), sem("at_row_made")
        zero = sb("zero", [128, pad_rows.shape[1]])
        block = ctx.enter_context(nc.Block())

        @block.gpsimd
        def _(pool):
            pool.iota(prio[:, :], [[-1, E]], base=E, channel_multiplier=0, allow_small_or_imprecise_dtypes=True).then_inc(consts, 1)
            pool.iota(iota[:, :], [[1, 128]], base=0, channel_multiplier=0, allow_small_or_imprecise_dtypes=True).then_inc(consts, 1)
            pool.iota(token[:, :], [[N, B]], base=-(T // 2), channel_multiplier=1, allow_small_or_imprecise_dtypes=True).then_inc(consts, 1)
            pool.iota(pad_row[:, :], [[1, 1]], base=T, channel_multiplier=1, allow_small_or_imprecise_dtypes=True).then_inc(consts, 1)
            pool.memset(ones16[:, :], 1.0).then_inc(consts, 1)
            pool.memset(at_or_after[:, :], -1.0).then_inc(consts, 1)
            pool.memset(ones[:, :], 1.0).then_inc(consts, 1)
            pool.memset(minus_one[:, :], -1.0).then_inc(consts, 1)
            pool.wait_ge(consts, 8)
            pool.affine_select(out=at_or_after[:, :], in_=at_or_after[:, :], compare_op=ALU.is_ge, fill=0.0, base=0,
                               pattern=[[-1, 128]], channel_multiplier=1).then_inc(consts, 1)
            pool.memset(zero[:, :], 0.0).then_inc(zeroed, 1)
            over_e = lambda a: a.unsqueeze(2).to_broadcast([N, B, E])
            pool.wait_ge(grown_done, 1)
            pool.tensor_scalar(sum2[:, :], grown[:, :], 1.0, 1.0, ALU.mult, ALU.add).then_inc(cw_steps, 1)
            pool.wait_ge(cw_steps, 1)
            pool.tensor_tensor(share[0][:, :], sum2[:, :], minus_one[:, :], ALU.pow).then_inc(cw_steps, 1)
            pool.wait_ge(cw_steps, 2)
            pool.tensor_tensor(share[1][:, :], grown[:, :], share[0][:, :], ALU.mult).then_inc(cw_steps, 1)
            pool.tensor_tensor(cw[:, :, :], one[0][:, :, :], over_e(share[0][:, :]), ALU.mult).then_inc(cw_steps, 1)
            pool.wait_ge(cw_steps, 3)
            pool.tensor_tensor(second[:, :, :], one[1][:, :, :], over_e(share[1][:, :]), ALU.mult).then_inc(cw_steps, 1)
            pool.wait_ge(cw_steps, 5)
            pool.tensor_tensor(cw[:, :, :], cw[:, :, :], second[:, :, :], ALU.add).then_inc(cw_steps, 1)
            for i in range(2):
                pool.wait_ge(tile_made, i + 1)
                pool.tensor_tensor(at_tile[:, i, :, 0, :], at_tile[:, i, :, 1, :],
                                   token[0:N, :].unsqueeze(2).to_broadcast([N, B, NTP]), ALU.mult).then_inc(numbered, 1)

        @block.scalar
        def _(act):
            act.wait_ge(steps, R["gap_step"])
            act.activation(grown[:, :], gap[:, :], ACT.Exp).then_inc(grown_done, 1)

        @block.sync
        def _(sp):
            load_expert(sp, R, 0)
            load_expert(sp, R, 1)
            sp.wait_ge(zeroed, 1)
            sp.dma_start(pad_rows, zero[:, :]).then_inc(pad_written, 16)
            sp.wait_ge(pad_written, 16)
            sp.wait_ge(cw_steps, 6)
            sp.dma_start(weights_by_token.rearrange("(b n) e -> n b e", n=N), cw[:, :, :]).then_inc(stored, 16)
            sp.wait_ge(stored, 16)

        @block.tensor
        def _(pe):
            pe.wait_ge(taken_done, 1)
            pe.wait_ge(consts, CONSTS)
            flat = taken[:, :, :].rearrange("p b e -> p (b e)")
            pe.matmul(rank_ps[0:N, 0:B * E], at_or_after[0:N, 0:N], flat, start=True, stop=True).then_inc(ranked, 1)
            pe.matmul(cols_ps[:, 0:B * E], ones16[0:N, :], flat, start=True, stop=True).then_inc(ranked, 1)
            for i in range(2):
                pe.wait_ge(numbered, i + 1)
                for b in range(B):
                    if b in (0, B // 2):
                        pe.wait_ge(row_made, 2 * i + (2 if b else 1))
                    mm = pe.matmul(slot_ps[:, 0:2 * NTP], at_row[:, i, b, :], at_tile[:, i, b, :, :].rearrange("p v t -> p (v t)"),
                                   start=(i == 0 and b == 0), stop=(i == 1 and b == B - 1))
            mm.then_inc(placed, 1)

        @block.vector
        def _(dve):
            count = [0]

            def link(ins):
                count[0] += 1
                ins.then_inc(steps, 1)
                dve.wait_ge(steps, count[0])

            over_b = lambda a: a.unsqueeze(1).to_broadcast([N, B, E])
            over_e = lambda a: a.unsqueeze(2).to_broadcast([N, B, E])
            left = lg[0:N, :, :]
            for i in range(2):
                link(dve.tensor_reduce(top[i][:, :], left, AX.X, ALU.max))
                link(dve.tensor_tensor(work[:, :, :], left, over_e(top[i][:, :]), ALU.is_equal))
                dve.wait_ge(consts, 1 if i == 0 else CONSTS)
                link(dve.tensor_tensor(work[:, :, :], work[:, :, :], over_b(prio[0:N, :]), ALU.mult))
                link(dve.tensor_reduce(best[:, :], work[:, :, :], AX.X, ALU.max))
                link(dve.tensor_tensor(one[i][:, :, :], over_b(prio[0:N, :]), over_e(best[:, :]), ALU.is_equal))
                if i == 0:
                    link(dve.scalar_tensor_tensor(rest[:, :, :], one[0][:, :, :], -BIG, left, ALU.mult, ALU.add))
                    left = rest[:, :, :]
            dve.tensor_tensor(taken[:, :, :], one[0][:, :, :], one[1][:, :, :], ALU.add).then_inc(taken_done, 1)
            link(dve.tensor_tensor(gap[:, :], top[1][:, :], top[0][:, :], ALU.subtract))
            assert count[0] == R["gap_step"]
            dve.wait_ge(ranked, 2)
            cols = cols_ps[:, 0:B * E].rearrange("p (b e) -> p b e", e=E)
            for e in range(E):
                dve.tensor_tensor_scan(until[:, :, e], ones[:, :], cols[:, :, e], 0.0, ALU.mult, ALU.add).then_inc(scanned, 1)
            dve.wait_ge(scanned, E)
            link(dve.tensor_scalar(cnt_i[:, :], until[:, B - 1, :], float(SLOTS - 1), float(SLOTS), ALU.add, ALU.max))
            link(dve.tensor_scalar(cnt_i[:, :], cnt_i[:, :], 7, None, ALU.arith_shift_right))
            link(dve.tensor_copy(tiles[:, :], cnt_i[:, :]))
            link(dve.tensor_tensor_scan(last[:, :], ones[:, 0:E] if B >= E else prio[:, :], tiles[:, :], 0.0, ALU.mult, ALU.add))
            link(dve.tensor_tensor(first[:, :], last[:, :], tiles[:, :], ALU.subtract))
            link(dve.tensor_scalar(first[:, :], first[:, :], float(SLOTS), None, ALU.mult))
            link(dve.tensor_tensor(slot[:, :, :], until[0:N, :, :], over_b(first[0:N, :]), ALU.add))
            link(dve.tensor_tensor(slot[:, :, :], slot[:, :, :],
                                   rank_ps[0:N, 0:B * E].rearrange("p (b e) -> p b e", e=E), ALU.add))
            for i in range(2):
                link(dve.tensor_tensor(work[:, :, :], one[i][:, :, :], slot[:, :, :], ALU.mult))
                link(dve.tensor_reduce(at[:, i, :], work[:, :, :], AX.X, ALU.add))
            link(dve.tensor_copy(at_i[:, :, :], at[:, :, :]))
            link(dve.tensor_scalar(hi_i[:, :, :], at_i[:, :, :], 7, None, ALU.arith_shift_right))
            link(dve.tensor_copy(hi_f[:, :, :], hi_i[:, :, :]))
            link(dve.scalar_tensor_tensor(lo_f[:, :, :], hi_f[:, :, :], -float(SLOTS), at[:, :, :], ALU.mult, ALU.add))
            for i in range(2):
                dve.tensor_tensor(at_tile[:, i, :, 1, :], iota[0:N, 0:NTP].unsqueeze(1).to_broadcast([N, B, NTP]),
                                  hi_f[:, i, :].unsqueeze(2).to_broadcast([N, B, NTP]), ALU.is_equal).then_inc(tile_made, 1)
                for b0, b1 in HALVES:
                    dve.tensor_tensor(at_row[:, i, b0:b1, :], iota[0:N, :].unsqueeze(1).to_broadcast([N, b1 - b0, SLOTS]),
                                      lo_f[:, i, b0:b1].unsqueeze(2).to_broadcast([N, b1 - b0, SLOTS]), ALU.is_equal).then_inc(row_made, 1)
            link(dve.tensor_tensor(past[:, :, :], iota[:, 0:NTP].unsqueeze(2).to_broadcast([128, NTP, E]),
                                   last[:, :].unsqueeze(1).to_broadcast([128, NTP, E]), ALU.is_ge))
            link(dve.tensor_reduce(expert[:, :], past[:, :, :], AX.X, ALU.add))
            link(dve.tensor_scalar(expert[:, :], expert[:, :], float(E - 1), None, ALU.min))
            link(dve.tensor_copy(R["expert"][:, :], expert[:, :]))
            link(dve.tensor_scalar(place_i[:, :], R["expert"][:, :], 1, None, ALU.bitwise_and))
            link(dve.tensor_copy(place[:, :], place_i[:, :]))
            link(dve.scalar_tensor_tensor(pair[:, 1:NTP - 1], expert[:, 1:NTP - 1], float(E), expert[:, 2:NTP], ALU.mult, ALU.add))
            link(dve.scalar_tensor_tensor(R["pair"][:, 1:NTP - 1], place[:, 0:NTP - 2], float(E * E), pair[:, 1:NTP - 1], ALU.mult, ALU.add))
            link(dve.tensor_copy(R["last"][:, :], last[:, :]))
            dve.wait_ge(placed, 1)
            link(dve.tensor_copy(found[:, :, :], slot_ps[:, 0:2 * NTP].rearrange("p (v t) -> p v t", v=2)))
            link(dve.scalar_tensor_tensor(number[:, :], found[:, 1, :], float(T // 2), found[:, 0, :], ALU.mult, ALU.add))
            link(dve.tensor_copy(R["gather"][:, :], number[:, :]))
            link(dve.tensor_scalar(found[:, 0, :], found[:, 1, :], -1.0, 1.0, ALU.mult, ALU.add))
            link(dve.scalar_tensor_tensor(number[:, :], found[:, 0, :], pad_row[:, 0:1], number[:, :], ALU.mult, ALU.add))
            link(dve.tensor_copy(R["scatter"][:, :], number[:, :]))


EXPERT_DMAS = 8


def load_expert(sp, R, e):
    C, F2 = R["gate_up_dram_hi"].shape[1:]
    F = F2 // 2
    full, KT = F // 128, C // 128
    FT = -(-F // 128)
    issued = 0
    for part in ("hi", "lo"):
        gate_up = R[f"gate_up_{part}"][:, e % 2 * KT * F2:(e % 2 + 1) * KT * F2].bitcast(F32).rearrange("p (t f) -> p t f", t=KT)
        down = R[f"down_{part}"][:, e % 2 * FT * C:(e % 2 + 1) * FT * C].bitcast(F32).rearrange("p (t c) -> p t c", t=FT)
        gate_up_src = R[f"gate_up_dram_{part}"][e, :, :].rearrange("(t p) f -> p t f", p=128)
        down_src = R[f"down_dram_{part}"][e, :, :]
        for pieces in (((gate_up[:, 0:KT // 2, :], gate_up_src[:, 0:KT // 2, :]),),
                       ((gate_up[:, KT // 2:KT, :], gate_up_src[:, KT // 2:KT, :]),),
                       ((down[:, 0:full, :], down_src[0:128 * full, :].rearrange("(t p) c -> p t c", p=128)),
                        (down[0:F - 128 * full, full, :], down_src[128 * full:F, :]))):
            if issued and e >= 2:
                sp.wait_ge(R["loaded"][e], 16 * issued)
            for dst, src in pieces:
                sp.dma_start(dst, src).then_inc(R["loaded"][e], 16)
                issued += 1


def experts(nc, W, R, h2, weights_by_token, out):
    NT = R["tiles"]
    C, F2 = R["gate_up_dram_hi"].shape[1:]
    F = F2 // 2
    KT, FT = C // 128, -(-F // 128)
    FP = FT * 128
    FK = [min(128, F - 128 * k) for k in range(FT)]
    with ExitStack() as ctx:
        sb = lambda name, shape, dt=F32: ctx.enter_context(nc.sbuf_tensor(name, shape, dt))
        sem = lambda name: ctx.enter_context(nc.semaphore(name))
        bank = lambda name: ctx.enter_context(nc.psum_tensor(name, [128, 512], F32))
        h_ps, a_ps = bank("h_ps"), bank("a_ps")
        gate_ps, up_ps, y_ps = [[bank(f"{n}_ps{i}") for i in range(2)] for n in ("gate", "up", "y")]
        rows, cw = sb("rows", [128, 2, C]), sb("cw_rows", [128, 2, E])
        gi, si = [sb(f"gather_idx{i}", [128, 1], I32) for i in range(2)], [sb(f"scatter_idx{i}", [128, 1], I32) for i in range(2)]
        share = sb("row_share", [128, 2])
        h_hi, h_lo = sb("h_hi", [128, 2, C], F32R), sb("h_lo", [128, 2, C], F32R)
        silu, a = sb("silu", [128, 2, F]), sb("a", [128, 2, FP])
        a_hi, a_lo = sb("a_hi", [128, FP], F32R), sb("a_lo", [128, FP], F32R)
        y = sb("y_rows", [128, 2, C])
        padded, place_free = sem("padded"), sem("place_free")
        gi_set, si_set, go = sem("gi_set"), sem("si_set"), sem("go")
        rows_in, cw_in, scattered = [sem("rows_in0"), sem("rows_in1")], [sem("cw_in0"), sem("cw_in1")], sem("scattered")
        h_turned, h_hi_made, h_lo_made, gated, silu_made, act_made = sem("h_turned"), sem("h_hi_made"), sem("h_lo_made"), sem("gated"), sem("silu_made"), sem("act_made")
        a_turned, a_hi_made, a_lo_made, down_made, share_made, y_made = sem("a_turned"), sem("a_hi_made"), sem("a_lo_made"), sem("down_made"), sem("share_made"), sem("y_made")

        def need(eng, s, count):
            if not isinstance(count, int) or count > 0:
                eng.wait_ge(s, count)

        def iterations(eng, body):
            lo, hi = 4, NT - 2 - NT % 2
            for t in range(-2, min(lo, NT + 2)):
                body(t, t // 2, t % 2)
            with eng.Fori(lo // 2, hi // 2) as j:
                for k in range(2):
                    body(j * 2 + k, j, k, True)
            for t in range(hi, NT + 2):
                body(t, t // 2, t % 2)

        def exists(t, inside):
            return inside or 0 <= t < NT

        def column(table, t, inside):
            return table[:, bass.ds(t, 1)] if inside else table[:, t:t + 1]

        def expert_of(eng, t, inside):
            return eng.value_load(R["expert"][0:1, bass.ds(t, 1)] if inside else R["expert"][0:1, t:t + 1], min_val=0, max_val=E - 1)

        block = ctx.enter_context(nc.Block())

        @block.sync
        def _(sp):
            for e in range(E):
                if e >= 2:
                    sp.wait_ge(down_made, sp.value_load(R["last"][0:1, e - 2:e - 1], min_val=0, max_val=NT) + 1)
                    sp.sem_inc(place_free, 1)
                    load_expert(sp, R, e)
                sp.wait_ge(R["loaded"][e], 16 * EXPERT_DMAS)
                sp.sem_inc(R["weights_ready"], 1)

        @block.gpsimd
        def _(pool):
            def body(t, half, par, inside=False):
                if exists(t + 2, inside):
                    need(pool, rows_in[par], 16 * (half + 1))
                    need(pool, cw_in[par], 16 * (half + 1))
                    pool.tensor_copy(gi[par][:, :], column(R["gather"], t + 2, inside)).then_inc(gi_set, 1)
                    need(pool, gi_set, t + 3)
                    need(pool, h_turned, t + 1)
                    pool.sem_inc(go, 1)
                    pool.indirect_dma_start(rows[:, par, :], None, h2, bass.IndirectOffsetOnAxis(ap=gi[par][:, 0:1], axis=0)).then_inc(rows_in[par], 16)
                if exists(t - 2, inside):
                    need(pool, scattered, 16 * (t - 2))
                    pool.tensor_copy(si[par][:, :], column(R["scatter"], t - 2, inside)).then_inc(si_set, 1)
                    need(pool, si_set, t - 1)
                    need(pool, y_made, t - 1)
                    pool.sem_inc(go, 1)
                    pool.indirect_dma_start(out, bass.IndirectOffsetOnAxis(ap=si[par][:, 0:1], axis=0), y[:, par, :], None,
                                            compute_op=ALU.add).then_inc(scattered, 16)
                if exists(t + 2, inside):
                    need(pool, share_made, t + 1)
                    pool.sem_inc(go, 1)
                    pool.indirect_dma_start(cw[:, par, :], None, weights_by_token, bass.IndirectOffsetOnAxis(ap=gi[par][:, 0:1], axis=0)).then_inc(cw_in[par], 16)

            iterations(pool, body)
            pool.wait_ge(scattered, 16 * NT)

        @block.scalar
        def _(act):
            def body(t, half, par, inside=False):
                other = 1 - par
                if exists(t - 1, inside):
                    need(act, a_turned, t)
                    need(act, down_made, t)
                    act.activation(a_hi[:, :], a_ps[:, 0:FP], ACT.Identity).then_inc(a_hi_made, 1)
                if exists(t + 1, inside):
                    need(act, h_turned, t + 2)
                    need(act, gated, t)
                    act.activation(h_hi[:, other, :], h_ps[:, 0:C], ACT.Identity).then_inc(h_hi_made, 1)
                if exists(t, inside):
                    need(act, gated, t + 1)
                    need(act, act_made, t - 1)
                    act.activation(silu[:, par, :], gate_ps[par][:, 0:F], ACT.Silu).then_inc(silu_made, 1)
                if exists(t - 1, inside):
                    need(act, down_made, t + 1)
                    need(act, share_made, t)
                    need(act, scattered, 16 * (t - 2))
                    act.activation(y[:, other, :], y_ps[other][:, 0:C], ACT.Copy, scale=share[:, other:other + 1]).then_inc(y_made, 1)

            iterations(act, body)

        @block.vector
        def _(dve):
            dve.memset(a[:, :, F:FP], 0.0).then_inc(padded, 1)

            def body(t, half, par, inside=False):
                other = 1 - par
                if exists(t - 1, inside):
                    need(dve, a_hi_made, t)
                    dve.tensor_tensor(a_lo[:, :], a_ps[:, 0:FP], a_hi[:, :].bitcast(F32), ALU.subtract).then_inc(a_lo_made, 1)
                if exists(t + 1, inside):
                    need(dve, h_hi_made, t + 2)
                    dve.tensor_tensor(h_lo[:, other, :], h_ps[:, 0:C], h_hi[:, other, :].bitcast(F32), ALU.subtract).then_inc(h_lo_made, 1)
                if exists(t, inside):
                    e = expert_of(dve, t, inside)
                    need(dve, cw_in[par], 16 * (half + 1))
                    need(dve, y_made, t - 1)
                    dve.tensor_copy(share[:, par:par + 1], cw[:, par, bass.ds(e, 1)]).then_inc(share_made, 1)
                    need(dve, silu_made, t + 1)
                    need(dve, a_turned, t - 1)
                    dve.tensor_tensor(a[:, par, 0:F], silu[:, par, :], up_ps[par][:, 0:F], ALU.mult).then_inc(act_made, 1)

            iterations(dve, body)

        @block.tensor
        def _(pe):
            pe.wait_ge(padded, 1)
            pe.sem_inc(down_made, 1)

            known = {}

            def experts_of(t, par, inside):
                if not inside:
                    return (expert_of(pe, t, False) if exists(t, False) else None,
                            expert_of(pe, t - 1, False) % 2 if exists(t - 1, False) else None)
                if par == 0:
                    pair = pe.value_load(R["pair"][0:1, bass.ds(t, 1)], min_val=0, max_val=2 * E * E - 1)
                    known["first"], known["second"] = pair // E % E, pair % E
                    return known["first"], pair // (E * E)
                return known["second"], known["first"] % 2

            def gate_and_up(t, par, place, steps):
                for k in steps:
                    for h, w in ((h_hi, "gate_up_hi"), (h_hi, "gate_up_lo"), (h_lo, "gate_up_hi")):
                        for i, ps in enumerate((gate_ps[par], up_ps[par])):
                            mm = pe.matmul(ps[:, 0:F], h[:, par, 128 * k:128 * k + 128],
                                           R[w][:, bass.ds(place * (KT * F2) + (k * F2 + i * F), F)],
                                           start=(k == 0 and h is h_hi and w == "gate_up_hi"), stop=(k == KT - 1 and h is h_lo))
                return mm

            def body(t, half, par, inside=False):
                other = 1 - par
                expert, place1 = experts_of(t, par, inside)
                if exists(t, inside):
                    place = expert % 2
                    pe.wait_ge(R["weights_ready"], expert + 1)
                    need(pe, h_lo_made, t + 1)
                    need(pe, act_made, t - 1)
                    gate_and_up(t, par, place, range(KT // 2))
                if exists(t - 1, inside):
                    need(pe, act_made, t)
                    need(pe, a_lo_made, t - 1)
                    for k in range(FT):
                        mm = pe.transpose(a_ps[:, 128 * k:128 * k + 128], a[:, other, 128 * k:128 * k + 128], W["ident"][:, :])
                    mm.then_inc(a_turned, 1)
                if exists(t + 1, inside):
                    need(pe, rows_in[other], 16 * ((par + 1) // 2 + half + 1))
                    need(pe, h_lo_made, t + 1)
                    for k in range(KT):
                        mm = pe.transpose(h_ps[:, 128 * k:128 * k + 128], rows[:, other, 128 * k:128 * k + 128], W["ident"][:, :])
                    mm.then_inc(h_turned, 1)
                if exists(t, inside):
                    gate_and_up(t, par, place, range(KT // 2, KT)).then_inc(gated, 1)
                if exists(t - 1, inside):
                    need(pe, a_lo_made, t)
                    need(pe, y_made, t - 2)
                    for k in range(FT):
                        for h, w in ((a_hi, "down_hi"), (a_hi, "down_lo"), (a_lo, "down_hi")):
                            mm = pe.matmul(y_ps[other][:, 0:C], h[0:FK[k], 128 * k:128 * k + 128],
                                           R[w][0:FK[k], bass.ds(place1 * (FT * C) + k * C, C)],
                                           start=(k == 0 and h is a_hi and w == "down_hi"), stop=(k == FT - 1 and h is a_lo))
                    mm.then_inc(down_made, 1)

            iterations(pe, body)


def program(nc, x, ctx_t, mask, wq, bq, wk_t, bk, wv_t, bv, wo, bo, gate_up_t, down_t, router_t, out):
    B, N, C = x.shape
    T = B * N
    dram = lambda name, shape: nc.dram_tensor(name, shape, F32, kind="Internal").ap()
    h2, weights_by_token = dram("h2_rows", (T, C)), dram("weights_by_token", (T, E))
    gate_up_dram = {part: dram(f"gate_up_dram_{part}", gate_up_t.shape) for part in ("hi", "lo")}
    down_dram = {part: dram(f"down_dram_{part}", down_t.shape) for part in ("hi", "lo")}
    flat = lambda a: a.rearrange("e k n -> (e k n)").rearrange("(p f) -> p f", p=128)
    with ExitStack() as ctx:
        sb = lambda name, shape, dt=F32: ctx.enter_context(nc.sbuf_tensor(name, shape, dt))
        W = {"tokens": N, "batches": B, "rows": T, "ident": sb("ident", [128, 128]), "ident16": sb("ident16", [128, 128], BF16),
             "logits": sb("logits", [128, B, E]), "gate_up_flat": flat(gate_up_t), "down_flat": flat(down_t)}
        for part in ("hi", "lo"):
            W[f"gate_up_{part}"], W[f"down_{part}"] = flat(gate_up_dram[part]), flat(down_dram[part])
        with ExitStack() as first:
            sb = lambda name, shape, dt=F32: first.enter_context(nc.sbuf_tensor(name, shape, dt))
            W.update({n: sb(n, [128, 4, C], F32R) for n in ("wk_hi", "wk_lo", "wv_hi", "wv_lo")})
            W.update({n: sb(n, [128, 4, C], BF16) for n in ("wq_int", "wo_int")})
            W.update({n: sb(n, [128, C]) for n in ("wq_row", "wo_row", "bq_row", "bv_row", "bo_row")})
            W.update(bk_col=sb("bk_col", [128, 4]), router=sb("router", [128, 4, E]), minus_half=sb("minus_half", [128, 1]))
            LP = ctx_t.shape[2] + ctx_t.shape[2] % 2
            W.update(stage=sb("ctx_stage", [128, 4, LP]), c_hi=sb("ctx_hi", [128, 2, 4, LP], F32R),
                     c_lo=sb("ctx_lo", [128, 2, 4, LP], F32R), x_in=sb("x_in", [N, 2, C]))
            W.update({n: first.enter_context(nc.semaphore(n)) for n in ("ctx_in", "x_in_ld", "stage_pad", "c_hi_made", "c_lo_made")})
            prepare_weights(nc, W, x, ctx_t, wq, wk_t, wv_t, wo, bq, bk, bv, bo, router_t)
            attention(nc, W, x, ctx_t, mask, out[0:T, :].rearrange("(b n) c -> b n c", n=N),
                      h2.rearrange("(b n) c -> b n c", n=N))
        sb = lambda name, shape, dt=F32: ctx.enter_context(nc.sbuf_tensor(name, shape, dt))
        NT = most_tiles(T)
        width = NT + NT % 2
        F2, FT = gate_up_t.shape[2], -(-down_t.shape[1] // 128)
        R = {"tiles": NT, "gap_step": 12, "gather": sb("gather", [128, width], I32),
             "scatter": sb("scatter", [128, width], I32), "expert": sb("expert_of_tile", [128, width], I32),
             "pair": sb("pair_of_tiles", [128, width], I32), "last": sb("last_tile", [128, E], I32),
             "loaded": [ctx.enter_context(nc.semaphore(f"expert_loaded{e}")) for e in range(E)],
             "weights_ready": ctx.enter_context(nc.semaphore("weights_ready"))}
        for part in ("hi", "lo"):
            R[f"gate_up_dram_{part}"], R[f"down_dram_{part}"] = gate_up_dram[part], down_dram[part]
            R[f"gate_up_{part}"] = sb(f"gate_up_{part}", [128, 2 * (C // 128) * F2], F32R)
            R[f"down_{part}"] = sb(f"down_{part}", [128, 2 * FT * C], F32R)
        route(nc, W, R, weights_by_token, out[T:T + PAD_ROWS, :])
        experts(nc, W, R, h2, weights_by_token, out)


_OUT = "out"


def kernel(x, ctx_2048, mask_BxSxS2_ff0, L0_xattn_wq, L0_xattn_bq, L0_xattn_wk, L0_xattn_bk, L0_xattn_wv, L0_xattn_bv,
           L0_xattn_wo, L0_xattn_bo, L0_ffn_gate_up_proj, L0_ffn_down_proj, L0_ffn_router_w):
    import numpy as np
    import concourse.bacc as bacc
    from concourse import mybir as _mybir
    from concourse.bass_utils import run_bass_kernel_spmd as run

    turn = lambda a, *axes: np.ascontiguousarray(np.transpose(np.asarray(a), axes))
    whole = lambda a: np.ascontiguousarray(np.asarray(a))
    arrays = {
        "x": whole(x), "ctx_t": turn(ctx_2048, 0, 2, 1), "mask": whole(mask_BxSxS2_ff0),
        "wq": whole(L0_xattn_wq), "bq": whole(L0_xattn_bq), "wk_t": turn(L0_xattn_wk, 1, 0), "bk": whole(L0_xattn_bk),
        "wv_t": turn(L0_xattn_wv, 1, 0), "bv": whole(L0_xattn_bv), "wo": whole(L0_xattn_wo), "bo": whole(L0_xattn_bo),
        "gate_up_t": turn(L0_ffn_gate_up_proj, 0, 2, 1), "down_t": turn(L0_ffn_down_proj, 0, 2, 1),
        "router_t": turn(L0_ffn_router_w, 1, 0),
    }
    nc = bacc.Bacc("TRN2", target_bir_lowering=False, num_devices=1)
    aps = {n: nc.dram_tensor(n, a.shape, _mybir.dt.from_np(a.dtype), kind="ExternalInput").ap() for n, a in arrays.items()}
    B, N, C = arrays["x"].shape
    aps[_OUT] = nc.dram_tensor(_OUT, (B * N + PAD_ROWS, C), _mybir.dt.float32, kind="ExternalOutput").ap()
    program(nc, **aps)
    r = run(nc, [arrays], core_ids=[0])
    return r.results[0][_OUT][:B * N].reshape(B, N, C)
```
